# Optimizing a Trainium2 kernel written in Bass

```python
import numpy as np
import jax
import jax.numpy as jnp

def _softmax(x, axis=-1):
    return jax.nn.softmax(x, axis=axis)

def _gelu(x):
    return jax.nn.gelu(x, approximate=True)

def _silu(x):
    return jax.nn.silu(x)

def _sigmoid(x):
    return jax.nn.sigmoid(x)

def _layernorm(x, axis=-1, eps=1e-05):
    m = jnp.mean(x, axis=axis, keepdims=True)
    v = jnp.var(x, axis=axis, keepdims=True)
    return (x - m) / jnp.sqrt(v + eps)

def _scatter_add(tgt, idx, src, axis=0):
    return tgt.at[idx].add(src)

def _segment_sum(src, seg, n):
    return jax.ops.segment_sum(src, seg, n)
kernel_name = 'mk_xattn_ffn_d4_seqx_r8_8e31cc'

def setup_inputs(seed: int=0):
    np.random.seed(seed)
    _w = jnp.asarray

    def _rec_inputs():
        import jax
        import jax.numpy as jnp
        _rk = jax.random.key(seed)
        x = 4.136e-05 + 0.9999 * jax.random.normal(jax.random.fold_in(_rk, 1), (32, 128, 128), jnp.float32)
        _lenS = 128 - jax.random.randint(jax.random.fold_in(_rk, 7), (32,), 0, max(1, 128 // 4) + 1, jnp.int32)
        _lenS2 = 128 - jax.random.randint(jax.random.fold_in(_rk, 8), (32,), 0, max(1, 128 // 4) + 1, jnp.int32)
        _ctx_2048P = jax.random.normal(jax.random.fold_in(_rk, 11), (32, 16, 256), jnp.float32)
        _ctx_2048c = jax.random.dirichlet(jax.random.fold_in(_rk, 511), 0.3 * jnp.ones((16,), jnp.float32), (32, 128))
        _ctx_2048t = jnp.einsum('bsk,bkd->bsd', _ctx_2048c, _ctx_2048P)
        _ctx_2048t = _ctx_2048t * jax.lax.rsqrt(jnp.mean(jnp.square(_ctx_2048t)) + 1e-12) * 0.953939
        ctx_2048 = -0.000392918 + 0.999932 * (_ctx_2048t + 0.3 * jax.random.normal(jax.random.fold_in(_rk, 611), (32, 128, 256), jnp.float32))
        itok_Bx1_68_817 = jax.random.randint(jax.random.fold_in(_rk, 12), (32, 1), 68, 818, jnp.int32)
        _validS = jnp.arange(128)[None, :] < _lenS[:, None]
        _validS2 = jnp.arange(128)[None, :] < _lenS2[:, None]
        _causal = jnp.tril(jnp.ones((128, 128), dtype=bool))
        mask_BxS2_if0 = jnp.where(jnp.ones((32, 128), dtype=bool), 4, 0).astype(jnp.int32)
        mask_BxS2_ik0 = jnp.where(jnp.broadcast_to(_validS2[:, :], (32, 128)), 0, 1).astype(jnp.int32)
        mask_BxS2_fk1 = jnp.where(jnp.broadcast_to(_validS2[:, :], (32, 128)), 1.0, 0.0).astype(jnp.float32)
        return (x, ctx_2048, itok_Bx1_68_817, mask_BxS2_if0, mask_BxS2_ik0, mask_BxS2_fk1)
    x, ctx_2048, itok_Bx1_68_817, mask_BxS2_if0, mask_BxS2_ik0, mask_BxS2_fk1 = _rec_inputs()

    def _L0_xattn_setup():
        import jax, jax.numpy as jnp
        import numpy as np
        UNITS = 128
        NUM_HEADS = 16
        MASK_VALUE = -1000000000000.0

        def _split_heads(x, n):
            B, S, D = x.shape
            return x.reshape(B, S, n, D // n).transpose(0, 2, 1, 3)
        key = jax.random.key(seed)
        k1, k2, k3, k4 = jax.random.split(key, 4)
        B, S = (8, 128)
        memory = jax.random.normal(k1, (B, S, 2 * UNITS), dtype=jnp.float32)
        query = jax.random.normal(k2, (B, S, UNITS), dtype=jnp.float32)
        b = jax.random.normal(k3, (S,), dtype=jnp.float32)
        seq_len = jax.random.randint(k4, (B, 1), 0, S, dtype=jnp.int32)
        return {'memory': memory, 'query': query, 'b': b, 'seq_len': seq_len}
    _L0_xattn_all = _L0_xattn_setup()
    _L0_xattn_in = {k: v for k, v in _L0_xattn_all.items() if k in ('b',)}
    del _L0_xattn_all

    def _L0_ffn_setup():
        import jax, jax.numpy as jnp
        import numpy as np
        A, M, H = (4, 128, 128)
        E, N = (8, 512)
        key = jax.random.key(seed)
        kx, k1, k2 = jax.random.split(key, 3)
        x = jax.random.normal(kx, (A, M, H), dtype=jnp.float32)
        w1 = jax.random.normal(k1, (E, H, N), dtype=jnp.float32) * 0.02
        w2 = jax.random.normal(k2, (E, N, H), dtype=jnp.float32) * 0.02
        return {'x': x, 'w1': w1, 'w2': w2}
    _L0_ffn_all = _L0_ffn_setup()
    _L0_ffn_in = {k: v for k, v in _L0_ffn_all.items() if k in ('w1', 'w2')}
    del _L0_ffn_all

    def _L1_xattn_setup():
        import jax, jax.numpy as jnp
        import numpy as np
        B, L, P = (4, 512, 128)
        D_MODEL = 128
        D_GLOBAL = 256
        HEADDIM = 32
        EPSILON = 0.001
        RMS_EPS = 1e-05

        def rmsnorm(x, g, eps=RMS_EPS):
            var = jnp.mean(jnp.square(x), axis=-1, keepdims=True)
            return x * jax.lax.rsqrt(var + eps) * g

        def _hnet_depool(h, h_patch_full, patch_lens):
            h_patch = h_patch_full[..., :D_MODEL]
            bsz, plen = (h_patch.shape[0], h_patch.shape[1])
            seqlen = h.shape[1]
            logp = jnp.full((bsz, plen), -EPSILON, dtype=jnp.float32)
            bidx = jnp.cumsum(patch_lens, axis=1) - 1
            boundary_mask = jnp.zeros((bsz, seqlen), dtype=jnp.int32)
            boundary_mask = boundary_mask.at[jnp.arange(bsz)[:, None], bidx].set(1)
            dt = (-jnp.log(-jnp.expm1(logp))).astype(h_patch.dtype)
            x = h_patch / dt[..., None]
            n_heads = D_MODEL // HEADDIM
            A = -jnp.ones((n_heads,), dtype=jnp.float32)
            bcoef = jnp.exp(logp).astype(h_patch.dtype)
            x4 = x.reshape(bsz, plen, n_heads, HEADDIM)
            a = jnp.exp(dt[:, :, None] * A[None, None, :])
            u = (dt * bcoef)[:, :, None, None] * x4
            a_b = jnp.broadcast_to(a[..., None], u.shape)

            def comb(lft, rgt):
                aL, uL = lft
                aR, uR = rgt
                return (aL * aR, uL * aR + uR)
            _, s = jax.lax.associative_scan(comb, (a_b, u), axis=1)
            depool = s.reshape(bsz, plen, D_MODEL)
            plug = jnp.clip(jnp.cumsum(boundary_mask, axis=1) - 1, 0, plen - 1)
            depool_out = depool[jnp.arange(bsz)[:, None], plug]
            return depool_out + h
        key = jax.random.key(seed)
        k1, k2, k3, k4 = jax.random.split(key, 4)
        embeds = jax.random.normal(k1, (B, L, D_MODEL), dtype=jnp.float32)
        patch_embeds = jax.random.normal(k2, (B, P, D_GLOBAL), dtype=jnp.float32)
        patch_lens = jnp.full((B, P), L // P, dtype=jnp.int64)
        W_in = jax.random.normal(k3, (D_MODEL, D_MODEL), dtype=jnp.float32) * 0.02
        b_in = jnp.zeros((D_MODEL,), dtype=jnp.float32)
        g_res = jnp.ones((D_MODEL,), dtype=jnp.float32)
        g_init = jnp.ones((D_GLOBAL,), dtype=jnp.float32)
        return {'embeds': embeds, 'patch_embeds': patch_embeds, 'patch_lens': patch_lens, 'W_in': W_in, 'b_in': b_in, 'g_res': g_res, 'g_init': g_init}
    _L1_xattn_all = _L1_xattn_setup()
    _L1_xattn_in = {k: v for k, v in _L1_xattn_all.items() if k in ('W_in', 'b_in', 'g_res', 'g_init')}
    del _L1_xattn_all

    def _L1_ffn_setup():
        import jax, jax.numpy as jnp
        import numpy as np
        B, S, D, H, F = (4, 512, 128, 16, 512)
        CAP = 0.125
        ROPE_BASE = 10000.0

        def rmsnorm(x, g):
            return x * jax.lax.rsqrt(jnp.mean(x * x, -1, keepdims=True) + 1e-06) * g

        def rope(t, pos):
            hd = t.shape[-1]
            inv = 1.0 / ROPE_BASE ** (jnp.arange(0, hd, 2, dtype=jnp.float32) / hd)
            f = pos[:, None, :, None].astype(jnp.float32) * inv
            emb = jnp.concatenate([f, f], axis=-1)
            cos, sin = (jnp.cos(emb), jnp.sin(emb))
            rot = jnp.concatenate([-t[..., hd // 2:], t[..., :hd // 2]], axis=-1)
            return t * cos + rot * sin
        key = jax.random.key(seed)
        ks = jax.random.split(key, 9)
        scale = 0.02
        x = jax.random.normal(ks[0], (B, S, D), jnp.float32)
        causal = jnp.where(jnp.tril(jnp.ones((S, S), bool)), 0.0, -1000000000.0).astype(jnp.float32)
        attention_mask = jnp.broadcast_to(causal[None, None], (B, 1, S, S))
        position_ids = jnp.broadcast_to(jnp.arange(S, dtype=jnp.int32), (B, S))
        return {'x': x, 'attention_mask': attention_mask, 'position_ids': position_ids, 'router_w': jax.random.normal(ks[1], (D, 1), jnp.float32) * scale, 'router_b': jnp.zeros((1,), jnp.float32), 'wq': jax.random.normal(ks[2], (D, D), jnp.float32) * scale, 'wk': jax.random.normal(ks[3], (D, D), jnp.float32) * scale, 'wv': jax.random.normal(ks[4], (D, D), jnp.float32) * scale, 'wo': jax.random.normal(ks[5], (D, D), jnp.float32) * scale, 'w1': jax.random.normal(ks[6], (D, F), jnp.float32) * scale, 'w2': jax.random.normal(ks[7], (F, D), jnp.float32) * scale, 'ln1': jnp.ones((D,), jnp.float32), 'ln2': jnp.ones((D,), jnp.float32)}
    _L1_ffn_all = _L1_ffn_setup()
    _L1_ffn_in = {k: v for k, v in _L1_ffn_all.items() if k in ('attention_mask', 'position_ids', 'router_w', 'router_b', 'wq', 'wk', 'wv', 'wo', 'w1', 'w2', 'ln1', 'ln2')}
    del _L1_ffn_all

    def _L2_xattn_setup():
        import jax, jax.numpy as jnp
        import numpy as np
        UNITS = 128
        NUM_HEADS = 8

        def _split_heads(x, n):
            B, S, D = x.shape
            return x.reshape(B, S, n, D // n).transpose(0, 2, 1, 3)
        key = jax.random.key(seed)
        k1, k2, k3 = jax.random.split(key, 3)
        B, S = (8, 128)
        memory = jax.random.normal(k1, (B, S, 2 * UNITS), dtype=jnp.float32)
        query = jax.random.normal(k2, (B, S, UNITS), dtype=jnp.float32)
        seq_mask = jax.random.randint(k3, (B, S), 0, 2, dtype=jnp.int32)
        b = jnp.zeros((1,), dtype=jnp.float32)
        return {'memory': memory, 'query': query, 'seq_mask': seq_mask, 'b': b}
    _L2_xattn_all = _L2_xattn_setup()
    _L2_xattn_in = {k: v for k, v in _L2_xattn_all.items() if k in ('b',)}
    del _L2_xattn_all

    def _L2_ffn_setup():
        import jax, jax.numpy as jnp
        import numpy as np
        B, S, D_MODEL, D_HIDDEN = (4, 256, 128, 512)

        def act_quant(x):
            scale = 127.0 / jnp.clip(jnp.max(jnp.abs(x), axis=-1, keepdims=True), 1e-05)
            return jnp.clip(jnp.round(x * scale), -128, 127) / scale

        def weight_quant(w):
            scale = 1.0 / jnp.clip(jnp.mean(jnp.abs(w)), 1e-05)
            return jnp.clip(jnp.round(w * scale), -1, 1) / scale

        def bit_linear(x, w):
            xq = x + jax.lax.stop_gradient(act_quant(x) - x)
            wq = w + jax.lax.stop_gradient(weight_quant(w) - w)
            return jnp.einsum('bsd,hd->bsh', xq, wq)

        def depthwise_conv1d(x_bcl, w, b):
            y = jax.lax.conv_general_dilated(x_bcl, w, window_strides=(1,), padding=[(1, 1)], dimension_numbers=('NCH', 'OIH', 'NCH'), feature_group_count=x_bcl.shape[1])
            return y + b[None, :, None]
        key = jax.random.key(seed)
        ks = jax.random.split(key, 5)
        lim1 = 1.0 / np.sqrt(D_MODEL)
        lim2 = 1.0 / np.sqrt(D_HIDDEN)
        limc = 1.0 / np.sqrt(3.0)
        return {'x': jax.random.normal(ks[0], (B, S, D_MODEL), dtype=jnp.float32), 'w1': jax.random.uniform(ks[1], (D_HIDDEN, D_MODEL), jnp.float32, -lim1, lim1), 'conv_w': jax.random.uniform(ks[2], (D_HIDDEN, 1, 3), jnp.float32, -limc, limc), 'conv_b': jax.random.uniform(ks[3], (D_HIDDEN,), jnp.float32, -limc, limc), 'w2': jax.random.uniform(ks[4], (D_MODEL, D_HIDDEN), jnp.float32, -lim2, lim2)}
    _L2_ffn_all = _L2_ffn_setup()
    _L2_ffn_in = {k: v for k, v in _L2_ffn_all.items() if k in ('w1', 'conv_w', 'conv_b', 'w2')}
    del _L2_ffn_all

    def _L3_xattn_setup():
        import jax, jax.numpy as jnp
        import numpy as np
        B, S, T = (32, 64, 64)
        SRC_SIZE, TGT_SIZE, OUT_SIZE, NUM_HEAD = (256, 128, 128, 8)
        HEAD_DIM = OUT_SIZE // NUM_HEAD
        key = jax.random.key(seed)
        ks = jax.random.split(key, 12)
        src = jax.random.normal(ks[0], (B, S, SRC_SIZE), dtype=jnp.float32)
        tgt = jax.random.normal(ks[1], (B, T, TGT_SIZE), dtype=jnp.float32)
        src_mask = (jax.random.uniform(ks[2], (B, S)) > 0.3).astype(jnp.float32)
        src_mask = src_mask.at[:, 0].set(1.0)
        tgt_mask = (jax.random.uniform(ks[3], (B, T)) > 0.3).astype(jnp.float32)
        tgt_mask = tgt_mask.at[:, 0].set(1.0)

        def lin(k, out_f, in_f):
            return jax.random.normal(k, (out_f, in_f), dtype=jnp.float32) / np.sqrt(in_f)
        W_src = lin(ks[4], 2 * OUT_SIZE, SRC_SIZE)
        b_src = jnp.zeros((2 * OUT_SIZE,), jnp.float32)
        W_tgt = lin(ks[5], OUT_SIZE, TGT_SIZE)
        b_tgt = jnp.zeros((OUT_SIZE,), jnp.float32)
        W_out = lin(ks[6], OUT_SIZE, OUT_SIZE + TGT_SIZE)
        b_out = jnp.zeros((OUT_SIZE,), jnp.float32)
        return {'src': src, 'tgt': tgt, 'src_mask': src_mask, 'tgt_mask': tgt_mask, 'W_src': W_src, 'b_src': b_src, 'W_tgt': W_tgt, 'b_tgt': b_tgt, 'W_out': W_out, 'b_out': b_out}
    _L3_xattn_all = _L3_xattn_setup()
    _L3_xattn_in = {k: v for k, v in _L3_xattn_all.items() if k in ('W_src', 'b_src', 'W_tgt', 'b_tgt', 'W_out', 'b_out')}
    del _L3_xattn_all

    def _L3_ffn_setup():
        import jax, jax.numpy as jnp
        import numpy as np
        D_MODEL = 128
        N_HEADS = 16
        HEAD_DIM = D_MODEL // N_HEADS
        KV_LATENT = 64
        N_EXPERTS = 4
        D_HIDDEN = 4 * D_MODEL
        B, T = (2, 128)

        def rmsnorm(x, w, eps=1e-06):
            return w * (x * jax.lax.rsqrt(jnp.mean(x * x, axis=-1, keepdims=True) + eps))

        def layernorm(x, g, b, eps=1e-05):
            mu = jnp.mean(x, axis=-1, keepdims=True)
            var = jnp.mean((x - mu) ** 2, axis=-1, keepdims=True)
            return (x - mu) * jax.lax.rsqrt(var + eps) * g + b

        def apply_rope(x):
            t, d = (x.shape[2], x.shape[3])
            half = d // 2
            pos = jnp.arange(t, dtype=x.dtype)[:, None]
            inv_freq = 1.0 / 10000.0 ** (jnp.arange(half, dtype=x.dtype) / half)
            ang = pos * inv_freq[None, :]
            sin, cos = (jnp.sin(ang), jnp.cos(ang))
            x1, x2 = (x[..., :half], x[..., half:])
            return jnp.concatenate([x1 * cos - x2 * sin, x1 * sin + x2 * cos], axis=-1)

        def mla_attention(x, Wq, Wdkv, Wuk, Wuv, Wo, ln_g, ln_b):
            b, t, _ = x.shape
            q = (x @ Wq.T).reshape(b, t, N_HEADS, HEAD_DIM).transpose(0, 2, 1, 3)
            latent = layernorm(x @ Wdkv.T, ln_g, ln_b)
            k = (latent @ Wuk.T).reshape(b, t, N_HEADS, HEAD_DIM).transpose(0, 2, 1, 3)
            v = (latent @ Wuv.T).reshape(b, t, N_HEADS, HEAD_DIM).transpose(0, 2, 1, 3)
            q = apply_rope(q)
            k = apply_rope(k)
            scores = jnp.einsum('bhqd,bhkd->bhqk', q, k) / np.sqrt(HEAD_DIM)
            causal = jnp.tril(jnp.ones((t, t), dtype=bool))
            scores = jnp.where(causal, scores, -jnp.inf)
            attn = jax.nn.softmax(scores, axis=-1)
            out = jnp.einsum('bhqk,bhkd->bhqd', attn, v).transpose(0, 2, 1, 3).reshape(b, t, D_MODEL)
            return out @ Wo.T

        def moe(x, gate_w, gate_b, W1, b1, W2, b2):
            logits = x @ gate_w.T + gate_b
            top = jnp.argmax(logits, axis=-1)
            onehot = jax.nn.one_hot(top, N_EXPERTS, dtype=x.dtype)
            h = jax.nn.relu(jnp.einsum('btd,ehd->bteh', x, W1) + b1)
            y = jnp.einsum('bteh,edh->bted', h, W2) + b2
            return jnp.einsum('bted,bte->btd', y, onehot)
        key = jax.random.key(seed)
        ks = jax.random.split(key, 16)
        s = lambda fan_in: 1.0 / np.sqrt(fan_in)
        return {'x': jax.random.normal(ks[0], (B, T, D_MODEL), jnp.float32), 'norm1_w': jnp.ones((D_MODEL,), jnp.float32), 'norm2_w': jnp.ones((D_MODEL,), jnp.float32), 'Wq': jax.random.normal(ks[1], (D_MODEL, D_MODEL), jnp.float32) * s(D_MODEL), 'Wdkv': jax.random.normal(ks[2], (KV_LATENT, D_MODEL), jnp.float32) * s(D_MODEL), 'Wuk': jax.random.normal(ks[3], (D_MODEL, KV_LATENT), jnp.float32) * s(KV_LATENT), 'Wuv': jax.random.normal(ks[4], (D_MODEL, KV_LATENT), jnp.float32) * s(KV_LATENT), 'Wo': jax.random.normal(ks[5], (D_MODEL, D_MODEL), jnp.float32) * s(D_MODEL), 'ln_g': jnp.ones((KV_LATENT,), jnp.float32), 'ln_b': jnp.zeros((KV_LATENT,), jnp.float32), 'gate_w': jax.random.normal(ks[6], (N_EXPERTS, D_MODEL), jnp.float32) * s(D_MODEL), 'gate_b': jnp.zeros((N_EXPERTS,), jnp.float32), 'W1': jax.random.normal(ks[7], (N_EXPERTS, D_HIDDEN, D_MODEL), jnp.float32) * s(D_MODEL), 'b1': jnp.zeros((N_EXPERTS, D_HIDDEN), jnp.float32), 'W2': jax.random.normal(ks[8], (N_EXPERTS, D_MODEL, D_HIDDEN), jnp.float32) * s(D_HIDDEN), 'b2': jnp.zeros((N_EXPERTS, D_MODEL), jnp.float32)}
    _L3_ffn_all = _L3_ffn_setup()
    _L3_ffn_in = {k: v for k, v in _L3_ffn_all.items() if k in ('norm1_w', 'norm2_w', 'Wq', 'Wdkv', 'Wuk', 'Wuv', 'Wo', 'ln_g', 'ln_b', 'gate_w', 'gate_b', 'W1', 'b1', 'W2', 'b2')}
    del _L3_ffn_all
    return {'x': x, 'ctx_2048': ctx_2048, 'itok_Bx1_68_817': itok_Bx1_68_817, 'mask_BxS2_if0': mask_BxS2_if0, 'mask_BxS2_ik0': mask_BxS2_ik0, 'mask_BxS2_fk1': mask_BxS2_fk1, 'L0_xattn_b': _L0_xattn_in['b'], 'L0_ffn_w1': _L0_ffn_in['w1'], 'L0_ffn_w2': _L0_ffn_in['w2'], 'L1_xattn_W_in': _L1_xattn_in['W_in'], 'L1_xattn_b_in': _L1_xattn_in['b_in'], 'L1_xattn_g_res': _L1_xattn_in['g_res'], 'L1_xattn_g_init': _L1_xattn_in['g_init'], 'L1_ffn_attention_mask': _L1_ffn_in['attention_mask'], 'L1_ffn_position_ids': _L1_ffn_in['position_ids'], 'L1_ffn_router_w': _L1_ffn_in['router_w'], 'L1_ffn_router_b': _L1_ffn_in['router_b'], 'L1_ffn_wq': _L1_ffn_in['wq'], 'L1_ffn_wk': _L1_ffn_in['wk'], 'L1_ffn_wv': _L1_ffn_in['wv'], 'L1_ffn_wo': _L1_ffn_in['wo'], 'L1_ffn_w1': _L1_ffn_in['w1'], 'L1_ffn_w2': _L1_ffn_in['w2'], 'L1_ffn_ln1': _L1_ffn_in['ln1'], 'L1_ffn_ln2': _L1_ffn_in['ln2'], 'L2_xattn_b': _L2_xattn_in['b'], 'L2_ffn_w1': _L2_ffn_in['w1'], 'L2_ffn_conv_w': _L2_ffn_in['conv_w'], 'L2_ffn_conv_b': _L2_ffn_in['conv_b'], 'L2_ffn_w2': _L2_ffn_in['w2'], 'L3_xattn_W_src': _L3_xattn_in['W_src'], 'L3_xattn_b_src': _L3_xattn_in['b_src'], 'L3_xattn_W_tgt': _L3_xattn_in['W_tgt'], 'L3_xattn_b_tgt': _L3_xattn_in['b_tgt'], 'L3_xattn_W_out': _L3_xattn_in['W_out'], 'L3_xattn_b_out': _L3_xattn_in['b_out'], 'L3_ffn_norm1_w': _L3_ffn_in['norm1_w'], 'L3_ffn_norm2_w': _L3_ffn_in['norm2_w'], 'L3_ffn_Wq': _L3_ffn_in['Wq'], 'L3_ffn_Wdkv': _L3_ffn_in['Wdkv'], 'L3_ffn_Wuk': _L3_ffn_in['Wuk'], 'L3_ffn_Wuv': _L3_ffn_in['Wuv'], 'L3_ffn_Wo': _L3_ffn_in['Wo'], 'L3_ffn_ln_g': _L3_ffn_in['ln_g'], 'L3_ffn_ln_b': _L3_ffn_in['ln_b'], 'L3_ffn_gate_w': _L3_ffn_in['gate_w'], 'L3_ffn_gate_b': _L3_ffn_in['gate_b'], 'L3_ffn_W1': _L3_ffn_in['W1'], 'L3_ffn_b1': _L3_ffn_in['b1'], 'L3_ffn_W2': _L3_ffn_in['W2'], 'L3_ffn_b2': _L3_ffn_in['b2']}

def reference(x, ctx_2048, itok_Bx1_68_817, mask_BxS2_if0, mask_BxS2_ik0, mask_BxS2_fk1, L0_xattn_b, L0_ffn_w1, L0_ffn_w2, L1_xattn_W_in, L1_xattn_b_in, L1_xattn_g_res, L1_xattn_g_init, L1_ffn_attention_mask, L1_ffn_position_ids, L1_ffn_router_w, L1_ffn_router_b, L1_ffn_wq, L1_ffn_wk, L1_ffn_wv, L1_ffn_wo, L1_ffn_w1, L1_ffn_w2, L1_ffn_ln1, L1_ffn_ln2, L2_xattn_b, L2_ffn_w1, L2_ffn_conv_w, L2_ffn_conv_b, L2_ffn_w2, L3_xattn_W_src, L3_xattn_b_src, L3_xattn_W_tgt, L3_xattn_b_tgt, L3_xattn_W_out, L3_xattn_b_out, L3_ffn_norm1_w, L3_ffn_norm2_w, L3_ffn_Wq, L3_ffn_Wdkv, L3_ffn_Wuk, L3_ffn_Wuv, L3_ffn_Wo, L3_ffn_ln_g, L3_ffn_ln_b, L3_ffn_gate_w, L3_ffn_gate_b, L3_ffn_W1, L3_ffn_b1, L3_ffn_W2, L3_ffn_b2):
    import jax
    import jax.numpy as jnp

    def _L0_xattn_ref(memory, query, b, seq_len):
        import jax, jax.numpy as jnp
        import numpy as np
        UNITS = 128
        NUM_HEADS = 16
        MASK_VALUE = -1000000000000.0

        def _split_heads(x, n):
            B, S, D = x.shape
            return x.reshape(B, S, n, D // n).transpose(0, 2, 1, 3)
        B, S, _ = query.shape
        dh = UNITS // NUM_HEADS
        k_mem, v_mem = jnp.split(memory, 2, axis=2)
        Q = _split_heads(query, NUM_HEADS) * dh ** (-0.5)
        Kh = _split_heads(k_mem, NUM_HEADS)
        Vh = _split_heads(v_mem, NUM_HEADS)
        logits = jnp.einsum('bhqd,bhkd->bhqk', Q, Kh) + b
        valid = (jnp.arange(S)[None, :] < seq_len[:, 0:1]).astype(jnp.float32)
        logits = logits + MASK_VALUE * (1.0 - valid)[:, None, None, :]
        weights = jax.nn.softmax(logits, axis=-1)
        out = jnp.einsum('bhqk,bhkd->bhqd', weights, Vh)
        return out.transpose(0, 2, 1, 3).reshape(B, S, UNITS)

    def _L0_ffn_ref(x, w1, w2):
        import jax, jax.numpy as jnp
        import numpy as np
        A, M, H = (4, 128, 128)
        E, N = (8, 512)
        mid = jnp.einsum('amh,ehn->aemn', x, w1)
        out = jnp.einsum('aemn,enh->amh', mid, w2)
        return out

    def _L1_xattn_ref(embeds, patch_embeds, patch_lens, W_in, b_in, g_res, g_init):
        import jax, jax.numpy as jnp
        import numpy as np
        B, L, P = (4, 512, 128)
        D_MODEL = 128
        D_GLOBAL = 256
        HEADDIM = 32
        EPSILON = 0.001
        RMS_EPS = 1e-05

        def rmsnorm(x, g, eps=RMS_EPS):
            var = jnp.mean(jnp.square(x), axis=-1, keepdims=True)
            return x * jax.lax.rsqrt(var + eps) * g

        def _hnet_depool(h, h_patch_full, patch_lens):
            h_patch = h_patch_full[..., :D_MODEL]
            bsz, plen = (h_patch.shape[0], h_patch.shape[1])
            seqlen = h.shape[1]
            logp = jnp.full((bsz, plen), -EPSILON, dtype=jnp.float32)
            bidx = jnp.cumsum(patch_lens, axis=1) - 1
            boundary_mask = jnp.zeros((bsz, seqlen), dtype=jnp.int32)
            boundary_mask = boundary_mask.at[jnp.arange(bsz)[:, None], bidx].set(1)
            dt = (-jnp.log(-jnp.expm1(logp))).astype(h_patch.dtype)
            x = h_patch / dt[..., None]
            n_heads = D_MODEL // HEADDIM
            A = -jnp.ones((n_heads,), dtype=jnp.float32)
            bcoef = jnp.exp(logp).astype(h_patch.dtype)
            x4 = x.reshape(bsz, plen, n_heads, HEADDIM)
            a = jnp.exp(dt[:, :, None] * A[None, None, :])
            u = (dt * bcoef)[:, :, None, None] * x4
            a_b = jnp.broadcast_to(a[..., None], u.shape)

            def comb(lft, rgt):
                aL, uL = lft
                aR, uR = rgt
                return (aL * aR, uL * aR + uR)
            _, s = jax.lax.associative_scan(comb, (a_b, u), axis=1)
            depool = s.reshape(bsz, plen, D_MODEL)
            plug = jnp.clip(jnp.cumsum(boundary_mask, axis=1) - 1, 0, plen - 1)
            depool_out = depool[jnp.arange(bsz)[:, None], plug]
            return depool_out + h
        h = rmsnorm(embeds, g_res)
        h = jnp.einsum('bld,ed->ble', h, W_in) + b_in
        h_patch = rmsnorm(patch_embeds, g_init)
        return _hnet_depool(h, h_patch, patch_lens)

    def _L1_ffn_ref(x, attention_mask, position_ids, router_w, router_b, wq, wk, wv, wo, w1, w2, ln1, ln2):
        import jax, jax.numpy as jnp
        import numpy as np
        B, S, D, H, F = (4, 512, 128, 16, 512)
        CAP = 0.125
        ROPE_BASE = 10000.0

        def rmsnorm(x, g):
            return x * jax.lax.rsqrt(jnp.mean(x * x, -1, keepdims=True) + 1e-06) * g

        def rope(t, pos):
            hd = t.shape[-1]
            inv = 1.0 / ROPE_BASE ** (jnp.arange(0, hd, 2, dtype=jnp.float32) / hd)
            f = pos[:, None, :, None].astype(jnp.float32) * inv
            emb = jnp.concatenate([f, f], axis=-1)
            cos, sin = (jnp.cos(emb), jnp.sin(emb))
            rot = jnp.concatenate([-t[..., hd // 2:], t[..., :hd // 2]], axis=-1)
            return t * cos + rot * sin
        b, s, d = x.shape
        hd = d // H
        weights = (x @ router_w)[..., 0] + router_b[0]
        k = int(CAP * s)
        topv, topi = jax.lax.top_k(weights, k)
        thr = topv[:, -1]
        sel_mask = (weights > thr[:, None]).astype(x.dtype)
        kc = k - 1
        sel_idx = jnp.sort(topi[:, :kc], axis=1)
        bidx = jnp.arange(b)[:, None]
        x_sel = x[bidx, sel_idx]
        pos_sel = position_ids[bidx, sel_idx]
        w_sel = weights[bidx, sel_idx]
        m = attention_mask[:, 0]
        m_sel = m[bidx[:, :, None], sel_idx[:, :, None], sel_idx[:, None, :]]
        hn = rmsnorm(x_sel, ln1)

        def heads(t):
            return t.reshape(b, kc, H, hd).transpose(0, 2, 1, 3)
        q = rope(heads(hn @ wq), pos_sel)
        kk = rope(heads(hn @ wk), pos_sel)
        v = heads(hn @ wv)
        sc = jnp.einsum('bhqd,bhkd->bhqk', q, kk) / np.sqrt(hd).astype(np.float32)
        sc = sc + m_sel[:, None]
        a = jax.nn.softmax(sc, axis=-1)
        o = jnp.einsum('bhqk,bhkd->bhqd', a, v).transpose(0, 2, 1, 3).reshape(b, kc, d) @ wo
        x1 = x_sel + o
        x2 = x1 + jax.nn.gelu(rmsnorm(x1, ln2) @ w1) @ w2
        proc = x2 * w_sel[..., None]
        out = jnp.zeros_like(x).at[bidx, sel_idx].set(proc)
        return out + x * (1.0 - sel_mask)[..., None]

    def _L2_xattn_ref(memory, query, seq_mask, b):
        import jax, jax.numpy as jnp
        import numpy as np
        UNITS = 128
        NUM_HEADS = 8

        def _split_heads(x, n):
            B, S, D = x.shape
            return x.reshape(B, S, n, D // n).transpose(0, 2, 1, 3)
        H = NUM_HEADS
        depth = UNITS // H
        Q = _split_heads(query, H) * depth ** (-0.5)
        k_mem, v_mem = jnp.split(memory, 2, axis=2)
        K = _split_heads(k_mem, H)
        V = _split_heads(v_mem, H)
        logits = jnp.einsum('bhqd,bhkd->bhqk', Q, K) + b[0]
        mask = seq_mask.astype(jnp.float32)[:, None, None, :]
        logits = logits + -1e+30 * (1.0 - mask)
        weights = jax.nn.softmax(logits, axis=-1)
        out = jnp.einsum('bhqk,bhkd->bhqd', weights, V)
        B, _, S, _ = out.shape
        return out.transpose(0, 2, 1, 3).reshape(B, S, UNITS)

    def _L2_ffn_ref(x, w1, conv_w, conv_b, w2):
        import jax, jax.numpy as jnp
        import numpy as np
        B, S, D_MODEL, D_HIDDEN = (4, 256, 128, 512)

        def act_quant(x):
            scale = 127.0 / jnp.clip(jnp.max(jnp.abs(x), axis=-1, keepdims=True), 1e-05)
            return jnp.clip(jnp.round(x * scale), -128, 127) / scale

        def weight_quant(w):
            scale = 1.0 / jnp.clip(jnp.mean(jnp.abs(w)), 1e-05)
            return jnp.clip(jnp.round(w * scale), -1, 1) / scale

        def bit_linear(x, w):
            xq = x + jax.lax.stop_gradient(act_quant(x) - x)
            wq = w + jax.lax.stop_gradient(weight_quant(w) - w)
            return jnp.einsum('bsd,hd->bsh', xq, wq)

        def depthwise_conv1d(x_bcl, w, b):
            y = jax.lax.conv_general_dilated(x_bcl, w, window_strides=(1,), padding=[(1, 1)], dimension_numbers=('NCH', 'OIH', 'NCH'), feature_group_count=x_bcl.shape[1])
            return y + b[None, :, None]
        h = bit_linear(x, w1)
        h = depthwise_conv1d(h.transpose(0, 2, 1), conv_w, conv_b)
        h = h.transpose(0, 2, 1)
        h = jax.nn.silu(h)
        return bit_linear(h, w2)

    def _L3_xattn_ref(src, tgt, src_mask, tgt_mask, W_src, b_src, W_tgt, b_tgt, W_out, b_out):
        import jax, jax.numpy as jnp
        import numpy as np
        B, S, T = (32, 64, 64)
        SRC_SIZE, TGT_SIZE, OUT_SIZE, NUM_HEAD = (256, 128, 128, 8)
        HEAD_DIM = OUT_SIZE // NUM_HEAD
        b, s, _ = src.shape
        t = tgt.shape[1]
        src_trans = jnp.einsum('bsf,of->bso', src, W_src) + b_src
        tgt_trans = jnp.einsum('btf,of->bto', tgt, W_tgt) + b_tgt
        src_trans = src_trans * src_mask[:, :, None]
        tgt_trans = tgt_trans * tgt_mask[:, :, None]
        src_key, src_val = jnp.split(src_trans, 2, axis=2)
        k = src_key.reshape(b, s, NUM_HEAD, HEAD_DIM)
        v = src_val.reshape(b, s, NUM_HEAD, HEAD_DIM)
        q = tgt_trans.reshape(b, t, NUM_HEAD, HEAD_DIM)
        scores = jnp.einsum('bthd,bshd->bhts', q, k) / np.sqrt(HEAD_DIM)
        scores = jnp.where(src_mask[:, None, None, :] == 0, -jnp.inf, scores)
        attn = jax.nn.softmax(scores, axis=-1)
        tgt_update = jnp.einsum('bhts,bshd->bthd', attn, v).reshape(b, t, OUT_SIZE)
        cat_tgt = jnp.concatenate([tgt, tgt_update], axis=2)
        return jnp.einsum('btf,of->bto', cat_tgt, W_out) + b_out

    def _L3_ffn_ref(x, norm1_w, norm2_w, Wq, Wdkv, Wuk, Wuv, Wo, ln_g, ln_b, gate_w, gate_b, W1, b1, W2, b2):
        import jax, jax.numpy as jnp
        import numpy as np
        D_MODEL = 128
        N_HEADS = 16
        HEAD_DIM = D_MODEL // N_HEADS
        KV_LATENT = 64
        N_EXPERTS = 4
        D_HIDDEN = 4 * D_MODEL
        B, T = (2, 128)

        def rmsnorm(x, w, eps=1e-06):
            return w * (x * jax.lax.rsqrt(jnp.mean(x * x, axis=-1, keepdims=True) + eps))

        def layernorm(x, g, b, eps=1e-05):
            mu = jnp.mean(x, axis=-1, keepdims=True)
            var = jnp.mean((x - mu) ** 2, axis=-1, keepdims=True)
            return (x - mu) * jax.lax.rsqrt(var + eps) * g + b

        def apply_rope(x):
            t, d = (x.shape[2], x.shape[3])
            half = d // 2
            pos = jnp.arange(t, dtype=x.dtype)[:, None]
            inv_freq = 1.0 / 10000.0 ** (jnp.arange(half, dtype=x.dtype) / half)
            ang = pos * inv_freq[None, :]
            sin, cos = (jnp.sin(ang), jnp.cos(ang))
            x1, x2 = (x[..., :half], x[..., half:])
            return jnp.concatenate([x1 * cos - x2 * sin, x1 * sin + x2 * cos], axis=-1)

        def mla_attention(x, Wq, Wdkv, Wuk, Wuv, Wo, ln_g, ln_b):
            b, t, _ = x.shape
            q = (x @ Wq.T).reshape(b, t, N_HEADS, HEAD_DIM).transpose(0, 2, 1, 3)
            latent = layernorm(x @ Wdkv.T, ln_g, ln_b)
            k = (latent @ Wuk.T).reshape(b, t, N_HEADS, HEAD_DIM).transpose(0, 2, 1, 3)
            v = (latent @ Wuv.T).reshape(b, t, N_HEADS, HEAD_DIM).transpose(0, 2, 1, 3)
            q = apply_rope(q)
            k = apply_rope(k)
            scores = jnp.einsum('bhqd,bhkd->bhqk', q, k) / np.sqrt(HEAD_DIM)
            causal = jnp.tril(jnp.ones((t, t), dtype=bool))
            scores = jnp.where(causal, scores, -jnp.inf)
            attn = jax.nn.softmax(scores, axis=-1)
            out = jnp.einsum('bhqk,bhkd->bhqd', attn, v).transpose(0, 2, 1, 3).reshape(b, t, D_MODEL)
            return out @ Wo.T

        def moe(x, gate_w, gate_b, W1, b1, W2, b2):
            logits = x @ gate_w.T + gate_b
            top = jnp.argmax(logits, axis=-1)
            onehot = jax.nn.one_hot(top, N_EXPERTS, dtype=x.dtype)
            h = jax.nn.relu(jnp.einsum('btd,ehd->bteh', x, W1) + b1)
            y = jnp.einsum('bteh,edh->bted', h, W2) + b2
            return jnp.einsum('bted,bte->btd', y, onehot)
        x = x + mla_attention(rmsnorm(x, norm1_w), Wq, Wdkv, Wuk, Wuv, Wo, ln_g, ln_b)
        x = x + moe(rmsnorm(x, norm2_w), gate_w, gate_b, W1, b1, W2, b2)
        return x
    x = x + _L0_xattn_ref(ctx_2048, _layernorm(x, axis=-1), L0_xattn_b, itok_Bx1_68_817)
    x = x + _L0_ffn_ref(_layernorm(x, axis=-1), L0_ffn_w1, L0_ffn_w2)
    x = x + _L1_xattn_ref(_layernorm(x, axis=-1), ctx_2048, mask_BxS2_if0, L1_xattn_W_in, L1_xattn_b_in, L1_xattn_g_res, L1_xattn_g_init)
    x = x + _L1_ffn_ref(_layernorm(x, axis=-1), L1_ffn_attention_mask, L1_ffn_position_ids, L1_ffn_router_w, L1_ffn_router_b, L1_ffn_wq, L1_ffn_wk, L1_ffn_wv, L1_ffn_wo, L1_ffn_w1, L1_ffn_w2, L1_ffn_ln1, L1_ffn_ln2)
    x = x + _L2_xattn_ref(ctx_2048, _layernorm(x, axis=-1), mask_BxS2_ik0, L2_xattn_b)
    x = x + _L2_ffn_ref(_layernorm(x, axis=-1), L2_ffn_w1, L2_ffn_conv_w, L2_ffn_conv_b, L2_ffn_w2)
    x = x + _L3_xattn_ref(ctx_2048, _layernorm(x, axis=-1), mask_BxS2_fk1, mask_BxS2_fk1, L3_xattn_W_src, L3_xattn_b_src, L3_xattn_W_tgt, L3_xattn_b_tgt, L3_xattn_W_out, L3_xattn_b_out)
    x = x + _L3_ffn_ref(_layernorm(x, axis=-1), L3_ffn_norm1_w, L3_ffn_norm2_w, L3_ffn_Wq, L3_ffn_Wdkv, L3_ffn_Wuk, L3_ffn_Wuv, L3_ffn_Wo, L3_ffn_ln_g, L3_ffn_ln_b, L3_ffn_gate_w, L3_ffn_gate_b, L3_ffn_W1, L3_ffn_b1, L3_ffn_W2, L3_ffn_b2)
    return x

_drawn_inputs = setup_inputs


def setup_inputs(seed=0):
    import zlib

    import numpy as np

    out = dict(_drawn_inputs(seed))
    spreads = {'L1_xattn_b_in': (0.0, 0.1),
     'L1_xattn_g_res': (1.0, 0.2),
     'L1_xattn_g_init': (1.0, 0.2),
     'L1_ffn_ln1': (1.0, 0.6),
     'L1_ffn_ln2': (1.0, 0.6),
     'L3_xattn_b_src': (0.0, 0.1),
     'L3_xattn_b_tgt': (0.0, 0.515),
     'L3_xattn_b_out': (0.0, 0.1),
     'L3_ffn_norm1_w': (1.0, 0.2),
     'L3_ffn_norm2_w': (1.0, 0.2),
     'L3_ffn_ln_g': (1.0, 0.2),
     'L3_ffn_ln_b': (0.0, 0.1),
     'L3_ffn_gate_b': (0.0, 0.1),
     'L3_ffn_b1': (0.0, 0.457),
     'L3_ffn_b2': (0.0, 0.319)}
    factors = {'L1_ffn_wq': 8.0,
     'L1_ffn_wk': 8.0,
     'L1_ffn_wv': 8.0,
     'L1_ffn_wo': 8.0,
     'L1_ffn_w1': 7.375,
     'L1_ffn_w2': 8.0}
    for name, (base, spread) in spreads.items():
        noise = np.random.default_rng([zlib.crc32(name.encode()), seed]).standard_normal(out[name].shape)
        drawn = base * np.exp(spread * noise) if base else spread * noise
        out[name] = jnp.asarray(drawn.astype(out[name].dtype))
    for name, factor in factors.items():
        out[name] = (out[name] * factor).astype(out[name].dtype)
    return out
```

```python
from contextlib import ExitStack

import numpy as np

import concourse.bass as bass
from concourse import mybir

F32 = mybir.dt.float32
BF16 = mybir.dt.bfloat16
I32 = mybir.dt.int32
ALU = mybir.AluOpType
ACT = mybir.ActivationFunctionType
AX = mybir.AxisListType

B, S, D = 32, 128, 128
C = 2 * D
N_EXP0, N_HID0 = 8, 512
HID = 512
N_EXP3 = 4
LATENT = 64
TILES, PER_TILE, SLOTS = 4, 8, 16
KEPT = int(0.125 * S) - 1
RING = 4
BIG = -1.0e30
TWO_PI = 2.0 * np.pi
PI_PARTS = (6.28125, 1.93500518798828125e-3, 3.0199159795e-7)
SIN_LIMIT = 3.1415925
PATCH_GAIN = float(np.exp(-0.001))
MAGIC = 12582912.0


def steps(engine, count, work):
    last = max(lag for lag, _ in work)

    def step(items):
        for lag, stage in work:
            if lag in items:
                stage(*items[lag])
    whole_steps(engine, count, last, step)


def whole_steps(engine, count, last, step):
    first = -(-(last + RING) // RING) * RING

    def plain(t):
        step({lag: (t - lag, (t - lag) % RING) for lag in range(last + 1) if 0 <= t - lag < count})

    if count < first + RING:
        for t in range(count + last):
            plain(t)
        return
    for t in range(first):
        plain(t)
    with engine.Fori(first // RING, count // RING) as round_:
        for u in range(RING):
            step({lag: (round_ * RING + (u - lag), (u - lag) % RING) for lag in range(last + 1)})
    for t in range(count, count + last):
        plain(t)


def wait_reuse(engine, signal, item, depth, per_item=1):
    if isinstance(item, int) and item < depth:
        return
    semaphore, begun = signal
    engine.wait_ge(semaphore, item * per_item + (begun - (depth - 1) * per_item))


class Link:

    def __init__(self, engine, signal, item, per_item, held=None):
        self.held, self.engine, self.per_item, self.n = held, engine, per_item, 0
        self.sem, begun = signal
        self.base = item * per_item + begun

    def __call__(self, instruction):
        self.n += 1
        instruction.then_inc(self.sem, 1)
        self.engine.wait_ge(self.sem, self.base + self.n)
        if self.held is not None:
            self.engine.sem_inc(self.held, 1)

    def count(self, instruction):
        self.n += 1
        instruction.then_inc(self.sem, 1)
        return self

    def end(self):
        assert self.n == self.per_item, (self.n, self.per_item)


def in_turns(*chains):
    going = list(chains)
    waits = {}
    while going:
        for chain in list(going):
            if chain in waits:
                link, n = waits.pop(chain)
                link.engine.wait_ge(link.sem, link.base + n)
            link = next(chain, None)
            if link is None:
                going.remove(chain)
            else:
                waits[chain] = link, link.n


class Seq:

    def __init__(self, engine, signal, counts):
        self.engine, self.sem, self.counts = engine, signal, counts

    def __call__(self, instruction):
        self.counts[self.sem] = self.counts.get(self.sem, 0) + 1
        instruction.then_inc(self.sem, 1)
        self.engine.wait_ge(self.sem, self.counts[self.sem])


def rows_of(heads):
    dh = D // heads
    return dh, (64 if dh == 8 else 128), heads // 8


def head_at(at, R):
    return at if R == 128 else at // 8 * 8 + at % 4 * 2 + at % 8 // 4


def build(nc, t_in, out):
    with ExitStack() as ctx_:
        sems = {}

        def sem(name):
            if name not in sems:
                sems[name] = ctx_.enter_context(nc.semaphore(name))
            return sems[name]

        begun = {}

        def after(name, n=0):
            return sem(name), n + begun.get(name, 0)

        def hold(engine):
            engine.sem_inc(sem("held_" + engine_name[engine]), 1)

        engine_name = {}

        def sb(name, shape, dt=F32):
            return ctx_.enter_context(nc.sbuf_tensor(name, shape, dt))

        x_all = sb("x_all", [S, B, D])
        ctx_all = sb("ctx_all", [S, B, C])
        q_all = sb("q_all", [S, B, D])
        kv_all = sb("kv_all", [S, B, C])
        ident = sb("ident", [128, 128])
        identb = sb("identb", [128, 128], BF16)
        upper = sb("upper", [128, 128])
        upperb = sb("upperb", [128, 128], BF16)
        below = sb("below", [128, 128])
        above = sb("above", [128, 128])
        ones = sb("ones", [128, 128])
        onesb = sb("onesb", [128, 128], BF16)
        iota_p = sb("iota_p", [128, 3])
        iota_row = sb("iota_row", [128, SLOTS])
        sel = sb("sel", [128, 16, 128], BF16)
        sel_col = sb("sel_col", [128, 16])
        k_scale = sb("k_scale", [128, 2, B])
        bias3 = sb("bias3", [128, 3, B, 3], BF16)
        small = sb("small", [128, 256])

        ps = ctx_.enter_context(nc.psum_tensor("ps", [128, 8, 512], F32))
        q_pad = sb("q_pad", [128, 2, 1024], BF16)
        k_pad = sb("k_pad", [128, 2, 1024], BF16)
        qT = sb("qT", [128, RING, 8, 128], BF16)
        kT = sb("kT", [128, RING, 8, 128], BF16)
        probs = sb("probs", [128, 2, 16 * 128])
        v_wide = sb("v_wide", [128, 2, 2, 648])
        pv = sb("pv", [72, 2, 256])
        row32 = sb("row32", [128, 2, 128])
        key32 = sb("key32", [128, 2, 128])
        rest = sb("rest", [128, 2, 128])
        k_rest = sb("k_rest", [128, 2, 128])
        neg_max = sb("neg_max", [128, RING, 16])
        nm_rest = sb("nm_rest", [128, 16])
        nm3 = sb("nm3", [128, RING, 128], BF16)
        nmT = sb("nmT", [128, RING, 128], BF16)
        inv_den = sb("inv_den", [128, 2, 16])
        o_sb = sb("o_sb", [128, 2, 128])
        oT = sb("oT", [128, 2, 128])
        stat = sb("stat", [128, TILES, 6])
        stats_all = sb("stats_all", [128, B, 6])
        mean_all = sb("mean_all", [128, B])
        inv_all = sb("inv_all", [128, B])
        moment = sb("moment", [128, 4, B])
        mv = sb("mv", [128, 2, 8])
        bank_b = [ps[:, i, :].bitcast(BF16) for i in range(8)]

        moments_taken = {}

        def moments_vector(dve, kind, stats=None, n=B):
            c = moments_taken["v"] = moments_taken.get("v", 0) + 1
            st = stats_all[:] if stats is None else stats
            q = Seq(dve, sem("moments_link"), moments_taken)
            mean, inv = mean_all[:, 0:n], inv_all[:, 0:n]
            half, var, root, t = (moment[:, i, 0:n] for i in range(4))
            V = nc.vector
            if kind != "direct":
                q(V.tensor_tensor(mean, st[:, :, 1], st[:, :, 4], ALU.add))
                q(V.tensor_scalar(mean, mean, 0.5, None, ALU.mult))
                q(V.tensor_tensor(half, st[:, :, 1], mean, ALU.subtract))
                q(V.tensor_tensor(half, half, half, ALU.mult))
                q(V.tensor_tensor(var, st[:, :, 2], st[:, :, 5], ALU.add))
                q(V.scalar_tensor_tensor(var, var, 1.0 / D, half, ALU.mult, ALU.add))
            if kind == "ln":
                q(V.tensor_scalar(var, var, 1e-5, None, ALU.add))
            elif kind == "ln_rms":
                q(V.tensor_scalar(var, var, 1.0 + 1e-5, 1e-10, ALU.mult, ALU.add))
            elif kind == "ln_rms6":
                q(V.tensor_scalar(var, var, 1.0 + 1e-6, 1e-11, ALU.mult, ALU.add))
            elif kind == "rms":
                q(V.tensor_tensor(half, mean, mean, ALU.mult))
                q(V.tensor_tensor(var, var, half, ALU.add))
                q(V.tensor_scalar(var, var, 1e-6, None, ALU.add))
            else:
                q(V.tensor_scalar(var, var, 1.0 / C, 1e-5, ALU.mult, ALU.add))
            dve.sem_inc(sem("variance"), 1)
            dve.wait_ge(sem("deviation"), c)
            q(V.reciprocal(inv, root))
            q(V.tensor_tensor(t, inv, inv, ALU.mult))
            q(V.tensor_tensor(t, t, var, ALU.mult))
            q(V.tensor_scalar(t, t, -0.5, 1.5, ALU.mult, ALU.add))
            q(V.tensor_tensor(inv, inv, t, ALU.mult))

        def moments_scalar(act, n=B):
            c = moments_taken["s"] = moments_taken.get("s", 0) + 1
            act.wait_ge(sem("variance"), c)
            nc.scalar.activation(moment[:, 2, 0:n], moment[:, 1, 0:n], ACT.Sqrt).then_inc(sem("deviation"), 1)

        def norm(dst, b, k=None):
            return nc.vector.tensor_scalar(dst, x_all[:, b, :], mean_all[:, bass.ts(b, 1)], inv_all[:, bass.ts(b, 1)],
                                           ALU.subtract, ALU.mult)

        def measure(dve, updated, b, rows=x_all):
            dve.wait_ge(updated[0], updated[1] + b + 1)
            nc.vector.bn_stats(stats_all[:, b, :], rows[:, b, :]).then_inc(sem("measured"), 1)

        def attention_counts(count, heads, raw, post):
            NU = rows_of(heads)[2]
            once = ("q_padded", "k_padded", "v_ready", "q_turned", "k_turned", "qT_ready", "kT_ready", "nm_split",
                    "nm_turned", "nmT_ready", "weighted", "o_ready")
            counts = {n: count for n in once + (("k_scaled",) if raw else ())
                      + (("o_turned", "oT_ready", "projected", "x_updated") if post else ())
                      + ("pv_ready", "pv_turned")}
            counts.update({n: count * NU for n in ("raw_scores", "max_taken", "scores", "probs_ready")})
            counts.update(q_link=count * (4 if raw else 3), k_link=count * 5, nm_link=count * 3,
                          o_link=count * (1 if post else 2))
            return counts

        def attention_vector(dve, L, count, heads, normalise, post):
            dh, R, NU = rows_of(heads)

            def split_q(b, k):
                link = Link(dve, after("q_link"), b, 4 if normalise else 3)
                if normalise:
                    yield link.count(norm(row32[:, k % 2, :], b))
                    src = row32[:, k % 2, :]
                else:
                    src = q_all[:, b, :]
                src = src.rearrange("p (h d) -> p h d", h=heads)
                pad = q_pad[:, k % 2, :].rearrange("p (h r) -> p h r", h=heads)
                left = rest[:, k % 2, :].rearrange("p (h d) -> p h d", h=heads)

                def groups(a, n):
                    return pad[:, :, a * dh:(a + n) * dh].rearrange("p h (n d) -> p h n d", n=n)

                wait_reuse(dve, after("q_turned"), b, 2)
                yield link.count(nc.vector.tensor_copy(groups(0, 3), src.unsqueeze(2).broadcast_to([128, heads, 3, dh])))
                yield link.count(nc.vector.tensor_tensor(left, src, pad[:, :, 0:dh], ALU.subtract))
                yield link.count(nc.vector.tensor_copy(groups(3, 2), left.unsqueeze(2).broadcast_to([128, heads, 2, dh])))
                nc.vector.tensor_tensor(pad[:, :, 5 * dh:6 * dh], left, pad[:, :, 3 * dh:4 * dh],
                                        ALU.subtract).then_inc(sem("q_padded"), 1)
                link.end()

            def take_qT(b, k):
                dve.wait_ge(*after("q_turned", b + 1))
                wait_reuse(dve, after("scores"), b, RING, NU)
                nc.vector.tensor_copy(qT[:, k, :, :], bank_b[0].rearrange("p (j q) -> p j q", j=8)).then_inc(sem("qT_ready"), 1)

            def take_max(b, k, u):
                dve.wait_ge(*after("raw_scores", b * NU + (u + 1)))
                nc.vector.tensor_reduce(neg_max[:, k, 8 * u:8 * u + 8],
                                        ps[:, 2 + 2 * u:4 + 2 * u, :].rearrange("p a (h k) -> p (a h) k", h=4),
                                        AX.X, ALU.max, negate=True).then_inc(sem("max_taken"), 1)

            def split_max(b, k):
                link = Link(dve, after("nm_link"), b, 3)
                nm = neg_max[:, k, 0:heads]
                copies = 128 // R
                spots = nm3[:, k, :].rearrange("p (r n) -> p r n", r=2)[:, 0:copies, 0:3 * heads].rearrange(
                    "p r (h c) -> p r h c", c=3)
                full = [128, copies, heads]
                left = nm_rest[:, 0:heads]

                def wide(v):
                    return v.unsqueeze(1).broadcast_to(full)
                dve.wait_ge(*after("max_taken", b * NU + NU))
                wait_reuse(dve, after("nm_turned"), b, RING)
                yield link.count(nc.vector.tensor_copy(spots[:, :, :, 0], wide(nm)))
                yield link.count(nc.vector.tensor_tensor(left, nm, spots[:, 0, :, 0], ALU.subtract))
                yield link.count(nc.vector.tensor_copy(spots[:, :, :, 1], wide(left)))
                nc.vector.tensor_tensor(spots[:, :, :, 2], wide(left), spots[:, :, :, 1],
                                        ALU.subtract).then_inc(sem("nm_split"), 1)
                link.end()

            def take_nmT(b, k):
                dve.wait_ge(*after("nm_turned", b + 1))
                wait_reuse(dve, after("scores"), b, RING, NU)
                nc.vector.tensor_copy(nmT[:, k, :], bank_b[6][:, 0:128]).then_inc(sem("nmT_ready"), 1)

            def take_o(b, k):
                link = Link(dve, after("o_link"), b, 1 if post else 2)
                got = ps[:, 6, 64:64 + heads * (dh + 1)].rearrange("p (h d) -> p h d", h=heads)
                o = o_sb[:, k % 2, :].rearrange("p (h d) -> p h d", h=heads)
                dve.wait_ge(*after("pv_turned", b + 1))
                yield link.count(nc.vector.reciprocal(inv_den[:, k % 2, 0:heads], got[:, :, dh]))
                inv = inv_den[:, k % 2, 0:heads].unsqueeze(2).broadcast_to([128, heads, dh])
                if post:
                    wait_reuse(dve, after("o_turned"), b, 2)
                    nc.vector.tensor_tensor(o, got[:, :, 0:dh], inv, ALU.mult).then_inc(sem("o_ready"), 1)
                else:
                    yield link.count(nc.vector.tensor_tensor(o, got[:, :, 0:dh], inv, ALU.mult))
                    nc.vector.tensor_tensor(x_all[:, b, :], x_all[:, b, :], o_sb[:, k % 2, :],
                                            ALU.add).then_inc(sem("o_ready"), 1)
                link.end()

            def take_oT(b, k):
                dve.wait_ge(*after("o_turned", b + 1))
                dve.wait_ge(*after("nm_turned", b + 4 if not isinstance(b, int) else min(b + 4, count)))
                nc.vector.tensor_copy(oT[:, k % 2, :], ps[:, 6, 256:384]).then_inc(sem("oT_ready"), 1)

            def add_post(b, k):
                dve.wait_ge(*after("projected", b + 1))
                for name, ahead in (("o_turned", 2), ("nm_turned", 5)):
                    dve.wait_ge(*after(name, b + ahead if not isinstance(b, int) else min(b + ahead, count)))
                stream = {"L1": x1_tiles, "L3": x_all, "L4": z_all}[L]
                dst = stream[:, b, :]
                nc.vector.tensor_tensor(dst, dst, ps[:, 6, 384:512], ALU.add).then_inc(sem("x_updated"), 1)
                if count == B:
                    measure(dve, after("x_updated"), b, stream)
                else:
                    dve.wait_ge(*after("x_updated", b + 1))
                    nc.vector.bn_stats(stat[:, b, :], x1_tiles[:, b, :]).then_inc(sem("tile_measured"), 1)

            def update(b, k):
                measure(dve, after("o_ready"), b)

            def step(items):
                def have(lag):
                    return lag in items
                if have(3):
                    take_nmT(*items[3])
                if post and have(6):
                    take_oT(*items[6])
                if post and have(7):
                    add_post(*items[7])
                if have(2):
                    take_max(*items[2], 0)
                if have(0):
                    in_turns(split_q(*items[0]))
                if have(2) and NU == 2:
                    take_max(*items[2], 1)
                in_turns(*([split_max(*items[2])] if have(2) else []), *([take_o(*items[5])] if have(5) else []))
                if have(1):
                    take_qT(*items[1])
                if not post and have(5):
                    update(*items[5])
            whole_steps(dve, count, 7 if post else 5, step)

        def attention_gpsimd(pool, L, count, heads, raw):
            dh, R, NU = rows_of(heads)

            def split_k(b, k):
                link = Link(pool, after("k_link"), b, 5, sem("held_gpsimd"))
                if raw:
                    pool.wait_ge(*after("k_scaled", b + 1))
                    src = key32[:, k % 2, :]
                else:
                    src = kv_all[:, b, 0:D]
                src = src.rearrange("p (h d) -> p h d", h=heads)
                pad = k_pad[:, k % 2, :].rearrange("p (h r) -> p h r", h=heads)
                left = k_rest[:, k % 2, :].rearrange("p (h d) -> p h d", h=heads)
                wait_reuse(pool, after("k_turned"), b, 2)
                hold(pool)
                link(nc.gpsimd.tensor_copy(pad[:, :, 0:dh], src))
                link(nc.gpsimd.tensor_tensor(left, src, pad[:, :, 0:dh], ALU.subtract))
                link(nc.gpsimd.tensor_copy(pad[:, :, dh:2 * dh], left))
                link(nc.gpsimd.tensor_tensor(pad[:, :, 2 * dh:3 * dh], left, pad[:, :, dh:2 * dh], ALU.subtract))
                if L in ("L0", "L2", "L3"):
                    which = ("L0", "L2", "L3").index(L)
                    nc.gpsimd.tensor_copy(pad[:, :, 6 * dh:6 * dh + 3],
                                          bias3[:, which, b, :].unsqueeze(1).broadcast_to([128, heads, 3]))
                link(nc.gpsimd.tensor_copy(pad[:, :, 3 * dh:5 * dh], pad[:, :, 0:2 * dh]))
                nc.gpsimd.tensor_copy(pad[:, :, 5 * dh:6 * dh], pad[:, :, 0:dh]).then_inc(sem("k_padded"), 1)
                link.end()

            def copy_v(b, k):
                src = ctx_all[:, b, D:C] if raw else kv_all[:, b, D:C]
                wait_reuse(pool, after("weighted"), b, 2)
                hold(pool)
                each, G = dh + 1, heads // 2
                dst = v_wide[:, k % 2, :, 0:G * (G + 1) * each].rearrange("p g (h n) -> p g h n", h=G)[:, :, :, 0:dh]
                nc.gpsimd.tensor_copy(dst, src.rearrange("p (g h d) -> p g h d", g=2, h=G)).then_inc(sem("v_ready"), 1)

            steps(pool, count, [(0, split_k), (3, copy_v)])

        def attention_scalar(act, L, count, heads, raw, post):
            dh, R, NU = rows_of(heads)

            def scale_k(b, k):
                wait_reuse(act, after("k_padded"), b, 2)
                nc.scalar.activation(key32[:, k % 2, :], ctx_all[:, b, 0:D], ACT.Copy,
                                     scale=k_scale[:, 0 if L == "L0" else 1, bass.ts(b, 1)]).then_inc(sem("k_scaled"), 1)

            def take_kT(b, k):
                act.wait_ge(*after("k_turned", b + 1))
                wait_reuse(act, after("scores"), b, RING, NU)
                nc.scalar.activation(kT[:, k, :, :], bank_b[1].rearrange("p (j q) -> p j q", j=8),
                                     ACT.Copy).then_inc(sem("kT_ready"), 1)

            def exps(b, k, u):
                slot = u if NU == 2 else 1
                act.wait_ge(*after("scores", b * NU + (u + 1)))
                wait_reuse(act, after("weighted"), b, 2)
                nc.scalar.activation(probs[:, k % 2, 1024 * u:1024 * u + 1024],
                                     ps[:, 2 + 2 * slot:4 + 2 * slot, :].rearrange("p a n -> p (a n)"),
                                     ACT.Exp).then_inc(sem("probs_ready"), 1)

            def take_pv(b, k):
                act.wait_ge(*after("weighted", b + 1))
                wait_reuse(act, after("pv_turned"), b, 2)
                W = heads // 2 * (dh + 1)
                nc.scalar.activation(pv[0:W, k % 2, :], ps[0:W, 7, 0:256], ACT.Copy).then_inc(sem("pv_ready"), 1)

            work = [(0, scale_k)] if raw else []
            work += [(4, take_pv), (3, lambda b, k: exps(b, k, 0)), (1, take_kT)]
            if NU == 2:
                work += [(3, lambda b, k: exps(b, k, 1))]
            steps(act, count, work)

        def attention_tensor(pe, L, count, heads, mask_parts, mask, post_w):
            dh, R, NU = rows_of(heads)
            per = 128 // R

            def turn(b, k):
                pe.wait_ge(*after("q_padded", b + 1))
                wait_reuse(pe, after("qT_ready"), b, 1)
                for j in range(8):
                    last = nc.tensor.transpose(bank_b[0][:, 128 * j:128 * j + 128],
                                               q_pad[:, k % 2, 128 * j:128 * j + 128], identb[:])
                last.then_inc(sem("q_turned"), 1)
                pe.wait_ge(*after("k_padded", b + 1))
                wait_reuse(pe, after("kT_ready"), b, 1)
                for j in range(8):
                    last = nc.tensor.transpose(bank_b[1][:, 128 * j:128 * j + 128],
                                               k_pad[:, k % 2, 128 * j:128 * j + 128], identb[:])
                last.then_inc(sem("k_turned"), 1)

            def tile_of(buf, k, h, n):
                base = R * (h % per)
                return buf[base:base + n, k, h // per, :]

            def product(u, slot, k, left, right, turned):
                n = 6 * dh + 3
                for a in range(2):
                    bank = ps[:, 2 + 2 * slot + a, :]
                    for part in range(mask_parts):
                        m = mask(u, k, part)
                        four = [128, 4, 128]
                        if turned:
                            nc.tensor.matmul(bank, m, identb[:].unsqueeze(1).broadcast_to(four),
                                             start=part == 0, stop=False, skip_group_check=True)
                        else:
                            nc.tensor.matmul(bank, identb[:], m.unsqueeze(1).broadcast_to(four),
                                             start=part == 0, stop=False, skip_group_check=True)
                    for i in range(4):
                        h = head_at(8 * u + 4 * a + i, R)
                        base = R * (h % per)
                        dst = bank[:, 128 * i:128 * i + 128]
                        last = nc.tensor.matmul(dst, tile_of(left, k, h, n), tile_of(right, k, h, n),
                                                start=mask_parts == 0, stop=not turned, skip_group_check=True)
                        if turned:
                            last = nc.tensor.matmul(dst, sel[base:base + R, 8 * u + 4 * a + i, :], nmT[base:base + R, k, :],
                                                    start=False, stop=True, skip_group_check=True)
                return last

            def raw_scores(b, k, u):
                slot = u if NU == 2 else 0
                if u == 0:
                    pe.wait_ge(*after("qT_ready", b + 1))
                    pe.wait_ge(*after("kT_ready", b + 1))
                if NU == 2:
                    if not isinstance(b, int) or b >= 2:
                        pe.wait_ge(*after("probs_ready", b * NU + (u + 1 - 2 * NU)))
                    elif b == 1:
                        pe.wait_ge(*after("max_taken", u + 1))
                else:
                    wait_reuse(pe, after("max_taken"), b, 1)
                product(u, slot, k, qT, kT, False).then_inc(sem("raw_scores"), 1)

            def scores(b, k, u):
                slot = u if NU == 2 else 1
                if u == 0:
                    pe.wait_ge(*after("nmT_ready", b + 1))
                if NU == 2:
                    if isinstance(b, int) and b == count - 1:
                        pe.wait_ge(*after("max_taken", b * NU + (u + 1)))
                    else:
                        pe.wait_ge(*after("max_taken", b * NU + (NU + u + 1)))
                else:
                    wait_reuse(pe, after("probs_ready"), b, 1)
                product(u, slot, k, kT, qT, True).then_inc(sem("scores"), 1)

            def bank_free(b, lag, reads):
                for name, its in reads:
                    n = b + (lag - its)
                    if isinstance(n, int):
                        n = min(n, count)
                        if n <= 0:
                            continue
                    pe.wait_ge(*after(name, n))

            reads = [("nmT_ready", 3), ("o_ready", 5)]
            if post_w is not None:
                reads += [("oT_ready", 6), ("x_updated", 7)]

            def turn_max(b, k):
                pe.wait_ge(*after("nm_split", b + 1))
                bank_free(b, 3, reads)
                hold(pe)
                nc.tensor.transpose(bank_b[6][:, 0:128], nm3[:, k, :],
                                    identb[:]).then_inc(sem("nm_turned"), 1)

            def turn_o(b, k):
                bank_free(b, 6, reads)
                hold(pe)
                nc.tensor.transpose(ps[:, 6, 256:384], o_sb[:, k % 2, :], ident[:]).then_inc(sem("o_turned"), 1)

            def project(b, k):
                bank_free(b, 7, reads)
                nc.tensor.matmul(ps[:, 6, 384:512], oT[:, k % 2, :], post_w, start=True,
                                 stop=True).then_inc(sem("projected"), 1)

            G, W = heads // 2, heads // 2 * (dh + 1)

            def weighted(b, k, half):
                if half == 0:
                    pe.wait_ge(*after("v_ready", b + 1))
                    wait_reuse(pe, after("pv_ready"), b, 1)
                if NU == 2 or half == 0:
                    pe.wait_ge(*after("probs_ready", b * NU + (half + 1)))
                where = {head_at(at, R): at for at in range(heads)}
                for j in range(G):
                    at = where[half * G + j]
                    last = nc.tensor.matmul(ps[0:W, 7, 128 * half:128 * half + 128],
                                            v_wide[:, k % 2, half, W * j:W * j + W],
                                            probs[:, k % 2, 128 * at:128 * at + 128], start=j == 0, stop=j == G - 1)
                if half:
                    last.then_inc(sem("weighted"), 1)

            def turn_pv(b, k):
                pe.wait_ge(*after("pv_ready", b + 1))
                bank_free(b, 6, reads[:1] + reads[2:])
                wait_reuse(pe, after("o_ready"), b, 1)
                hold(pe)
                for half in range(2):
                    last = nc.tensor.transpose(ps[:, 6, 64 + W * half:64 + W * half + W],
                                               pv[0:W, k % 2, 128 * half:128 * half + 128], ident[0:W, 0:W])
                last.then_inc(sem("pv_turned"), 1)

            work = [(7, project), (6, turn_o)] if post_w is not None else []
            work += [(3, turn_max), (2, lambda b, k: raw_scores(b, k, 0)), (5, turn_pv),
                     (4, lambda b, k: weighted(b, k, 0))]
            if NU == 2:
                work += [(2, lambda b, k: raw_scores(b, k, 1))]
            work += [(4, lambda b, k: weighted(b, k, 1))]
            if NU == 2:
                work += [(3, lambda b, k: scores(b, k, 0)), (1, turn), (3, lambda b, k: scores(b, k, 1))]
            else:
                work += [(1, turn), (3, lambda b, k: scores(b, k, 0))]
            steps(pe, count, work)

        wc = sb("wc", [128, 128])
        wg = sb("wg", [128, 128])
        toep = sb("toep", [128, 128])
        lens_f = sb("lens_f", [128, B])
        q_room = qT[:].rearrange("p k j t -> p (k j t)").bitcast(F32)
        lens_rep, hot, spread, patch = (q_room[:, 256 * i:256 * i + 256].rearrange("p (k t) -> p k t", k=2)
                                        for i in range(4))
        bound = sb("bound", [128, 2, 2])
        bound_rep = sb("bound_rep", [128, 2, 128], BF16)
        g_init = sb("g_init", [128, D])
        bias_rows = sb("bias_rows", [3, 1152], BF16)
        cols = sb("cols", [128, 16])
        COL = {n: i for i, n in enumerate(("g_res", "router_w", "ln1", "ln2", "norm1", "norm2", "ln_g", "ln_b",
                                           "router_b", "L0_b", "L2_b"))}

        def col(name, n=128):
            return cols[0:n, COL[name]:COL[name] + 1]

        ctx_inv = sb("ctx_inv", [128, B])
        rowT = sb("rowT", [128, 2, 128])
        junk = sb("junk", [128, 256])
        wb = sb("wb", [128, 2, 128])
        rank = sb("rank", [128, 2, 4])
        picked = sb("picked", [128, B])
        keep = sb("keep", [128, B])
        wcol = sb("wcol", [128, B])
        place = sb("place", [128, B])
        pick = sb("pick", [128, B, SLOTS])
        rw_rep = sb("rw_rep", [128, 128])
        x1_tiles = sb("x1_tiles", [128, TILES, 128])
        x1_T = probs[:, 1, 1024:1536].rearrange("p (t s) -> p t s", t=TILES)
        aux = q_room[:, 512:512 + 9 * B].rearrange("p (b n) -> p b n", b=B)
        auxT = q_room[0:9, 0:512].rearrange("p (t s) -> p t s", t=TILES)
        aux_t = sb("aux_t", [128, TILES, 9])
        cls_mask = sb("cls_mask", [128, 4, 128])
        mg = probs[:, 1, 1536:2048].rearrange("p (t s) -> p t s", t=TILES)
        mask3 = kv_all[:, 8:11, :].rearrange("p a b -> p (a b)").bitcast(BF16).rearrange("p (t c k) -> p t c k", t=TILES, c=3)
        outside = sb("outside", [128, 128])
        own = sb("own", [128, PER_TILE])
        freq = sb("freq", [128, 4])
        pos_f = sb("pos_f", [128, 4])
        w_qkv = sb("w_qkv", [128, 384])
        w_o1 = sb("w_o1", [128, 128])
        w1_l1 = sb("w1_l1", [128, 512])
        w2_l1 = sb("w2_l1", [128, 4, 128])
        tap_w = sb("tap_w", [128, 3, 512])
        w2_q = sb("w2_q", [128, 4, 128], BF16)
        inv_w = sb("inv_w", [128, 4])
        xqT = sb("xqT", [128, 2, 130])
        q2 = q_pad[:, :, 0:512]
        q2T = k_pad[:, :, 0:512].rearrange("p k (c t) -> p k c t", c=4)
        w_src = sb("w_src", [128, 2, 256])
        w_tgt = sb("w_tgt", [128, 256])
        w_out2 = sb("w_out2", [128, 128])
        mask_f = sb("mask_f", [128, B])
        mask_q = sb("mask_q", [128, B])
        causal = sb("causal", [128, 128], BF16)
        rope = sb("rope", [128, 4, 128])
        w_h1 = sb("w_h1", [128, 320])
        w_h2 = sb("w_h2", [64, 384])
        w_o3 = sb("w_o3", [128, 128])
        gate_w = sb("gate_w", [128, N_EXP3])
        gate_b = sb("gate_b", [128, N_EXP3])
        first_row = sb("first_row", [128, N_EXP3])
        b1_col = sb("b1_col", [128, 16])
        b2_col = sb("b2_col", [128, N_EXP3])

        rowT2 = sb("rowT2", [128, 128])
        scale2 = sb("scale2", [128, RING])
        w_part = q_pad[:].rearrange("p k r -> p (k r)")[:, 0:1152]

        z_all = ctx_all[:, 16:32, :].rearrange("p a b -> p (a b)").rearrange("p (b d) -> p b d", b=B)
        inv_ln = ctx_inv

        phase_no = {}

        def phase_end(engine):
            n = phase_no.get(engine, 0) + 1
            phase_no[engine] = n
            engine.drain().then_inc(sem("phase_done"), 1)
            engine.wait_ge(sem("phase_done"), 5 * n)

        def turn_rows(pe):
            def stage(b, k):
                pe.wait_ge(*after("normed", b + 1))
                wait_reuse(pe, after("rowT"), b, 2)
                hold(pe)
                nc.tensor.transpose(ps[:, k % 2, 0:128], row32[:, k % 2, :], ident[:]).then_inc(sem("turned"), 1)
            return stage

        def take_rows(act, scale=1.0, dst=None):
            def stage(b, k):
                act.wait_ge(*after("turned", b + 1))
                wait_reuse(act, after("used"), b, 2)
                to = rowT[:, k % 2, :] if dst is None else dst(k)
                nc.scalar.activation(to, ps[:, k % 2, 0:128], ACT.Copy, scale=scale).then_inc(sem("rowT"), 1)
            return stage

        def ffn0_prep_tensor(pe):
            pe.wait_ge(sem("l0_weights"), 32)
            for c in range(32):
                last = nc.tensor.matmul(ps[:, 7, 256:384], kv_all[:, c, 0:128], kv_all[:, c, 128:256],
                                        start=c == 0, stop=c == 31)
            last.then_inc(sem("wc_ready"), 1)

        def ffn0_prep_vector(dve):
            dve.wait_ge(sem("wc_ready"), 1)
            nc.vector.tensor_copy(wc[:], ps[:, 7, 256:384]).then_inc(sem("wc_taken"), 1)
            dve.wait_ge(sem("wc_taken"), 1)

        def ffn0_vector(dve):
            def norm_b(b, k):
                wait_reuse(dve, after("turned"), b, 2)
                norm(row32[:, k % 2, :], b).then_inc(sem("normed"), 1)

            def add(b, k):
                dve.wait_ge(*after("used", b + 1))
                nc.vector.tensor_tensor(x_all[:, b, :], x_all[:, b, :], ps[:, 2 + k % 2, 0:128],
                                        ALU.add).then_inc(sem("added"), 1)
                measure(dve, after("added"), b)
            steps(dve, B, [(0, norm_b), (3, add)])

        def ffn0_scalar(act):
            steps(act, B, [(1, take_rows(act))])

        def ffn0_tensor(pe):
            def multiply(b, k):
                pe.wait_ge(*after("rowT", b + 1))
                wait_reuse(pe, after("added"), b, 2)
                nc.tensor.matmul(ps[:, 2 + k % 2, 0:128], rowT[:, k % 2, :], wc[:], start=True,
                                 stop=True).then_inc(sem("used"), 1)
            steps(pe, B, [(1, turn_rows(pe)), (2, multiply)])

        def depool_vector(dve):
            def norm_b(b, k):
                wait_reuse(dve, after("turned"), b, 2)
                norm(row32[:, k % 2, :], b).then_inc(sem("normed"), 1)
                wait_reuse(dve, after("used"), b, 2)
                nc.vector.scalar_tensor_tensor(patch[:, k % 2, :], ctx_all[:, b, 0:D], ctx_inv[:, bass.ts(b, 1)],
                                               g_init[:], ALU.mult, ALU.mult).then_inc(sem("dp_patch"), 1)

            def find(b, k):
                dve.wait_ge(sem("dp_ends"), b + 1)
                link = Link(dve, after("link2"), b, 2)
                nc.vector.tensor_scalar(junk[:, 0:128], ps[:, 4, 0:128], iota_p[:, 1:2], 0.0, ALU.is_equal, ALU.max,
                                        accum_out=bound[:, k % 2, 0:1]).then_inc(sem("dp_bound_a"), 1)
                link(nc.vector.tensor_scalar(junk[:, 128:256], ps[:, 4, 0:128], iota_p[:, 2:3], 0.0, ALU.is_equal,
                                             ALU.max, accum_out=bound[:, k % 2, 1:2]))
                dve.wait_ge(sem("dp_bound_a"), b + 1)
                link(nc.vector.tensor_tensor(bound[:, k % 2, 0:1], bound[:, k % 2, 0:1], bound[:, k % 2, 1:2], ALU.max))
                wait_reuse(dve, after("dp_counts"), b, 2)
                nc.vector.tensor_scalar(bound_rep[:, k % 2, :], ones[:], bound[:, k % 2, 0:1], None,
                                        ALU.mult).then_inc(sem("dp_bound"), 1)
                link.end()

            def choose(b, k):
                dve.wait_ge(sem("dp_counts"), b + 1)
                wait_reuse(dve, after("dp_matrix"), b, 2)
                link = Link(dve, after("link3"), b, 1)
                link(nc.vector.tensor_scalar(hot[:, k % 2, :], ps[:, 5, 0:128], 1.0, 0.0, ALU.subtract, ALU.max))
                nc.vector.tensor_scalar(hot[:, k % 2, :], hot[:, k % 2, :], float(S - 1), iota_p[:, 0:1],
                                        ALU.min, ALU.is_equal).then_inc(sem("dp_hot"), 1)
                link.end()

            def add(b, k):
                dve.wait_ge(*after("used", b + 1))
                nc.vector.tensor_tensor(x_all[:, b, :], x_all[:, b, :], ps[:, 2 + k % 2, 0:128],
                                        ALU.add).then_inc(sem("added"), 1)
                measure(dve, after("added"), b)

            steps(dve, B, [(0, find), (1, choose), (1, norm_b), (4, add)])

        def depool_scalar(act):
            def spread_lens(b, k):
                wait_reuse(act, after("dp_ends"), b, 2)
                nc.scalar.activation(lens_rep[:, k % 2, :], ones[:], ACT.Copy,
                                     scale=lens_f[:, bass.ts(b, 1)]).then_inc(sem("dp_lens"), 1)

            def take_matrix(b, k):
                act.wait_ge(sem("dp_matrix"), b + 1)
                wait_reuse(act, after("used"), b, 2)
                nc.scalar.activation(spread[:, k % 2, :], ps[:, 6, 0:128], ACT.Copy).then_inc(sem("dp_spread"), 1)

            steps(act, B, [(0, spread_lens), (2, take_rows(act)), (2, take_matrix)])

        def depool_tensor(pe):
            def ends(b, k):
                pe.wait_ge(sem("dp_lens"), b + 1)
                wait_reuse(pe, after("dp_bound"), b, 1)
                nc.tensor.matmul(ps[:, 4, 0:128], lens_rep[:, k % 2, :], upper[:], start=True,
                                 stop=True).then_inc(sem("dp_ends"), 1)

            def counts(b, k):
                pe.wait_ge(sem("dp_bound"), b + 1)
                wait_reuse(pe, after("dp_hot"), b, 1)
                nc.tensor.matmul(ps[:, 5, 0:128], bound_rep[:, k % 2, :], upperb[:], start=True,
                                 stop=True).then_inc(sem("dp_counts"), 1)

            def matrix(b, k):
                pe.wait_ge(sem("dp_hot"), b + 1)
                wait_reuse(pe, after("dp_spread"), b, 1)
                nc.tensor.matmul(ps[:, 6, 0:128], toep[:], hot[:, k % 2, :], start=True,
                                 stop=True).then_inc(sem("dp_matrix"), 1)

            def total(b, k):
                pe.wait_ge(*after("rowT", b + 1))
                pe.wait_ge(sem("dp_spread"), b + 1)
                pe.wait_ge(sem("dp_patch"), b + 1)
                wait_reuse(pe, after("added"), b, 2)
                dst = ps[:, 2 + k % 2, 0:128]
                nc.tensor.matmul(dst, rowT[:, k % 2, :], wg[:], start=True, stop=False)
                nc.tensor.matmul(dst, onesb[0:3, :], bias_rows[:, 0:128], start=False, stop=False)
                nc.tensor.matmul(dst, spread[:, k % 2, :], patch[:, k % 2, :], start=False,
                                 stop=True).then_inc(sem("used"), 1)

            steps(pe, B, [(0, ends), (1, counts), (2, matrix), (2, turn_rows(pe)), (3, total)])

        xd_all = q_all

        def route_vector(dve):
            def norm_b(b, k):
                wait_reuse(dve, after("turned"), b, 2)
                norm(row32[:, k % 2, :], b).then_inc(sem("normed"), 1)
                dve.wait_ge(*after("normed", b + 1))
                nc.vector.tensor_copy(xd_all[:, b, :], row32[:, k % 2, :]).then_inc(sem("rt_kept"), 1)

            def rank_tokens(b, k):
                dve.wait_ge(sem("rt_wb"), b + 1)
                link = Link(dve, after("link2"), b, 7)
                w, r = wb[:, k % 2, :], rank[:, k % 2, :]
                link(nc.vector.tensor_tensor(junk[:, 0:128], w, ident[:], ALU.mult))
                link(nc.vector.tensor_reduce(r[:, 0:1], junk[:, 0:128], AX.X, ALU.add))
                link(nc.vector.scalar_tensor_tensor(junk[:, 0:128], w, r[:, 0:1], below[:], ALU.is_ge, ALU.mult,
                                                    accum_out=r[:, 1:2]))
                link(nc.vector.scalar_tensor_tensor(junk[:, 128:256], w, r[:, 0:1], above[:], ALU.is_gt, ALU.mult,
                                                    accum_out=r[:, 2:3]))
                link(nc.vector.tensor_scalar(junk[:, 0:128], w, r[:, 0:1], 0.0, ALU.is_ge, ALU.add,
                                             accum_out=r[:, 3:4]))
                link(nc.vector.tensor_scalar(picked[:, bass.ts(b, 1)], r[:, 1:2], r[:, 2:3], KEPT - 0.5, ALU.add, ALU.is_lt))
                link(nc.vector.tensor_scalar(keep[:, bass.ts(b, 1)], r[:, 3:4], KEPT + 0.5, None, ALU.is_gt))
                nc.vector.tensor_copy(wcol[:, bass.ts(b, 1)], r[:, 0:1]).then_inc(sem("rt_wcol"), 1)
                dve.wait_ge(sem("rt_kept"), b + 1)
                nc.vector.scalar_tensor_tensor(x_all[:, b, :], xd_all[:, b, :], keep[:, bass.ts(b, 1)], x_all[:, b, :],
                                               ALU.mult, ALU.add).then_inc(sem("rt_done"), 1)
                link.end()

            steps(dve, B, [(0, norm_b), (3, rank_tokens)])

        def route_scalar(act):
            def take_w(b, k):
                act.wait_ge(*after("used", b + 1))
                wait_reuse(act, after("rt_done"), b, 2)
                nc.scalar.activation(wb[:, k % 2, :], ps[:, 2 + k % 2, 0:128], ACT.Identity,
                                     bias=col("router_b")).then_inc(sem("rt_wb"), 1)
            steps(act, B, [(1, take_rows(act)), (2, take_w)])

        def route_tensor(pe):
            def weigh(b, k):
                pe.wait_ge(*after("rowT", b + 1))
                wait_reuse(pe, after("rt_wb"), b, 2)
                nc.tensor.matmul(ps[:, 2 + k % 2, 0:128], rw_rep[:], rowT[:, k % 2, :], start=True,
                                 stop=True).then_inc(sem("used"), 1)
            steps(pe, B, [(1, turn_rows(pe)), (2, weigh)])

        qD, kvD = q_all, kv_all

        def gather_tensor(pe):
            pe.wait_ge(sem("ga_picked"), 1)
            nc.tensor.matmul(ps[:, 7, 0:B], above[:], picked[:], start=True, stop=True).then_inc(sem("ga_place"), 1)
            pe.wait_ge(sem("ga_pick"), 1)
            for T in range(TILES):
                for j in range(PER_TILE):
                    b = T * PER_TILE + j
                    spot = slice(128 * T + SLOTS * j, 128 * T + SLOTS * (j + 1))
                    nc.tensor.matmul(ps[:, 0, spot], xd_all[:, b, :], pick[:, b, :], start=True, stop=True)
                    nc.tensor.matmul(ps[0:9, 1, spot], aux[:, b, :], pick[:, b, :], start=True, stop=True)
                    last = nc.tensor.matmul(ps[:, 2, spot], cls_mask[:, min(b, 3), :], pick[:, b, :],
                                            start=True, stop=True)
            last.then_inc(sem("ga_gathered"), 1)
            pe.wait_ge(sem("ga_taken"), 3)
            for T in range(TILES):
                nc.tensor.matmul(ps[:, 3, 128 * T:128 * T + 128], mg[:, T, :],
                                 pick[:, T * PER_TILE:(T + 1) * PER_TILE, :], start=True, stop=True)
                nc.tensor.transpose(ps[:, 4, 128 * T:128 * T + 128], x1_T[:, T, :], ident[:])
                last = nc.tensor.transpose(ps[:, 5, 16 * T:16 * T + 9], auxT[:, T, :], ident[0:9, 0:9])
            last.then_inc(sem("ga_rows"), 1)
            for T in range(TILES):
                pe.wait_ge(sem("ga_normed"), T + 1)
                nc.tensor.transpose(ps[:, 6, 0:128], row32[:, T % 2, :], ident[:]).then_inc(sem("ga_turned"), 1)
                pe.wait_ge(sem("ga_rowT"), T + 1)
                if T:
                    pe.wait_ge(sem("ga_roped"), T)
                nc.tensor.matmul(ps[:, 7, 0:384], rowT[:, T % 2, :], w_qkv[:], start=True,
                                 stop=True).then_inc(sem("ga_projected"), 1)

        def gather_scalar(act):
            moments_scalar(act, TILES)
            for T in range(TILES):
                act.wait_ge(sem("ga_turned"), T + 1)
                nc.scalar.activation(rowT[:, T % 2, :], ps[:, 6, 0:128], ACT.Copy,
                                     scale=col("ln1")).then_inc(sem("ga_rowT"), 1)

        def gather_vector(dve):
            q = Seq(dve, sem("ga_seq"), moments_taken)
            dve.sem_inc(sem("ga_picked"), 1)
            dve.wait_ge(sem("ga_place"), 1)
            q(nc.vector.tensor_copy(place[:], ps[:, 7, 0:B]))
            full = [128, B, SLOTS]
            q(nc.vector.tensor_tensor(pick[:], iota_row[:].unsqueeze(1).broadcast_to(full),
                                      place[:].unsqueeze(2).broadcast_to(full), ALU.is_equal))
            q(nc.vector.tensor_tensor(pick[:], pick[:], picked[:].unsqueeze(2).broadcast_to(full), ALU.mult))
            ang = small[:, 0:32].rearrange("p (s c f) -> p s c f", s=2, c=4)
            turns = small[:, 32:64].rearrange("p (s c f) -> p s c f", s=2, c=4)
            for c in range(4):
                q(nc.vector.tensor_scalar(ang[:, 0, c, :], freq[:], pos_f[:, c:c + 1], None, ALU.mult))
            q(nc.vector.tensor_scalar(turns[:, 0], ang[:, 0], 1.0 / TWO_PI, MAGIC, ALU.mult, ALU.add))
            q(nc.vector.tensor_scalar(turns[:, 0], turns[:, 0], MAGIC, None, ALU.subtract))
            q(nc.vector.tensor_scalar(turns[:, 1], ang[:, 0], 1.0 / TWO_PI, 0.25, ALU.mult, ALU.add))
            q(nc.vector.tensor_scalar(turns[:, 1], turns[:, 1], MAGIC, MAGIC, ALU.add, ALU.subtract))
            q(nc.vector.tensor_copy(ang[:, 1], ang[:, 0]))
            fa = small[:, 0:32]
            ft = small[:, 32:64]
            for part in PI_PARTS:
                q(nc.vector.scalar_tensor_tensor(fa, ft, -part, fa, ALU.mult, ALU.add))
            q(nc.vector.tensor_scalar(ang[:, 1], ang[:, 1], TWO_PI / 4, None, ALU.add))
            q(nc.vector.tensor_scalar(fa, fa, SIN_LIMIT, -SIN_LIMIT, ALU.min, ALU.max))
            dve.sem_inc(sem("ga_angles"), 1)
            dve.wait_ge(sem("ga_sines"), 1)
            sin = small[:, 64:96].rearrange("p (s c f) -> p s c f", s=2, c=4)
            for s, at in ((1, 0), (0, 4)):
                q(nc.vector.tensor_copy(aux[:, 0:3, at:at + 4], sin[:, s, 0:3, :]))
                q(nc.vector.tensor_copy(aux[:, 3:B, at:at + 4],
                                        sin[:, s, 3:4, :].broadcast_to([128, B - 3, 4])))
            q(nc.vector.tensor_copy(aux[:, :, 8], wcol[:]))
            dve.sem_inc(sem("ga_pick"), 1)
            dve.wait_ge(sem("ga_gathered"), 1)
            flat = "p t s -> p (t s)"
            nc.vector.tensor_copy(probs[:, 1, 1024:1536], ps[:, 0, :]).then_inc(sem("ga_taken"), 1)
            nc.vector.tensor_copy(q_room[0:9, 0:512], ps[0:9, 1, :]).then_inc(sem("ga_taken"), 1)
            nc.vector.tensor_copy(probs[:, 1, 1536:2048], ps[:, 2, :]).then_inc(sem("ga_taken"), 1)
            dve.wait_ge(sem("ga_rows"), 1)
            q(nc.vector.tensor_copy(x1_tiles[:].rearrange(flat), ps[:, 4, :]))
            q(nc.vector.tensor_copy(aux_t[:], ps[:, 5, 0:64].rearrange("p (t s) -> p t s", t=TILES)[:, :, 0:9]))
            m = probs[:, 0, 0:512].rearrange("p (t s) -> p t s", t=TILES)
            q(nc.vector.tensor_tensor(m, ps[:, 3, :].rearrange("p (t s) -> p t s", t=TILES),
                                      outside[:].unsqueeze(1).broadcast_to([128, TILES, 128]), ALU.add))
            q(nc.vector.tensor_copy(mask3[:, :, 0, :], m))
            q(nc.vector.tensor_tensor(m, m, mask3[:, :, 0, :], ALU.subtract))
            q(nc.vector.tensor_copy(mask3[:, :, 1, :], m))
            q(nc.vector.tensor_tensor(mask3[:, :, 2, :], m, mask3[:, :, 1, :], ALU.subtract))
            for T in range(TILES):
                q(nc.vector.bn_stats(stat[:, T, :], x1_tiles[:, T, :]))
            moments_vector(dve, "rms", stat[:], TILES)
            for T in range(TILES):
                if T >= 2:
                    dve.wait_ge(sem("ga_turned"), T - 1)
                nc.vector.tensor_scalar(row32[:, T % 2, :], x1_tiles[:, T, :], inv_all[:, T:T + 1], None,
                                        ALU.mult).then_inc(sem("ga_normed"), 1)
                dve.wait_ge(sem("ga_projected"), T + 1)
                t = ps[:, 7, 0:256].rearrange("p (h s f) -> p h s f", s=2, f=4)
                shape = [128, 32, 4]
                cs = aux_t[:, T, 0:4].unsqueeze(1).broadcast_to(shape)
                sn = aux_t[:, T, 4:8].unsqueeze(1).broadcast_to(shape)
                a, c_, d, e = (probs[:, 1, 128 * i:128 * i + 128].rearrange("p (h f) -> p h f", f=4) for i in range(4))
                q(nc.vector.tensor_tensor(a, t[:, :, 0, :], cs, ALU.mult))
                q(nc.vector.tensor_tensor(c_, t[:, :, 1, :], sn, ALU.mult))
                q(nc.vector.tensor_tensor(d, t[:, :, 1, :], cs, ALU.mult))
                q(nc.vector.tensor_tensor(e, t[:, :, 0, :], sn, ALU.mult))
                qk = probs[:, 1, 512:768].rearrange("p (h s f) -> p h s f", s=2, f=4)
                q(nc.vector.tensor_tensor(qk[:, :, 0, :], a, c_, ALU.subtract))
                q(nc.vector.tensor_tensor(qk[:, :, 1, :], d, e, ALU.add))
                q(nc.vector.tensor_copy(kvD[:, T, 128:256], ps[:, 7, 256:384]))
                q(nc.vector.tensor_copy(qD[:, T, :], probs[:, 1, 512:640]))
                q(nc.vector.tensor_scalar(kvD[:, T, 0:128], probs[:, 1, 640:768], 8 ** -0.5, None, ALU.mult))
                dve.sem_inc(sem("ga_roped"), 1)

        def gather_scalar_sines(act):
            act.wait_ge(sem("ga_angles"), 1)
            nc.scalar.activation(small[:, 64:96], small[:, 0:32], ACT.Sin).then_inc(sem("ga_sines"), 1)

        def expand_tensor(pe):
            for T in range(TILES):
                pe.wait_ge(sem("ex_normed"), T + 1)
                nc.tensor.transpose(ps[:, 0, 0:128], row32[:, T % 2, :], ident[:]).then_inc(sem("ex_turned"), 1)
                pe.wait_ge(sem("ex_rowT"), T + 1)
                if T:
                    pe.wait_ge(sem("ex_gelu"), T)
                for c in range(4):
                    last = nc.tensor.matmul(ps[:, 1, 128 * c:128 * c + 128], w1_l1[:, 128 * c:128 * c + 128],
                                            rowT[:, T % 2, :], start=True, stop=True)
                last.then_inc(sem("ex_hidden"), 1)
                pe.wait_ge(sem("ex_gelu"), T + 1)
                if T:
                    pe.wait_ge(sem("ex_spread"), T)
                for c in range(4):
                    last = nc.tensor.matmul(ps[:, 2, 0:128], probs[:, 0, 128 * c:128 * c + 128], w2_l1[:, c, :],
                                            start=c == 0, stop=c == 3)
                last.then_inc(sem("ex_out"), 1)
                nc.tensor.transpose(ps[:, 3, 0:128], pick[:, T * PER_TILE:(T + 1) * PER_TILE, :]
                                    .rearrange("p b s -> p (b s)"), ident[:]).then_inc(sem("ex_pickT"), 1)
                pe.wait_ge(sem("ex_spread"), T + 1)
                if T:
                    pe.wait_ge(sem("ex_added"), T)
                for half in range(2):
                    last = nc.tensor.matmul(ps[:, 4 + half, :], rowT2[:], probs[:, 1, 512 * half:512 * half + 512],
                                            start=True, stop=True)
                last.then_inc(sem("ex_scattered"), 1)

        def expand_scalar(act):
            moments_scalar(act, TILES)
            for T in range(TILES):
                act.wait_ge(sem("ex_turned"), T + 1)
                nc.scalar.activation(rowT[:, T % 2, :], ps[:, 0, 0:128], ACT.Copy,
                                     scale=col("ln2")).then_inc(sem("ex_rowT"), 1)
                act.wait_ge(sem("ex_hidden"), T + 1)
                if T:
                    act.wait_ge(sem("ex_out"), T)
                nc.scalar.activation(probs[:, 0, 0:512], ps[:, 1, :], ACT.Gelu_apprx_tanh).then_inc(sem("ex_gelu"), 1)

        def expand_vector(dve):
            q = Seq(dve, sem("ex_seq"), moments_taken)
            moments_vector(dve, "rms", stat[:], TILES)
            for T in range(TILES):
                nc.vector.tensor_scalar(row32[:, T % 2, :], x1_tiles[:, T, :], inv_all[:, T:T + 1], None,
                                        ALU.mult).then_inc(sem("ex_normed"), 1)
                dve.wait_ge(sem("ex_pickT"), T + 1)
                if T:
                    dve.wait_ge(sem("ex_scattered"), T)
                q(nc.vector.tensor_copy(rowT2[:], ps[:, 3, 0:128]))
                dve.wait_ge(sem("ex_out"), T + 1)
                q(nc.vector.tensor_tensor(x1_tiles[:, T, :], x1_tiles[:, T, :], ps[:, 2, 0:128], ALU.add))
                q(nc.vector.tensor_scalar(x1_tiles[:, T, :], x1_tiles[:, T, :], aux_t[:, T, 8:9], None, ALU.mult))
                full = [128, PER_TILE, 128]
                q(nc.vector.tensor_tensor(probs[:, 1, 0:1024].rearrange("p (b d) -> p b d", b=PER_TILE),
                                          x1_tiles[:, T:T + 1, :].broadcast_to(full),
                                          own[:].unsqueeze(2).broadcast_to(full), ALU.mult))
                dve.sem_inc(sem("ex_spread"), 1)
                dve.wait_ge(sem("ex_scattered"), T + 1)
                part = x_all[:, T * PER_TILE:(T + 1) * PER_TILE, :]
                nc.vector.tensor_tensor(part, part, ps[:, 4:6, :].rearrange("p a (b d) -> p (a b) d", b=4),
                                        ALU.add).then_inc(sem("ex_added"), 1)
                dve.wait_ge(sem("ex_added"), T + 1)
                for b in range(T * PER_TILE, (T + 1) * PER_TILE):
                    nc.vector.bn_stats(stats_all[:, b, :], x_all[:, b, :]).then_inc(sem("measured"), 1)

        def bit_vector(dve):
            def norm_b(b, k):
                wait_reuse(dve, after("turned"), b, 2)
                link = Link(dve, after("link"), b, 6)
                m, r = mv[:, k % 2, :], row32[:, k % 2, :]
                link(norm(r, b))
                link(nc.vector.tensor_reduce(m[:, 3:4], r, AX.X, ALU.max, apply_absolute_value=True))
                link(nc.vector.tensor_scalar(m[:, 3:4], m[:, 3:4], 1e-5, 1.0 / 127.0, ALU.max, ALU.mult))
                link(nc.vector.reciprocal(m[:, 4:5], m[:, 3:4]))
                link(nc.vector.tensor_scalar(r, r, m[:, 4:5], MAGIC, ALU.mult, ALU.add))
                link(nc.vector.tensor_scalar(r, r, MAGIC, m[:, 3:4], ALU.subtract, ALU.mult))
                dve.sem_inc(sem("normed"), 1)
                link.end()

            def quantise(b, k):
                dve.wait_ge(sem("bt_silu"), b + 1)
                link = Link(dve, after("link2"), b, 5)
                h, r = probs[:, k % 2, 0:512], rank[:, k % 2, :]
                link(nc.vector.tensor_reduce(r[:, 0:1], h, AX.X, ALU.max, apply_absolute_value=True))
                link(nc.vector.tensor_scalar(r[:, 0:1], r[:, 0:1], 1e-5, 1.0 / 127.0, ALU.max, ALU.mult))
                link(nc.vector.reciprocal(r[:, 1:2], r[:, 0:1]))
                link(nc.vector.tensor_tensor(scale2[:, k:k + 1], r[:, 0:1], inv_w[:, 3:4], ALU.mult))
                link(nc.vector.tensor_scalar(h, h, r[:, 1:2], MAGIC, ALU.mult, ALU.add))
                wait_reuse(dve, after("bt_turned2"), b, 2)
                nc.vector.tensor_scalar(q2[:, k % 2, :], h, MAGIC, None, ALU.subtract).then_inc(sem("bt_quantised"), 1)
                link.end()

            def add(b, k):
                dve.wait_ge(sem("bt_out"), b + 1)
                nc.vector.scalar_tensor_tensor(x_all[:, b, :], ps[:, 6 + k % 2, 0:128], scale2[:, k:k + 1],
                                               x_all[:, b, :], ALU.mult, ALU.add).then_inc(sem("added"), 1)
                measure(dve, after("added"), b)

            def take2(b, k):
                dve.wait_ge(sem("bt_turned2"), b + 1)
                wait_reuse(dve, after("bt_out"), b, 2)
                nc.vector.tensor_copy(q2T[:, k % 2, :, :].rearrange("p c t -> p (c t)"),
                                      bank_b[4 + k % 2][:, 0:512]).then_inc(sem("bt_q2T"), 1)
            steps(dve, B, [(0, norm_b), (3, take2), (2, quantise), (4, add)])

        def bit_scalar(act):
            def silu(b, k):
                act.wait_ge(*after("used", b + 1))
                wait_reuse(act, after("bt_quantised"), b, 2)
                nc.scalar.activation(probs[:, k % 2, 0:512], ps[:, 2 + k % 2, :], ACT.Silu).then_inc(sem("bt_silu"), 1)
            steps(act, B, [(1, take_rows(act, dst=lambda k: xqT[:, k % 2, 1:129])), (2, silu)])

        def bit_tensor(pe):
            def hidden(b, k):
                pe.wait_ge(*after("rowT", b + 1))
                wait_reuse(pe, after("bt_silu"), b, 2)
                dst = ps[:, 2 + k % 2, :]
                nc.tensor.matmul(dst, onesb[0:3, :], bias_rows[:, 640:1152], start=True, stop=False)
                for tap in range(3):
                    last = nc.tensor.matmul(dst, xqT[:, k % 2, tap:tap + 128], tap_w[:, tap, :],
                                            start=False, stop=tap == 2)
                last.then_inc(sem("used"), 1)

            def turn2(b, k):
                pe.wait_ge(sem("bt_quantised"), b + 1)
                wait_reuse(pe, after("bt_q2T"), b, 2)
                for c in range(4):
                    last = nc.tensor.transpose(bank_b[4 + k % 2][:, 128 * c:128 * c + 128],
                                               q2[:, k % 2, 128 * c:128 * c + 128], identb[:])
                last.then_inc(sem("bt_turned2"), 1)

            def output(b, k):
                pe.wait_ge(sem("bt_q2T"), b + 1)
                wait_reuse(pe, after("added"), b, 2)
                for c in range(4):
                    last = nc.tensor.matmul(ps[:, 6 + k % 2, 0:128], q2T[:, k % 2, c, :], w2_q[:, c, :],
                                            start=c == 0, stop=c == 3)
                last.then_inc(sem("bt_out"), 1)
            steps(pe, B, [(1, turn_rows(pe)), (2, hidden), (3, turn2), (4, output)])

        def cross_vector(dve):
            def norm_b(b, k):
                wait_reuse(dve, after("turned"), b, 2)
                norm(row32[:, k % 2, :], b).then_inc(sem("normed"), 1)

            def take_ctx(b, k):
                dve.wait_ge(sem("cr_ctx_turned"), b + 1)
                wait_reuse(dve, after("cr_kv"), b, 2)
                nc.vector.tensor_copy(probs[:, k % 2, 0:256], ps[:, 2 + k % 2, 0:256]).then_inc(sem("cr_ctxT"), 1)

            def add(b, k):
                dve.wait_ge(*after("used", b + 1))
                nc.vector.tensor_tensor(x_all[:, b, :], x_all[:, b, :], ps[:, 4 + k % 2, 128:256],
                                        ALU.add).then_inc(sem("added"), 1)
            steps(dve, B, [(0, norm_b), (1, take_ctx), (3, add)])

        def cross_gpsimd(pool):
            def copy_ctx(b, k):
                wait_reuse(pool, after("cr_ctx_turned"), b, 2)
                hold(pool)
                nc.gpsimd.tensor_copy(probs[:, k % 2, 256:512], ctx_all[:, b, :]).then_inc(sem("cr_ctx"), 1)
            steps(pool, B, [(0, copy_ctx)])

        def cross_scalar(act):
            def take_q(b, k):
                act.wait_ge(*after("added", b + 1))
                nc.scalar.activation(q_all[:, b, :], ps[:, 4 + k % 2, 0:128], ACT.Copy,
                                     scale=mask_q[:, bass.ts(b, 1)]).then_inc(sem("cr_q"), 1)

            def take_kv(b, k):
                act.wait_ge(sem("cr_kv"), b + 1)
                nc.scalar.activation(kv_all[:, b, :], ps[:, 6 + k % 2, 0:256], ACT.Copy,
                                     scale=mask_f[:, bass.ts(b, 1)]).then_inc(sem("cr_kv_taken"), 1)
            steps(act, B, [(1, take_rows(act)), (3, take_kv), (3, take_q)])

        def cross_tensor(pe):
            def turn_ctx(b, k):
                pe.wait_ge(sem("cr_ctx"), b + 1)
                wait_reuse(pe, after("cr_ctxT"), b, 2)
                hold(pe)
                for c in range(2):
                    last = nc.tensor.transpose(ps[:, 2 + k % 2, 128 * c:128 * c + 128],
                                               probs[:, k % 2, 256 + 128 * c:384 + 128 * c], ident[:])
                last.then_inc(sem("cr_ctx_turned"), 1)

            def queries(b, k):
                pe.wait_ge(*after("rowT", b + 1))
                wait_reuse(pe, after("cr_q"), b, 2)
                dst = ps[:, 4 + k % 2, 0:256]
                nc.tensor.matmul(dst, onesb[0:3, :], bias_rows[:, 384:640], start=True, stop=False)
                nc.tensor.matmul(dst, rowT[:, k % 2, :], w_tgt[:], start=False, stop=True).then_inc(sem("used"), 1)

            def keys(b, k):
                pe.wait_ge(sem("cr_ctxT"), b + 1)
                wait_reuse(pe, after("cr_kv_taken"), b, 2)
                dst = ps[:, 6 + k % 2, 0:256]
                nc.tensor.matmul(dst, onesb[0:3, :], bias_rows[:, 128:384], start=True, stop=False)
                for c in range(2):
                    last = nc.tensor.matmul(dst, probs[:, k % 2, 128 * c:128 * c + 128], w_src[:, c, :],
                                            start=False, stop=c == 1)
                last.then_inc(sem("cr_kv"), 1)
            steps(pe, B, [(1, turn_rows(pe)), (1, turn_ctx), (2, queries), (2, keys)])

        def latent_vector(dve):
            def norm_b(b, k):
                wait_reuse(dve, after("turned"), b, 2)
                norm(row32[:, k % 2, :], b).then_inc(sem("normed"), 1)
                nc.vector.tensor_scalar(z_all[:, b, :], x_all[:, b, :], mean_all[:, bass.ts(b, 1)],
                                        inv_ln[:, bass.ts(b, 1)], ALU.subtract, ALU.mult).then_inc(sem("z_set"), 1)

            def rotate(link, src, at, dst, tmp):
                link(nc.vector.tensor_tensor(tmp[:, 0:128], src[:, 0:128], rope[:, at, :], ALU.mult))
                link(nc.vector.tensor_tensor(tmp[:, 128:256], src[:, 128:256], rope[:, at + 1, :], ALU.mult))
                return nc.vector.tensor_tensor(dst, tmp[:, 0:128], tmp[:, 128:256], ALU.add)

            def query(b, k):
                dve.wait_ge(*after("used", b + 1))
                link = Link(dve, after("link2"), b, 9)
                src = ps[:, 2 + k % 2, :]
                m, st = small[:, 8 * (k % 2):8 * (k % 2) + 8], small[:, 32 + 8 * (k % 2):38 + 8 * (k % 2)]
                link(nc.vector.bn_stats(st, src[:, 256:320]))
                hold(dve)
                link(nc.vector.bn_aggr(m[:, 0:2], st))
                link(nc.vector.tensor_scalar(m[:, 2:3], m[:, 1:2], 1e-5, None, ALU.add))
                dve.sem_inc(sem("la_variance"), 1)
                rotate(link, src, 0, q_all[:, b, :], junk).then_inc(sem("la_q"), 1)
                dve.wait_ge(sem("la_root"), b + 1)
                link(nc.vector.reciprocal(m[:, 4:5], m[:, 3:4]))
                link(nc.vector.tensor_scalar(m[:, 5:6], m[:, 4:5], m[:, 4:5], m[:, 2:3], ALU.mult, ALU.mult))
                link(nc.vector.tensor_scalar(m[:, 5:6], m[:, 5:6], -0.5, 1.5, ALU.mult, ALU.add))
                link(nc.vector.tensor_tensor(m[:, 4:5], m[:, 4:5], m[:, 5:6], ALU.mult))
                wait_reuse(dve, after("la_latent_turned"), b, 2)
                nc.vector.tensor_scalar(o_sb[:, k % 2, 0:LATENT], src[:, 256:320], m[:, 0:1], m[:, 4:5],
                                        ALU.subtract, ALU.mult).then_inc(sem("la_latent"), 1)
                link.end()

            def latent(b, k):
                dve.wait_ge(sem("la_latent_turned"), b + 1)
                wait_reuse(dve, after("la_kv"), b, 2)
                nc.vector.tensor_scalar(oT[0:LATENT, k % 2, :], ps[0:LATENT, 4 + k % 2, 0:128], col("ln_g", LATENT),
                                        col("ln_b", LATENT), ALU.mult, ALU.add).then_inc(sem("la_latentT"), 1)

            def key(b, k):
                dve.wait_ge(sem("la_kv"), b + 1)
                link = Link(dve, after("link3"), b, 2)
                rotate(link, ps[:, 6 + k % 2, :], 2, kv_all[:, b, 0:128], probs[:, k % 2, 0:256]).then_inc(sem("la_k"), 1)
                link.end()
            steps(dve, B, [(0, norm_b), (2, query), (3, latent), (4, key)])

        def latent_scalar(act):
            def root(b, k):
                act.wait_ge(sem("la_variance"), b + 1)
                m = small[:, 8 * (k % 2):8 * (k % 2) + 8]
                nc.scalar.activation(m[:, 3:4], m[:, 2:3], ACT.Sqrt).then_inc(sem("la_root"), 1)

            def take_v(b, k):
                act.wait_ge(sem("la_k"), b + 1)
                nc.scalar.activation(kv_all[:, b, 128:256], ps[:, 6 + k % 2, 256:384],
                                     ACT.Copy).then_inc(sem("la_v"), 1)
            steps(act, B, [(1, take_rows(act, col("norm1"))), (2, root), (4, take_v)])

        def latent_tensor(pe):
            def queries(b, k):
                pe.wait_ge(*after("rowT", b + 1))
                wait_reuse(pe, after("la_latent"), b, 2)
                nc.tensor.matmul(ps[:, 2 + k % 2, 0:320], rowT[:, k % 2, :], w_h1[:], start=True,
                                 stop=True).then_inc(sem("used"), 1)

            def turn_latent(b, k):
                pe.wait_ge(sem("la_latent"), b + 1)
                wait_reuse(pe, after("la_latentT"), b, 2)
                hold(pe)
                nc.tensor.transpose(ps[0:LATENT, 4 + k % 2, 0:128], o_sb[:, k % 2, 0:LATENT],
                                    ident[:]).then_inc(sem("la_latent_turned"), 1)

            def keys(b, k):
                pe.wait_ge(sem("la_latentT"), b + 1)
                wait_reuse(pe, after("la_v"), b, 2)
                nc.tensor.matmul(ps[:, 6 + k % 2, 0:384], oT[0:LATENT, k % 2, :], w_h2[:], start=True,
                                 stop=True).then_inc(sem("la_kv"), 1)
            steps(pe, B, [(1, turn_rows(pe)), (2, queries), (3, turn_latent), (4, keys)])

        GROUPS = B // 4
        w_up = ctx_all[:, 0:8, :].rearrange("p a b -> p (a b)").rearrange("p (c h) -> p c h", c=16)
        w_down = ctx_all[:, 8:16, :].rearrange("p a b -> p (a b)").rearrange("p (c h) -> p c h", c=16)
        work_m = kv_all[:, 0:24, :].rearrange("p a b -> p (a b)")
        xm_rows = work_m[:, 0:512]
        xm_T = work_m[:, 512:1024]
        chosen = work_m[:, 1024:3072].rearrange("p (e t) -> p e t", e=4)
        total = work_m[:, 3072:3584]
        term = work_m[:, 3584:4096]
        hid = work_m[:, 4096:6144].rearrange("p (s t) -> p s t", s=4)

        def loop_groups(engine, body):
            with engine.Fori(0, GROUPS, 1) as i:
                body(i)

        def expert_vector(dve):
            def group(i):
                link = Link(dve, after("mo_link"), i, 17)
                rows = x_all[:, bass.ts(i, 4), :]
                for j in range(4):
                    link(nc.vector.tensor_scalar(xm_rows[:, 128 * j:128 * j + 128], z_all[:, i * 4 + j, :],
                                                 inv_all[:, bass.ts(i * 4 + j, 1)], None, ALU.mult))
                dve.sem_inc(sem("mo_normed"), 1)
                dve.wait_ge(sem("mo_turned"), i + 1)
                nc.vector.tensor_scalar(xm_T, ps[:, 2, :], col("norm2"), None, ALU.mult).then_inc(sem("mo_rowT"), 1)
                dve.wait_ge(sem("mo_logits"), i + 1)
                lg = small[:, 64:80].rearrange("p (j e) -> p j e", j=4)
                eq = small[:, 80:96].rearrange("p (j e) -> p j e", j=4)
                top = small[:, 96:100]
                full = [128, 4, 4]
                link(nc.vector.tensor_tensor(lg, ps[:, 3, 0:16].rearrange("p (j e) -> p j e", j=4),
                                             gate_b[:].unsqueeze(1).broadcast_to(full), ALU.add))
                link(nc.vector.tensor_reduce(top, lg, AX.X, ALU.max))
                link(nc.vector.tensor_tensor(eq, lg, top.unsqueeze(2).broadcast_to(full), ALU.is_equal))
                link(nc.vector.tensor_tensor(eq, eq, first_row[:].unsqueeze(1).broadcast_to(full), ALU.mult))
                link(nc.vector.tensor_reduce(top, eq, AX.X, ALU.max))
                nc.vector.tensor_tensor(nm3[:, 0, 0:48].rearrange("p (e j c) -> p j e c", e=4, c=3)[:, :, :, 0], eq,
                                        top.unsqueeze(2).broadcast_to(full), ALU.is_equal).then_inc(sem("mo_choice"), 1)
                dve.wait_ge(sem("mo_choice_turned"), i + 1)
                nc.vector.tensor_copy(nmT[:, 0, :], bank_b[3][:, 128:256]).then_inc(sem("mo_choiceT"), 1)
                for e in range(N_EXP3):
                    dve.wait_ge(sem("mo_along"), i * 4 + (e + 1))
                    nc.vector.tensor_copy(chosen[:, e, :], ps[:, 6, :]).then_inc(sem("mo_chosen"), 1)
                dve.wait_ge(sem("mo_chosen"), i * 4 + 4)
                for c in range(16):
                    e = c // 4
                    if c % 2:
                        dve.wait_ge(sem("mo_hidden"), i * 16 + (c + 1))
                        if c >= 4:
                            dve.wait_ge(sem("mo_down"), i * 16 + (c - 3))
                        nc.vector.tensor_scalar(hid[:, c % 4, :], ps[:, c % 2, :], b1_col[:, c:c + 1], 0.0,
                                                ALU.add, ALU.max).then_inc(sem("mo_relu_odd"), 1)
                    if c % 4 == 3 and e > 0:
                        combine(i, link, e - 1)
                combine(i, link, 3)
                dve.sem_inc(sem("mo_total"), 1)
                dve.wait_ge(sem("mo_joined"), i + 1)
                dve.wait_ge(sem("mo_back"), i + 1)
                nc.vector.tensor_tensor(rows, rows, ps[:, 7, :].rearrange("p (j d) -> p j d", j=4),
                                        ALU.add).then_inc(sem("mo_done"), 1)
                dve.wait_ge(sem("mo_done"), i + 1)
                link.end()

            def combine(i, link, e):
                dve.wait_ge(sem("mo_down"), i * 16 + 4 * (e + 1))
                dst = total if e == 0 else term
                link(nc.vector.scalar_tensor_tensor(dst, ps[:, 4 + e % 2, :], b2_col[:, e:e + 1], chosen[:, e, :],
                                                    ALU.add, ALU.mult))
                dve.sem_inc(sem("mo_combined"), 1)
                link(nc.vector.tensor_tensor(total, total, term, ALU.add) if e else
                     nc.vector.tensor_copy(small[:, 100:101], b2_col[:, 0:1]))

            loop_groups(dve, group)

        def expert_scalar(act):
            def group(i):
                for c in range(0, 16, 2):
                    act.wait_ge(sem("mo_hidden"), i * 16 + (c + 1))
                    if c >= 4:
                        act.wait_ge(sem("mo_down"), i * 16 + (c - 3))
                    nc.scalar.activation(hid[:, c % 4, :], ps[:, c % 2, :], ACT.Relu,
                                         bias=b1_col[:, c:c + 1]).then_inc(sem("mo_relu_even"), 1)
            loop_groups(act, group)

        def expert_gpsimd(pool):
            def group(i):
                rows = x_all[:, bass.ts(i, 4), :]
                nc.gpsimd.tensor_tensor(rows, rows, z_all[:, bass.ts(i, 4), :], ALU.add).then_inc(sem("mo_joined"), 1)
            loop_groups(pool, group)

        def expert_tensor(pe):
            def group(i):
                pe.wait_ge(sem("mo_normed"), i + 1)
                hold(pe)
                for j in range(4):
                    last = nc.tensor.transpose(ps[:, 2, 128 * j:128 * j + 128], xm_rows[:, 128 * j:128 * j + 128],
                                               ident[:])
                last.then_inc(sem("mo_turned"), 1)
                pe.wait_ge(sem("mo_rowT"), i + 1)
                for j in range(4):
                    last = nc.tensor.matmul(ps[:, 3, 4 * j:4 * j + 4], xm_T[:, 128 * j:128 * j + 128], gate_w[:],
                                            start=True, stop=True)
                last.then_inc(sem("mo_logits"), 1)

                def up(c):
                    if c >= 2:
                        pe.wait_ge(sem("mo_relu_odd" if c % 2 else "mo_relu_even"), i * 8 + c // 2)
                    nc.tensor.matmul(ps[:, c % 2, :], w_up[:, c, :], xm_T, start=True,
                                     stop=True).then_inc(sem("mo_hidden"), 1)

                up(0)
                up(1)
                pe.wait_ge(sem("mo_choice"), i + 1)
                hold(pe)
                nc.tensor.transpose(bank_b[3][:, 128:256], nm3[:, 0, :], identb[:]).then_inc(sem("mo_choice_turned"), 1)
                pe.wait_ge(sem("mo_choiceT"), i + 1)
                for e in range(N_EXP3):
                    if e:
                        pe.wait_ge(sem("mo_chosen"), i * 4 + e)
                    for j in range(4):
                        last = nc.tensor.matmul(ps[:, 6, 128 * j:128 * j + 128], sel[:, 4 * e + j, :], nmT[:, 0, :],
                                                start=True, stop=True)
                    last.then_inc(sem("mo_along"), 1)
                for c in range(16):
                    e = c // 4
                    pe.wait_ge(sem("mo_relu_odd" if c % 2 else "mo_relu_even"), i * 8 + (c // 2 + 1))
                    if c % 4 == 0 and e >= 2:
                        pe.wait_ge(sem("mo_combined"), i * 4 + (e - 1))
                    nc.tensor.matmul(ps[:, 4 + e % 2, :], w_down[:, c, :], hid[:, c % 4, :], start=c % 4 == 0,
                                     stop=c % 4 == 3).then_inc(sem("mo_down"), 1)
                    if c + 2 < 16:
                        up(c + 2)
                pe.wait_ge(sem("mo_total"), i + 1)
                hold(pe)
                for j in range(4):
                    last = nc.tensor.transpose(ps[:, 7, 128 * j:128 * j + 128], total[:, 128 * j:128 * j + 128],
                                               ident[:])
                last.then_inc(sem("mo_back"), 1)
            loop_groups(pe, group)

        lens_i = probs[:, 1, 1664:1792].bitcast(I32).rearrange("p (n b) -> p n b", n=4)
        bias_rows_f = probs[0:3, 1, 512:1664]
        w2_nat = probs[:, 1, 0:512]
        w1_nat = probs[:, 0, 0:512]
        conv_f = probs[:, 0, 512:2048].rearrange("p (t c) -> p t c", t=3)

        loads = [
            (ident[:], t_in["c_ident"]), (upper[:], t_in["c_upper"]), (below[:], t_in["c_below"]),
            (above[:], t_in["c_above"]), (toep[:], t_in["c_toep"]), (iota_p[:], t_in["c_iota_p"]),
            (iota_row[:], t_in["c_iota_row"]), (sel_col[:], t_in["c_sel"]),
            (rope[:], t_in["c_rope"]), (outside[:], t_in["c_outside"]), (own[:], t_in["c_own"]),
            (freq[:], t_in["c_freq"]), (first_row[:], t_in["c_first"]),
            (lens_i[:, 0, :], t_in["itok"].rearrange("b one -> (one b)").partition_broadcast(128)),
            (lens_i[:, 1, :], t_in["ik0T"]), (lens_i[:, 2, :], t_in["if0T"]),
            (lens_i[:, 3, 0:4], t_in["posT"][0:S, :]),
            (mask_f[:], t_in["fk1T"]),
            (g_init[:], t_in["g_init"][0:D].partition_broadcast(128)),
            (wg[:], t_in["w_inT"]), (w_qkv[:, 0:128], t_in["wq"]), (w_qkv[:, 128:256], t_in["wk"]),
            (w_qkv[:, 256:384], t_in["wv"]), (w_o1[:], t_in["wo"]), (w1_l1[:], t_in["w1"]),
            (w2_l1[:], t_in["w2"].rearrange("(c n) d -> n c d", n=128)),
            (cls_mask[:], t_in["amask"][:, 0, 0:S, 0:S].rearrange("c t u -> t c u")),
            (w1_nat, t_in["b_w1T"]), (w2_nat.rearrange("p (c d) -> p c d", c=4),
                                      t_in["b_w2T"].rearrange("(c n) d -> n c d", n=128)),
            (conv_f, t_in["conv_wT"].partition_broadcast(128)),
            (w_src[:], t_in["W_srcT"].rearrange("(c f) o -> f c o", f=128)),
            (w_tgt[:, 0:128], t_in["W_tgtT"]), (w_tgt[:, 128:256], t_in["W_outT"][0:128, :]),
            (w_out2[:], t_in["W_outT"][128:256, :]),
            (w_h1[:, 0:128], t_in["WqT"]), (w_h1[:, 128:256], t_in["WqT_turned"]), (w_h1[:, 256:320], t_in["WdkvT"]),
            (w_h2[:, 0:128], t_in["WukT"]), (w_h2[:, 128:256], t_in["WukT_turned"]), (w_h2[:, 256:384], t_in["WuvT"]),
            (w_o3[:], t_in["WoT"]), (gate_w[:], t_in["gateT"]), (gate_b[:], t_in["gate_b"].partition_broadcast(128)),
            (b1_col[:], t_in["b1T"]), (b2_col[:], t_in["b2T"]),
            (bias_rows_f[:, 0:128], t_in["b_in"].partition_broadcast(3)),
            (bias_rows_f[:, 128:384], t_in["b_src"].partition_broadcast(3)),
            (bias_rows_f[:, 384:512], t_in["b_tgt"].partition_broadcast(3)),
            (bias_rows_f[:, 512:640], t_in["b_out"].partition_broadcast(3)),
            (bias_rows_f[:, 640:1152], t_in["conv_b"].partition_broadcast(3)),
            (col("L0_b"), t_in["L0_b"].rearrange("(s one) -> s one", one=1)),
            (col("L2_b"), t_in["L2_b"].partition_broadcast(128)),
            (col("router_b"), t_in["router_b"].partition_broadcast(128)),
            (col("router_w"), t_in["router_w"]),
        ] + [(col(n, t_in[n].shape[0]), t_in[n].rearrange("(s one) -> s one", one=1))
             for n in ("g_res", "ln1", "ln2", "norm1", "norm2", "ln_g", "ln_b")]

        def prep_sync(sp):
            sp.dma_start(ctx_all[:], t_in["ctx"].rearrange("b s d -> s b d")).then_inc(sem("ctx_loaded"), 16)
            sp.dma_start(x_all[:], t_in["x"].rearrange("b s d -> s b d")).then_inc(sem("x_loaded"), 16)
            sp.dma_start(kv_all[:, :, 0:128], t_in["f0_w1T"].rearrange("e (c n) h -> n (e c) h", n=128)
                         ).then_inc(sem("l0_weights"), 16)
            sp.dma_start(kv_all[:, :, 128:256], t_in["f0_w2"].rearrange("e (c n) h -> n (e c) h", n=128)
                         ).then_inc(sem("l0_weights"), 16)
            sp.wait_ge(sem("x_loaded"), 16)
            sp.wait_ge(sem("ctx_loaded"), 16)

        def prep_scalar(act):
            for dst, src in loads:
                act.dma_start(dst, src, allow_slow_non_contiguous=True).then_inc(sem("small_loaded"), 16)

        def prep_tensor(pe):
            pe.wait_ge(sem("valid_ready"), 1)
            nc.tensor.matmul(ps[:, 0, 0:B], ones[:], lens_f[:], start=True, stop=True).then_inc(sem("valid_counted"), 1)
            pe.wait_ge(sem("abs_ready"), 1)
            nc.tensor.matmul(ps[:, 1, 0:2], ones[:], inv_w[:, 0:2], start=True, stop=True).then_inc(sem("abs_summed"), 1)
            ffn0_prep_tensor(pe)

        def prep_gpsimd(pool):
            nc.gpsimd.memset(ones[:], 1.0).then_inc(sem("ones_set"), 1)

        def prep_vector(dve):
            q = Seq(dve, sem("prep_seq"), moments_taken)
            dve.wait_ge(sem("small_loaded"), 16 * len(loads))
            dve.wait_ge(sem("ones_set"), 1)
            V = nc.vector
            q(V.tensor_copy(identb[:], ident[:]))
            q(V.tensor_copy(upperb[:], upper[:]))
            q(V.tensor_copy(onesb[:], ones[:]))
            q(V.memset(xqT[:], 0.0))
            q(V.tensor_copy(sel[:], sel_col[:].unsqueeze(2).broadcast_to([128, 16, 128])))
            q(V.tensor_scalar(causal[:], above[:], BIG, None, ALU.mult))
            bias = small[:, 0:B]
            valid = small[:, B:2 * B]
            q(V.tensor_copy(lens_f[:], lens_i[:, 1, :]))
            dve.sem_inc(sem("valid_ready"), 1)
            dve.wait_ge(sem("valid_counted"), 1)
            q(V.tensor_scalar(k_scale[:, 1, :], ps[:, 0, 0:B], 0.5, 16 ** -0.5, ALU.is_gt, ALU.mult))

            def to_bias(which, penalty, add, any_valid):
                q(V.tensor_scalar(bias, valid, 1.0, penalty, ALU.subtract, ALU.mult))
                if add is not None:
                    q(V.tensor_scalar(bias, bias, add, None, ALU.add))
                if any_valid is not None:
                    q(V.tensor_tensor(bias, bias, any_valid, ALU.mult))
                for part in range(3):
                    q(V.tensor_copy(bias3[:, which, :, part], bias))
                    q(V.tensor_tensor(bias, bias, bias3[:, which, :, part], ALU.subtract))

            q(V.tensor_scalar(valid, ps[:, 0, 0:B], 0.5, None, ALU.is_gt))
            q(V.tensor_copy(small[:, 96:128], valid))
            q(V.tensor_copy(valid, lens_f[:]))
            to_bias(1, 1e30, col("L2_b"), small[:, 96:128])
            q(V.tensor_copy(lens_f[:], lens_i[:, 0, :]))
            q(V.tensor_scalar(valid, lens_f[:], iota_p[:, 0:1], None, ALU.is_gt))
            q(V.tensor_scalar(k_scale[:, 0, :], lens_f[:], 0.0, 8 ** -0.5, ALU.is_gt, ALU.mult))
            q(V.tensor_scalar(small[:, 96:128], lens_f[:], 0.0, None, ALU.is_gt))
            to_bias(0, 1e12, col("L0_b"), small[:, 96:128])
            q(V.tensor_scalar(valid, mask_f[:], 0.0, None, ALU.not_equal))
            to_bias(2, 1e30, None, None)
            q(V.tensor_scalar(mask_q[:], mask_f[:], 0.25, None, ALU.mult))
            q(V.tensor_copy(lens_f[:], lens_i[:, 2, :]))
            q(V.tensor_copy(pos_f[:], lens_i[:, 3, 0:4]))
            q(V.tensor_scalar(wg[:], wg[:], col("g_res"), None, ALU.mult))
            q(V.tensor_scalar(rw_rep[:], ones[:], col("router_w"), None, ALU.mult))
            q(V.tensor_scalar(g_init[:], g_init[:], PATCH_GAIN, None, ALU.mult))
            part = w_part[0:3, :]
            for p in range(3):
                q(V.tensor_copy(part, bias_rows_f))
                q(V.tensor_tensor(bias_rows_f, bias_rows_f, part, ALU.subtract))
                if p == 0:
                    q(V.tensor_scalar(bias_rows[:], part, ident[0:3, 0:1], None, ALU.mult))
                else:
                    q(V.scalar_tensor_tensor(bias_rows[:], part, ident[0:3, p:p + 1], bias_rows[:], ALU.mult, ALU.add))
            q(V.tensor_reduce(inv_w[:, 0:1], w1_nat, AX.X, ALU.add, apply_absolute_value=True))
            q(V.tensor_reduce(inv_w[:, 1:2], w2_nat, AX.X, ALU.add, apply_absolute_value=True))
            dve.sem_inc(sem("abs_ready"), 1)
            dve.wait_ge(sem("abs_summed"), 1)
            q(V.tensor_scalar(inv_w[:, 2:4], ps[:, 1, 0:2], 1.0 / (D * HID), 1e-5, ALU.mult, ALU.max))
            q(V.reciprocal(inv_w[:, 0:2], inv_w[:, 2:4]))
            for w, i in ((w1_nat, 0), (w2_nat, 1)):
                q(V.tensor_scalar(w, w, inv_w[:, i:i + 1], MAGIC, ALU.mult, ALU.add))
                q(V.tensor_scalar(w, w, MAGIC, -1.0, ALU.subtract, ALU.max))
            q(V.tensor_scalar(w1_nat, w1_nat, 1.0, inv_w[:, 2:3], ALU.min, ALU.mult))
            q(V.tensor_scalar(w2_q[:].rearrange("p c d -> p (c d)"), w2_nat, 1.0, None, ALU.min))
            for tap in range(3):
                q(V.tensor_tensor(tap_w[:, tap, :], w1_nat, conv_f[:, tap, :], ALU.mult))
            ffn0_prep_vector(dve)

        setups = {}

        def pads_vector(dve, heads):
            n = setups["v"] = setups.get("v", 0) + 1
            dh, R, NU = rows_of(heads)
            nc.vector.memset(q_pad[:], 0.0).then_inc(sem("q_cleared"), 1)
            nc.vector.memset(nm3[:], 0.0).then_inc(sem("q_cleared"), 1)
            dve.wait_ge(sem("q_cleared"), 2 * n)
            for i in range(2):
                nc.vector.memset(q_pad[:, i, :].rearrange("p (h r) -> p h r", h=heads)[:, :, 6 * dh:6 * dh + 3],
                                 1.0).then_inc(sem("q_ones"), 1)
            dve.wait_ge(sem("q_ones"), 2 * n)

        def pads_gpsimd(pool, heads):
            n = setups["g"] = setups.get("g", 0) + 1
            dh, R, NU = rows_of(heads)
            G, each = heads // 2, dh + 1
            nc.gpsimd.memset(k_pad[:], 0.0).then_inc(sem("k_cleared"), 1)
            nc.gpsimd.memset(v_wide[:], 0.0).then_inc(sem("k_cleared"), 1)
            pool.wait_ge(sem("k_cleared"), 4 * n - 2)
            for i in range(2):
                nc.gpsimd.memset(v_wide[:, i, :, 0:G * (G + 1) * each].rearrange(
                    "p g (h n) -> p g h n", h=G)[:, :, :, dh:each], 1.0).then_inc(sem("k_cleared"), 1)
            pool.wait_ge(sem("k_cleared"), 4 * n)

        def latent_moments_vector(dve):
            moments_vector(dve, "ln")
            nc.vector.tensor_copy(inv_ln[:], inv_all[:]).then_inc(sem("inv_ln_kept"), 1)
            dve.wait_ge(sem("inv_ln_kept"), 1)
            moments_vector(dve, "ln_rms6")

        def expert_loads(sp):
            sp.dma_start(w_up.rearrange("p (e c) h -> p e (c h)", e=N_EXP3), t_in["W1T"].rearrange("e d n -> d e n")).then_inc(sem("experts_loaded"), 16)
            sp.dma_start(w_down, t_in["W2T"].rearrange("e (c h) d -> h (e c) d", h=128)).then_inc(sem("experts_loaded"), 16)
            sp.wait_ge(sem("experts_loaded"), 32)

        def store(sp):
            sp.dma_start(out.rearrange("b s d -> s b d"), x_all[:]).then_inc(sem("stored"), 16)
            sp.wait_ge(sem("stored"), 16)

        def tile_mask(u, k, part):
            return mask3[:, k, part, :]

        def causal_mask(u, k, part):
            return causal[:]

        def clear_choice(dve):
            nc.vector.memset(nm3[:], 0.0).then_inc(sem("choice_cleared"), 1)
            dve.wait_ge(sem("choice_cleared"), 1)

        def gather_act(act):
            gather_scalar_sines(act)
            gather_scalar(act)

        def first_stats_vector(dve):
            for b in range(B):
                nc.vector.bn_stats(stats_all[:, b, :], x_all[:, b, :]).then_inc(sem("measured"), 1)
            dve.wait_ge(sem("squares_ready"), 1)
            moments_vector(dve, "direct")
            nc.vector.tensor_copy(ctx_inv[:], inv_all[:]).then_inc(sem("ctx_measured"), 1)

        def first_stats_scalar(act):
            for b in range(B):
                if b >= 2:
                    act.wait_ge(sem("squares"), b - 1)
                nc.scalar.activation(probs[:, b % 2, 0:C], ctx_all[:, b, :], ACT.Square,
                                     accum_out=moment[:, 1, b:b + 1]).then_inc(sem("squares"), 1)
            act.wait_ge(sem("squares"), B)
            act.sem_inc(sem("squares_ready"), 1)
            moments_scalar(act)

        def row_counts(**more):
            return {n: B * each for n, each in dict(normed=1, turned=1, rowT=1, used=1, **more).items()}

        phases = [
            dict(sync=prep_sync, scalar=prep_scalar, tensor=prep_tensor, gpsimd=prep_gpsimd, vector=prep_vector),
            dict(vector=first_stats_vector, scalar=first_stats_scalar),
            dict(vector=lambda e: (pads_vector(e, 16), attention_vector(e, "L0", B, 16, True, False)),
                 counts=attention_counts(B, 16, True, False),
                 gpsimd=lambda e: (pads_gpsimd(e, 16), attention_gpsimd(e, "L0", B, 16, True)),
                 scalar=lambda e: attention_scalar(e, "L0", B, 16, True, False),
                 tensor=lambda e: attention_tensor(e, "L0", B, 16, 0, None, None)),
            dict(vector=ffn0_vector, scalar=ffn0_scalar, tensor=ffn0_tensor, counts=row_counts(added=1)),
            dict(vector=depool_vector, scalar=depool_scalar, tensor=depool_tensor,
                 counts=row_counts(added=1, link2=2, link3=1)),
            dict(vector=route_vector, scalar=route_scalar, tensor=route_tensor, counts=row_counts(link2=7)),
            dict(vector=gather_vector, scalar=gather_act, tensor=gather_tensor),
            dict(vector=lambda e: (pads_vector(e, 16), attention_vector(e, "L1", TILES, 16, False, True)),
                 counts=attention_counts(TILES, 16, False, True),
                 gpsimd=lambda e: (pads_gpsimd(e, 16), attention_gpsimd(e, "L1", TILES, 16, False)),
                 scalar=lambda e: attention_scalar(e, "L1", TILES, 16, False, True),
                 tensor=lambda e: attention_tensor(e, "L1", TILES, 16, 3, tile_mask, w_o1[:])),
            dict(vector=expand_vector, scalar=expand_scalar, tensor=expand_tensor),
            dict(vector=lambda e: (pads_vector(e, 8), attention_vector(e, "L2", B, 8, True, False)),
                 counts=attention_counts(B, 8, True, False),
                 gpsimd=lambda e: (pads_gpsimd(e, 8), attention_gpsimd(e, "L2", B, 8, True)),
                 scalar=lambda e: attention_scalar(e, "L2", B, 8, True, False),
                 tensor=lambda e: attention_tensor(e, "L2", B, 8, 0, None, None)),
            dict(vector=bit_vector, scalar=bit_scalar, tensor=bit_tensor,
                 counts=row_counts(added=1, link=6, link2=5)),
            dict(vector=cross_vector, scalar=cross_scalar, tensor=cross_tensor, gpsimd=cross_gpsimd,
                 counts=row_counts(added=1)),
            dict(vector=lambda e: (pads_vector(e, 8), attention_vector(e, "L3", B, 8, False, True)),
                 counts=attention_counts(B, 8, False, True),
                 gpsimd=lambda e: (pads_gpsimd(e, 8), attention_gpsimd(e, "L3", B, 8, False)),
                 scalar=lambda e: attention_scalar(e, "L3", B, 8, False, True),
                 tensor=lambda e: attention_tensor(e, "L3", B, 8, 0, None, w_out2[:])),
            dict(vector=lambda e: (latent_moments_vector(e), latent_vector(e)), tensor=latent_tensor,
                 scalar=lambda e: (moments_scalar(e), moments_scalar(e), latent_scalar(e)),
                 counts=row_counts(link2=9, link3=2)),
            dict(vector=lambda e: (pads_vector(e, 16), attention_vector(e, "L4", B, 16, False, True)),
                 counts=attention_counts(B, 16, False, True),
                 gpsimd=lambda e: (pads_gpsimd(e, 16), attention_gpsimd(e, "L4", B, 16, False)),
                 scalar=lambda e: attention_scalar(e, "L4", B, 16, False, True),
                 tensor=lambda e: attention_tensor(e, "L4", B, 16, 1, causal_mask, w_o3[:]),
                 sync=expert_loads),
            dict(vector=lambda e: (clear_choice(e), expert_vector(e)), scalar=expert_scalar, tensor=expert_tensor, gpsimd=expert_gpsimd),
        ]

        def with_moments(kind, phase):
            v, a = phase["vector"], phase["scalar"]
            return dict(phase, vector=lambda e: (moments_vector(e, kind), v(e)),
                        scalar=lambda e: (moments_scalar(e), a(e)))

        for at, kind in ((2, "ln"), (3, "ln"), (4, "ln_rms"), (5, "ln"), (9, "ln"), (10, "ln"), (11, "ln"),
                         (15, "rms")):
            phases[at] = with_moments(kind, phases[at])

        def run(engine, name):
            engine_name[engine] = name
            begun.clear()
            for phase in phases:
                if name in phase:
                    phase[name](engine)
                phase_end(engine)
                for n, count in phase.get("counts", {}).items():
                    begun[n] = begun.get(n, 0) + count

        block = ctx_.enter_context(nc.Block())

        @block.sync
        def _(sp):
            run(sp, "sync")
            store(sp)

        @block.scalar
        def _(act):
            run(act, "scalar")

        @block.gpsimd
        def _(pool):
            run(pool, "gpsimd")

        @block.vector
        def _(dve):
            run(dve, "vector")

        @block.tensor
        def _(pe):
            run(pe, "tensor")


def constants():
    t = np.arange(128)
    a = np.exp(np.float64(np.log(-np.expm1(-0.001))))
    power = t[:, None] - t[None, :]
    f32 = np.float32
    inv = 1.0 / 10000.0 ** (np.arange(4) / 4)
    ang = np.arange(S)[:, None].astype(f32) * inv.astype(f32)[None, :]
    cos, sin = np.cos(ang.astype(np.float64)), np.sin(ang.astype(np.float64))
    cos_q = np.tile(np.concatenate([cos, cos], 1), (1, 16))
    sin_q = np.tile(np.concatenate([-sin, sin], 1), (1, 16))
    s = 8 ** -0.5
    slot = np.arange(128) % SLOTS
    batch = np.arange(128) // SLOTS
    sel = np.zeros((128, 16))
    for i in range(16):
        sel[3 * i:3 * i + 3, i] = sel[64 + 3 * i:64 + 3 * i + 3, i] = 1
    return {
        "c_ident": np.eye(128, dtype=f32),
        "c_upper": (t[:, None] <= t[None, :]).astype(f32),
        "c_below": (t[None, :] < t[:, None]).astype(f32),
        "c_above": (t[None, :] > t[:, None]).astype(f32),
        "c_toep": np.where(power >= 0, a ** np.maximum(power, 0), 0).astype(f32),
        "c_iota_p": np.stack([t, t + 1, t - 127], 1).astype(f32),
        "c_iota_row": np.tile(np.arange(SLOTS), (128, 1)).astype(f32),
        "c_sel": sel.astype(f32),
        "c_rope": np.stack([cos_q, sin_q, cos_q * s, sin_q * s], 1).astype(f32),
        "c_outside": np.where((batch[:, None] == batch[None, :]) & (slot[None, :] < KEPT), 0, BIG).astype(f32),
        "c_own": (batch[:, None] == np.arange(PER_TILE)[None, :]).astype(f32),
        "c_freq": np.tile(inv.astype(f32), (128, 1)),
        "c_first": np.tile(np.arange(N_EXP3, 0, -1), (128, 1)).astype(f32),
    }


def kernel(**inputs):
    import concourse.bacc as bacc
    from concourse.bass_utils import run_bass_kernel_spmd
    get = {k: np.asarray(v) for k, v in inputs.items()}
    T = lambda a, *p: np.ascontiguousarray(np.transpose(a, p or None))
    turned = np.arange(128).reshape(16, 2, 4)[:, ::-1, :].reshape(-1)
    wqT, wukT = T(get["L3_ffn_Wq"]), T(get["L3_ffn_Wuk"])
    arrays = {
        "x": get["x"], "ctx": get["ctx_2048"], "itok": get["itok_Bx1_68_817"],
        "if0T": T(get["mask_BxS2_if0"]), "ik0T": T(get["mask_BxS2_ik0"]), "fk1T": T(get["mask_BxS2_fk1"]),
        "L0_b": get["L0_xattn_b"], "f0_w1T": T(get["L0_ffn_w1"], 0, 2, 1), "f0_w2": get["L0_ffn_w2"],
        "w_inT": T(get["L1_xattn_W_in"]), "b_in": get["L1_xattn_b_in"], "g_res": get["L1_xattn_g_res"],
        "g_init": get["L1_xattn_g_init"], "amask": get["L1_ffn_attention_mask"],
        "posT": T(get["L1_ffn_position_ids"]), "router_w": get["L1_ffn_router_w"],
        "router_b": get["L1_ffn_router_b"], "wq": get["L1_ffn_wq"], "wk": get["L1_ffn_wk"],
        "wv": get["L1_ffn_wv"], "wo": get["L1_ffn_wo"], "w1": get["L1_ffn_w1"], "w2": get["L1_ffn_w2"],
        "ln1": get["L1_ffn_ln1"], "ln2": get["L1_ffn_ln2"], "L2_b": get["L2_xattn_b"],
        "b_w1T": T(get["L2_ffn_w1"]), "conv_wT": T(get["L2_ffn_conv_w"][:, 0, :]), "conv_b": get["L2_ffn_conv_b"],
        "b_w2T": T(get["L2_ffn_w2"]), "W_srcT": T(get["L3_xattn_W_src"]), "b_src": get["L3_xattn_b_src"],
        "W_tgtT": T(get["L3_xattn_W_tgt"]), "b_tgt": get["L3_xattn_b_tgt"], "W_outT": T(get["L3_xattn_W_out"]),
        "b_out": get["L3_xattn_b_out"], "norm1": get["L3_ffn_norm1_w"], "norm2": get["L3_ffn_norm2_w"],
        "WqT": wqT, "WqT_turned": np.ascontiguousarray(wqT[:, turned]), "WdkvT": T(get["L3_ffn_Wdkv"]),
        "WukT": wukT, "WukT_turned": np.ascontiguousarray(wukT[:, turned]), "WuvT": T(get["L3_ffn_Wuv"]),
        "WoT": T(get["L3_ffn_Wo"]), "ln_g": get["L3_ffn_ln_g"], "ln_b": get["L3_ffn_ln_b"],
        "gateT": T(get["L3_ffn_gate_w"]), "gate_b": get["L3_ffn_gate_b"],
        "W1T": T(get["L3_ffn_W1"], 0, 2, 1), "W2T": T(get["L3_ffn_W2"], 0, 2, 1),
        "b1T": T(get["L3_ffn_b1"].reshape(16, 128)), "b2T": T(get["L3_ffn_b2"]),
    }
    arrays.update(constants())
    nc = bacc.Bacc("TRN2", target_bir_lowering=False, num_devices=1)
    t_in = {n: nc.dram_tensor("in_" + n, a.shape, mybir.dt.from_np(a.dtype), kind="ExternalInput").ap()
            for n, a in arrays.items()}
    out = nc.dram_tensor("out_0", (B, S, D), F32, kind="ExternalOutput").ap()
    build(nc, t_in, out)
    got = run_bass_kernel_spmd(nc, [{"in_" + n: a for n, a in arrays.items()}], core_ids=[0])
    return got.results[0]["out_0"]
```

```python
from contextlib import ExitStack

import numpy as np

import concourse.bass as bass
from concourse import mybir

F32 = mybir.dt.float32
BF16 = mybir.dt.bfloat16
I32 = mybir.dt.int32
ALU = mybir.AluOpType
ACT = mybir.ActivationFunctionType
AX = mybir.AxisListType

B, S, D = 32, 128, 128
C = 2 * D
N_EXP0, N_HID0 = 8, 512
HID = 512
N_EXP3 = 4
LATENT = 64
TILES, PER_TILE, SLOTS = 4, 8, 16
KEPT = int(0.125 * S) - 1
RING = 4
BIG = -1.0e30
TWO_PI = 2.0 * np.pi
PI_PARTS = (6.28125, 1.93500518798828125e-3, 3.0199159795e-7)
SIN_LIMIT = 3.1415925
PATCH_GAIN = float(np.exp(-0.001))
MAGIC = 12582912.0


def steps(engine, count, work):
    last = max(lag for lag, _ in work)

    def step(items):
        for lag, stage in work:
            if lag in items:
                stage(*items[lag])
    whole_steps(engine, count, last, step)


def whole_steps(engine, count, last, step):
    first = -(-(last + RING) // RING) * RING

    def plain(t):
        step({lag: (t - lag, (t - lag) % RING) for lag in range(last + 1) if 0 <= t - lag < count})

    if count < first + RING:
        for t in range(count + last):
            plain(t)
        return
    for t in range(first):
        plain(t)
    with engine.Fori(first // RING, count // RING) as round_:
        for u in range(RING):
            step({lag: (round_ * RING + (u - lag), (u - lag) % RING) for lag in range(last + 1)})
    for t in range(count, count + last):
        plain(t)


def wait_reuse(engine, signal, item, depth, per_item=1):
    if isinstance(item, int) and item < depth:
        return
    semaphore, begun = signal
    engine.wait_ge(semaphore, item * per_item + (begun - (depth - 1) * per_item))


class Link:

    def __init__(self, engine, signal, item, per_item, held=None):
        self.held, self.engine, self.per_item, self.n = held, engine, per_item, 0
        self.sem, begun = signal
        self.base = item * per_item + begun

    def __call__(self, instruction):
        self.n += 1
        instruction.then_inc(self.sem, 1)
        self.engine.wait_ge(self.sem, self.base + self.n)
        if self.held is not None:
            self.engine.sem_inc(self.held, 1)

    def count(self, instruction):
        self.n += 1
        instruction.then_inc(self.sem, 1)
        return self

    def end(self):
        assert self.n == self.per_item, (self.n, self.per_item)


def in_turns(*chains):
    going = list(chains)
    waits = {}
    while going:
        for chain in list(going):
            if chain in waits:
                link, n = waits.pop(chain)
                link.engine.wait_ge(link.sem, link.base + n)
            link = next(chain, "end")
            if link == "end":
                going.remove(chain)
            elif link is not None:
                waits[chain] = link, link.n


class Seq:

    def __init__(self, engine, signal, counts):
        self.engine, self.sem, self.counts = engine, signal, counts

    def __call__(self, instruction):
        self.counts[self.sem] = self.counts.get(self.sem, 0) + 1
        instruction.then_inc(self.sem, 1)
        self.engine.wait_ge(self.sem, self.counts[self.sem])


def rows_of(heads):
    dh = D // heads
    return dh, (64 if dh == 8 else 128), heads // 8


def head_at(at, R):
    return at if R == 128 else at // 8 * 8 + at % 4 * 2 + at % 8 // 4


def build(nc, t_in, out):
    with ExitStack() as ctx_:
        sems = {}

        def sem(name):
            if name not in sems:
                sems[name] = ctx_.enter_context(nc.semaphore(name))
            return sems[name]

        begun = {}

        def after(name, n=0):
            return sem(name), n + begun.get(name, 0)

        def hold(engine):
            engine.sem_inc(sem("held_" + engine_name[engine]), 1)

        engine_name = {}

        def sb(name, shape, dt=F32):
            return ctx_.enter_context(nc.sbuf_tensor(name, shape, dt))

        x_all = sb("x_all", [S, B, D])
        ctx_all = sb("ctx_all", [S, B, C])
        q_all = sb("q_all", [S, B, D])
        kv_all = sb("kv_all", [S, B, C])
        ident = sb("ident", [128, 128])
        identb = sb("identb", [128, 128], BF16)
        upper = sb("upper", [128, 128])
        upperb = sb("upperb", [128, 128], BF16)
        below = sb("below", [128, 128])
        above = sb("above", [128, 128])
        ones = sb("ones", [128, 128])
        onesb = sb("onesb", [128, 128], BF16)
        iota_p = sb("iota_p", [128, 3])
        iota_row = sb("iota_row", [128, SLOTS])
        sel = sb("sel", [128, 16, 128], BF16)
        sel_col = sb("sel_col", [128, 16])
        k_scale = sb("k_scale", [128, 2, B])
        bias3 = sb("bias3", [128, 3, B, 3], BF16)
        small = sb("small", [128, 256])

        ps = ctx_.enter_context(nc.psum_tensor("ps", [128, 8, 512], F32))
        q_pad = sb("q_pad", [128, 2, 1024], BF16)
        k_pad = sb("k_pad", [128, 2, 1024], BF16)
        qT = sb("qT", [128, RING, 8, 128], BF16)
        kT = sb("kT", [128, RING, 8, 128], BF16)
        probs = sb("probs", [128, 2, 16 * 128])
        v_wide = sb("v_wide", [128, 2, 2, 648])
        pv = sb("pv", [72, 2, 256])
        row32 = sb("row32", [128, 2, 128])
        key32 = sb("key32", [128, 2, 128])
        rest = sb("rest", [128, 2, 128])
        k_rest = sb("k_rest", [128, 2, 128])
        neg_max = sb("neg_max", [128, RING, 16])
        nm_rest = sb("nm_rest", [128, 16])
        nm3 = sb("nm3", [128, RING, 128], BF16)
        nmT = sb("nmT", [128, RING, 128], BF16)
        inv_den = sb("inv_den", [128, 2, 16])
        o_sb = sb("o_sb", [128, 2, 128])
        oT = sb("oT", [128, 2, 128])
        stat = sb("stat", [128, TILES, 6])
        stats_all = sb("stats_all", [128, B, 6])
        mean_all = sb("mean_all", [128, B])
        inv_all = sb("inv_all", [128, B])
        moment = sb("moment", [128, 4, B])
        mv = sb("mv", [128, 2, 8])
        bank_b = [ps[:, i, :].bitcast(BF16) for i in range(8)]

        moments_taken = {}

        def moments_vector(dve, kind, stats=None, n=B):
            c = moments_taken["v"] = moments_taken.get("v", 0) + 1
            st = stats_all[:] if stats is None else stats
            q = Seq(dve, sem("moments_link"), moments_taken)
            mean, inv = mean_all[:, 0:n], inv_all[:, 0:n]
            half, var, root, t = (moment[:, i, 0:n] for i in range(4))
            V = nc.vector
            if kind != "direct":
                q(V.tensor_tensor(mean, st[:, :, 1], st[:, :, 4], ALU.add))
                q(V.tensor_scalar(mean, mean, 0.5, None, ALU.mult))
                q(V.tensor_tensor(half, st[:, :, 1], mean, ALU.subtract))
                q(V.tensor_tensor(half, half, half, ALU.mult))
                q(V.tensor_tensor(var, st[:, :, 2], st[:, :, 5], ALU.add))
                q(V.scalar_tensor_tensor(var, var, 1.0 / D, half, ALU.mult, ALU.add))
            if kind == "ln":
                q(V.tensor_scalar(var, var, 1e-5, None, ALU.add))
            elif kind == "ln_rms":
                q(V.tensor_scalar(var, var, 1.0 + 1e-5, 1e-10, ALU.mult, ALU.add))
            elif kind == "ln_rms6":
                q(V.tensor_scalar(var, var, 1.0 + 1e-6, 1e-11, ALU.mult, ALU.add))
            elif kind == "rms":
                q(V.tensor_tensor(half, mean, mean, ALU.mult))
                q(V.tensor_tensor(var, var, half, ALU.add))
                q(V.tensor_scalar(var, var, 1e-6, None, ALU.add))
            else:
                q(V.tensor_scalar(var, var, 1.0 / C, 1e-5, ALU.mult, ALU.add))
            dve.sem_inc(sem("variance"), 1)
            dve.wait_ge(sem("deviation"), c)
            q(V.reciprocal(inv, root))
            q(V.tensor_tensor(t, inv, inv, ALU.mult))
            q(V.tensor_tensor(t, t, var, ALU.mult))
            q(V.tensor_scalar(t, t, -0.5, 1.5, ALU.mult, ALU.add))
            q(V.tensor_tensor(inv, inv, t, ALU.mult))

        def moments_scalar(act, n=B):
            c = moments_taken["s"] = moments_taken.get("s", 0) + 1
            act.wait_ge(sem("variance"), c)
            nc.scalar.activation(moment[:, 2, 0:n], moment[:, 1, 0:n], ACT.Sqrt).then_inc(sem("deviation"), 1)

        def norm(dst, b, k=None):
            return nc.vector.tensor_scalar(dst, x_all[:, b, :], mean_all[:, bass.ts(b, 1)], inv_all[:, bass.ts(b, 1)],
                                           ALU.subtract, ALU.mult)

        def measure(dve, updated, b, rows=x_all):
            dve.wait_ge(updated[0], updated[1] + b + 1)
            nc.vector.bn_stats(stats_all[:, b, :], rows[:, b, :]).then_inc(sem("measured"), 1)

        def attention_counts(count, heads, raw, post):
            NU = rows_of(heads)[2]
            once = ("q_padded", "k_padded", "v_ready", "q_turned", "k_turned", "qT_ready", "kT_ready", "nm_split",
                    "nm_turned", "nmT_ready", "weighted", "o_ready")
            counts = {n: count for n in once + (("k_scaled",) if raw else ())
                      + (("o_turned", "oT_ready", "projected", "x_updated") if post else ())
                      + ("pv_ready", "pv_turned")}
            counts.update({n: count * NU for n in ("raw_scores", "max_taken", "scores", "probs_ready")})
            counts.update(q_link=count * (4 if raw else 3), k_link=count * 5, nm_link=count * 3,
                          o_link=count * (1 if post else 2))
            return counts

        def attention_vector(dve, L, count, heads, normalise, post):
            dh, R, NU = rows_of(heads)

            def split_q(b, k):
                link = Link(dve, after("q_link"), b, 4 if normalise else 3)
                if normalise:
                    yield link.count(norm(row32[:, k % 2, :], b))
                    src = row32[:, k % 2, :]
                else:
                    src = q_all[:, b, :]
                src = src.rearrange("p (h d) -> p h d", h=heads)
                pad = q_pad[:, k % 2, :].rearrange("p (h r) -> p h r", h=heads)
                left = rest[:, k % 2, :].rearrange("p (h d) -> p h d", h=heads)

                def groups(a, n):
                    return pad[:, :, a * dh:(a + n) * dh].rearrange("p h (n d) -> p h n d", n=n)

                wait_reuse(dve, after("q_turned"), b, 2)
                yield link.count(nc.vector.tensor_copy(groups(0, 3), src.unsqueeze(2).broadcast_to([128, heads, 3, dh])))
                yield link.count(nc.vector.tensor_tensor(left, src, pad[:, :, 0:dh], ALU.subtract))
                yield link.count(nc.vector.tensor_copy(groups(3, 2), left.unsqueeze(2).broadcast_to([128, heads, 2, dh])))
                nc.vector.tensor_tensor(pad[:, :, 5 * dh:6 * dh], left, pad[:, :, 3 * dh:4 * dh],
                                        ALU.subtract).then_inc(sem("q_padded"), 1)
                link.end()

            def take_qT(b, k):
                dve.wait_ge(*after("q_turned", b + 1))
                wait_reuse(dve, after("scores"), b, RING, NU)
                nc.vector.tensor_copy(qT[:, k, :, :], bank_b[0].rearrange("p (j q) -> p j q", j=8)).then_inc(sem("qT_ready"), 1)

            def take_max(b, k, u):
                dve.wait_ge(*after("raw_scores", b * NU + (u + 1)))
                nc.vector.tensor_reduce(neg_max[:, k, 8 * u:8 * u + 8],
                                        ps[:, 2 + 2 * u:4 + 2 * u, :].rearrange("p a (h k) -> p (a h) k", h=4),
                                        AX.X, ALU.max, negate=True).then_inc(sem("max_taken"), 1)

            def split_max(b, k):
                link = Link(dve, after("nm_link"), b, 3)
                nm = neg_max[:, k, 0:heads]
                copies = 128 // R
                spots = nm3[:, k, :].rearrange("p (r n) -> p r n", r=2)[:, 0:copies, 0:3 * heads].rearrange(
                    "p r (h c) -> p r h c", c=3)
                full = [128, copies, heads]
                left = nm_rest[:, 0:heads]

                def wide(v):
                    return v.unsqueeze(1).broadcast_to(full)
                dve.wait_ge(*after("max_taken", b * NU + NU))
                wait_reuse(dve, after("nm_turned"), b, RING)
                yield link.count(nc.vector.tensor_copy(spots[:, :, :, 0], wide(nm)))
                yield link.count(nc.vector.tensor_tensor(left, nm, spots[:, 0, :, 0], ALU.subtract))
                yield link.count(nc.vector.tensor_copy(spots[:, :, :, 1], wide(left)))
                nc.vector.tensor_tensor(spots[:, :, :, 2], wide(left), spots[:, :, :, 1],
                                        ALU.subtract).then_inc(sem("nm_split"), 1)
                link.end()

            def take_nmT(b, k):
                dve.wait_ge(*after("nm_turned", b + 1))
                wait_reuse(dve, after("scores"), b, RING, NU)
                nc.vector.tensor_copy(nmT[:, k, :], bank_b[6][:, 0:128]).then_inc(sem("nmT_ready"), 1)

            def take_o(b, k):
                link = Link(dve, after("o_link"), b, 1 if post else 2)
                got = ps[:, 6, 64:64 + heads * (dh + 1)].rearrange("p (h d) -> p h d", h=heads)
                o = o_sb[:, k % 2, :].rearrange("p (h d) -> p h d", h=heads)
                dve.wait_ge(*after("pv_turned", b + 1))
                yield link.count(nc.vector.reciprocal(inv_den[:, k % 2, 0:heads], got[:, :, dh]))
                inv = inv_den[:, k % 2, 0:heads].unsqueeze(2).broadcast_to([128, heads, dh])
                if post:
                    wait_reuse(dve, after("o_turned"), b, 2)
                    nc.vector.tensor_tensor(o, got[:, :, 0:dh], inv, ALU.mult).then_inc(sem("o_ready"), 1)
                else:
                    yield link.count(nc.vector.tensor_tensor(o, got[:, :, 0:dh], inv, ALU.mult))
                    nc.vector.tensor_tensor(x_all[:, b, :], x_all[:, b, :], o_sb[:, k % 2, :],
                                            ALU.add).then_inc(sem("o_ready"), 1)
                link.end()

            def take_oT(b, k):
                dve.wait_ge(*after("o_turned", b + 1))
                dve.wait_ge(*after("nm_turned", b + 4 if not isinstance(b, int) else min(b + 4, count)))
                nc.vector.tensor_copy(oT[:, k % 2, :], ps[:, 6, 256:384]).then_inc(sem("oT_ready"), 1)

            def add_post(b, k):
                dve.wait_ge(*after("projected", b + 1))
                for name, ahead in (("o_turned", 2), ("nm_turned", 5)):
                    dve.wait_ge(*after(name, b + ahead if not isinstance(b, int) else min(b + ahead, count)))
                stream = {"L1": x1_tiles, "L3": x_all, "L4": z_all}[L]
                dst = stream[:, b, :]
                nc.vector.tensor_tensor(dst, dst, ps[:, 6, 384:512], ALU.add).then_inc(sem("x_updated"), 1)
                if count == B:
                    measure(dve, after("x_updated"), b, stream)
                else:
                    dve.wait_ge(*after("x_updated", b + 1))
                    nc.vector.bn_stats(stat[:, b, :], x1_tiles[:, b, :]).then_inc(sem("tile_measured"), 1)

            def update(b, k):
                measure(dve, after("o_ready"), b)

            def step(items):
                def have(lag):
                    return lag in items
                if have(3):
                    take_nmT(*items[3])
                if post and have(6):
                    take_oT(*items[6])
                if post and have(7):
                    add_post(*items[7])
                if have(2):
                    take_max(*items[2], 0)
                if have(0):
                    in_turns(split_q(*items[0]))
                if have(2) and NU == 2:
                    take_max(*items[2], 1)
                in_turns(*([split_max(*items[2])] if have(2) else []), *([take_o(*items[5])] if have(5) else []))
                if have(1):
                    take_qT(*items[1])
                if not post and have(5):
                    update(*items[5])
            whole_steps(dve, count, 7 if post else 5, step)

        def attention_gpsimd(pool, L, count, heads, raw):
            dh, R, NU = rows_of(heads)

            def split_k(b, k):
                link = Link(pool, after("k_link"), b, 5, sem("held_gpsimd"))
                if raw:
                    pool.wait_ge(*after("k_scaled", b + 1))
                    src = key32[:, k % 2, :]
                else:
                    src = kv_all[:, b, 0:D]
                src = src.rearrange("p (h d) -> p h d", h=heads)
                pad = k_pad[:, k % 2, :].rearrange("p (h r) -> p h r", h=heads)
                left = k_rest[:, k % 2, :].rearrange("p (h d) -> p h d", h=heads)
                wait_reuse(pool, after("k_turned"), b, 2)
                hold(pool)
                link(nc.gpsimd.tensor_copy(pad[:, :, 0:dh], src))
                link(nc.gpsimd.tensor_tensor(left, src, pad[:, :, 0:dh], ALU.subtract))
                link(nc.gpsimd.tensor_copy(pad[:, :, dh:2 * dh], left))
                link(nc.gpsimd.tensor_tensor(pad[:, :, 2 * dh:3 * dh], left, pad[:, :, dh:2 * dh], ALU.subtract))
                if L in ("L0", "L2", "L3"):
                    which = ("L0", "L2", "L3").index(L)
                    nc.gpsimd.tensor_copy(pad[:, :, 6 * dh:6 * dh + 3],
                                          bias3[:, which, b, :].unsqueeze(1).broadcast_to([128, heads, 3]))
                link(nc.gpsimd.tensor_copy(pad[:, :, 3 * dh:5 * dh], pad[:, :, 0:2 * dh]))
                nc.gpsimd.tensor_copy(pad[:, :, 5 * dh:6 * dh], pad[:, :, 0:dh]).then_inc(sem("k_padded"), 1)
                link.end()

            def copy_v(b, k):
                src = ctx_all[:, b, D:C] if raw else kv_all[:, b, D:C]
                wait_reuse(pool, after("weighted"), b, 2)
                hold(pool)
                each, G = dh + 1, heads // 2
                dst = v_wide[:, k % 2, :, 0:G * (G + 1) * each].rearrange("p g (h n) -> p g h n", h=G)[:, :, :, 0:dh]
                nc.gpsimd.tensor_copy(dst, src.rearrange("p (g h d) -> p g h d", g=2, h=G)).then_inc(sem("v_ready"), 1)

            steps(pool, count, [(0, split_k), (3, copy_v)])

        def attention_scalar(act, L, count, heads, raw, post):
            dh, R, NU = rows_of(heads)

            def scale_k(b, k):
                wait_reuse(act, after("k_padded"), b, 2)
                nc.scalar.activation(key32[:, k % 2, :], ctx_all[:, b, 0:D], ACT.Copy,
                                     scale=k_scale[:, 0 if L == "L0" else 1, bass.ts(b, 1)]).then_inc(sem("k_scaled"), 1)

            def take_kT(b, k):
                act.wait_ge(*after("k_turned", b + 1))
                wait_reuse(act, after("scores"), b, RING, NU)
                nc.scalar.activation(kT[:, k, :, :], bank_b[1].rearrange("p (j q) -> p j q", j=8),
                                     ACT.Copy).then_inc(sem("kT_ready"), 1)

            def exps(b, k, u):
                slot = u if NU == 2 else 1
                act.wait_ge(*after("scores", b * NU + (u + 1)))
                wait_reuse(act, after("weighted"), b, 2)
                nc.scalar.activation(probs[:, k % 2, 1024 * u:1024 * u + 1024],
                                     ps[:, 2 + 2 * slot:4 + 2 * slot, :].rearrange("p a n -> p (a n)"),
                                     ACT.Exp).then_inc(sem("probs_ready"), 1)

            def take_pv(b, k):
                act.wait_ge(*after("weighted", b + 1))
                wait_reuse(act, after("pv_turned"), b, 2)
                W = heads // 2 * (dh + 1)
                nc.scalar.activation(pv[0:W, k % 2, :], ps[0:W, 7, 0:256], ACT.Copy).then_inc(sem("pv_ready"), 1)

            work = [(0, scale_k)] if raw else []
            work += [(4, take_pv)]
            if NU == 2:
                work += [(3, lambda b, k: exps(b, k, 0)), (1, take_kT), (3, lambda b, k: exps(b, k, 1))]
            else:
                work += [(1, take_kT), (3, lambda b, k: exps(b, k, 0))]
            steps(act, count, work)

        def attention_tensor(pe, L, count, heads, mask_parts, mask, post_w):
            dh, R, NU = rows_of(heads)
            per = 128 // R

            def turn(b, k):
                pe.wait_ge(*after("q_padded", b + 1))
                wait_reuse(pe, after("qT_ready"), b, 1)
                for j in range(8):
                    last = nc.tensor.transpose(bank_b[0][:, 128 * j:128 * j + 128],
                                               q_pad[:, k % 2, 128 * j:128 * j + 128], identb[:])
                last.then_inc(sem("q_turned"), 1)
                pe.wait_ge(*after("k_padded", b + 1))
                wait_reuse(pe, after("kT_ready"), b, 1)
                for j in range(8):
                    last = nc.tensor.transpose(bank_b[1][:, 128 * j:128 * j + 128],
                                               k_pad[:, k % 2, 128 * j:128 * j + 128], identb[:])
                last.then_inc(sem("k_turned"), 1)

            def tile_of(buf, k, h, n):
                base = R * (h % per)
                return buf[base:base + n, k, h // per, :]

            def product(u, slot, k, left, right, turned):
                n = 6 * dh + 3
                for a in range(2):
                    bank = ps[:, 2 + 2 * slot + a, :]
                    for part in range(mask_parts):
                        m = mask(u, k, part)
                        four = [128, 4, 128]
                        if turned:
                            nc.tensor.matmul(bank, m, identb[:].unsqueeze(1).broadcast_to(four),
                                             start=part == 0, stop=False, skip_group_check=True)
                        else:
                            nc.tensor.matmul(bank, identb[:], m.unsqueeze(1).broadcast_to(four),
                                             start=part == 0, stop=False, skip_group_check=True)
                    for i in range(4):
                        h = head_at(8 * u + 4 * a + i, R)
                        base = R * (h % per)
                        dst = bank[:, 128 * i:128 * i + 128]
                        last = nc.tensor.matmul(dst, tile_of(left, k, h, n), tile_of(right, k, h, n),
                                                start=mask_parts == 0, stop=not turned, skip_group_check=True)
                        if turned:
                            last = nc.tensor.matmul(dst, sel[base:base + R, 8 * u + 4 * a + i, :], nmT[base:base + R, k, :],
                                                    start=False, stop=True, skip_group_check=True)
                return last

            def raw_scores(b, k, u):
                slot = u if NU == 2 else 0
                if u == 0:
                    pe.wait_ge(*after("qT_ready", b + 1))
                    pe.wait_ge(*after("kT_ready", b + 1))
                if NU == 2:
                    if not isinstance(b, int) or b >= 2:
                        pe.wait_ge(*after("probs_ready", b * NU + (u + 1 - 2 * NU)))
                    elif b == 1:
                        pe.wait_ge(*after("max_taken", u + 1))
                else:
                    wait_reuse(pe, after("max_taken"), b, 1)
                product(u, slot, k, qT, kT, False).then_inc(sem("raw_scores"), 1)

            def scores(b, k, u):
                slot = u if NU == 2 else 1
                if u == 0:
                    pe.wait_ge(*after("nmT_ready", b + 1))
                if NU == 2:
                    if isinstance(b, int) and b == count - 1:
                        pe.wait_ge(*after("max_taken", b * NU + (u + 1)))
                    else:
                        pe.wait_ge(*after("max_taken", b * NU + (NU + u + 1)))
                else:
                    wait_reuse(pe, after("probs_ready"), b, 1)
                product(u, slot, k, kT, qT, True).then_inc(sem("scores"), 1)

            def bank_free(b, lag, reads):
                for name, its in reads:
                    n = b + (lag - its)
                    if isinstance(n, int):
                        n = min(n, count)
                        if n <= 0:
                            continue
                    pe.wait_ge(*after(name, n))

            reads = [("nmT_ready", 3), ("o_ready", 5)]
            if post_w is not None:
                reads += [("oT_ready", 6), ("x_updated", 7)]

            def turn_max(b, k):
                pe.wait_ge(*after("nm_split", b + 1))
                bank_free(b, 3, reads)
                hold(pe)
                nc.tensor.transpose(bank_b[6][:, 0:128], nm3[:, k, :],
                                    identb[:]).then_inc(sem("nm_turned"), 1)

            def turn_o(b, k):
                bank_free(b, 6, reads)
                hold(pe)
                nc.tensor.transpose(ps[:, 6, 256:384], o_sb[:, k % 2, :], ident[:]).then_inc(sem("o_turned"), 1)

            def project(b, k):
                bank_free(b, 7, reads)
                nc.tensor.matmul(ps[:, 6, 384:512], oT[:, k % 2, :], post_w, start=True,
                                 stop=True).then_inc(sem("projected"), 1)

            G, W = heads // 2, heads // 2 * (dh + 1)

            def weighted(b, k, half):
                if half == 0:
                    pe.wait_ge(*after("v_ready", b + 1))
                    wait_reuse(pe, after("pv_ready"), b, 1)
                if NU == 2 or half == 0:
                    pe.wait_ge(*after("probs_ready", b * NU + (half + 1)))
                where = {head_at(at, R): at for at in range(heads)}
                for j in range(G):
                    at = where[half * G + j]
                    last = nc.tensor.matmul(ps[0:W, 7, 128 * half:128 * half + 128],
                                            v_wide[:, k % 2, half, W * j:W * j + W],
                                            probs[:, k % 2, 128 * at:128 * at + 128], start=j == 0, stop=j == G - 1)
                if half:
                    last.then_inc(sem("weighted"), 1)

            def turn_pv(b, k):
                pe.wait_ge(*after("pv_ready", b + 1))
                bank_free(b, 6, reads[:1] + reads[2:])
                wait_reuse(pe, after("o_ready"), b, 1)
                hold(pe)
                for half in range(2):
                    last = nc.tensor.transpose(ps[:, 6, 64 + W * half:64 + W * half + W],
                                               pv[0:W, k % 2, 128 * half:128 * half + 128], ident[0:W, 0:W])
                last.then_inc(sem("pv_turned"), 1)

            work = [(7, project), (6, turn_o)] if post_w is not None else []
            work += [(3, turn_max), (2, lambda b, k: raw_scores(b, k, 0)), (5, turn_pv),
                     (4, lambda b, k: weighted(b, k, 0))]
            if NU == 2:
                work += [(2, lambda b, k: raw_scores(b, k, 1))]
            work += [(4, lambda b, k: weighted(b, k, 1))]
            if NU == 2:
                work += [(3, lambda b, k: scores(b, k, 0)), (1, turn), (3, lambda b, k: scores(b, k, 1))]
            else:
                work += [(1, turn), (3, lambda b, k: scores(b, k, 0))]
            steps(pe, count, work)

        wc = sb("wc", [128, 128])
        wg = sb("wg", [128, 128])
        toep = sb("toep", [128, 128])
        lens_f = sb("lens_f", [128, B])
        q_room = qT[:].rearrange("p k j t -> p (k j t)").bitcast(F32)
        lens_rep, hot, spread, patch = (q_room[:, 256 * i:256 * i + 256].rearrange("p (k t) -> p k t", k=2)
                                        for i in range(4))
        bound = sb("bound", [128, 2, 2])
        bound_rep = sb("bound_rep", [128, 2, 128], BF16)
        g_init = sb("g_init", [128, D])
        bias_rows = sb("bias_rows", [3, 1152], BF16)
        cols = sb("cols", [128, 16])
        COL = {n: i for i, n in enumerate(("g_res", "router_w", "ln1", "ln2", "norm1", "norm2", "ln_g", "ln_b",
                                           "router_b", "L0_b", "L2_b"))}

        def col(name, n=128):
            return cols[0:n, COL[name]:COL[name] + 1]

        ctx_inv = sb("ctx_inv", [128, B])
        rowT = sb("rowT", [128, 2, 128])
        junk = sb("junk", [128, 256])
        wb = sb("wb", [128, 2, 128])
        rank = sb("rank", [128, 2, 4])
        ranks = sb("ranks", [128, 3, B])
        route_tmp = probs[:, :, 0:512]
        picked = sb("picked", [128, B])
        keep = sb("keep", [128, B])
        wcol = sb("wcol", [128, B])
        place = sb("place", [128, B])
        pick = sb("pick", [128, B, SLOTS])
        rw_rep = sb("rw_rep", [128, 128])
        x1_tiles = sb("x1_tiles", [128, TILES, 128])
        x1_T = probs[:, 1, 1024:1536].rearrange("p (t s) -> p t s", t=TILES)
        aux = q_room[:, 512:512 + 9 * B].rearrange("p (b n) -> p b n", b=B)
        auxT = q_room[0:9, 0:512].rearrange("p (t s) -> p t s", t=TILES)
        aux_t = sb("aux_t", [128, TILES, 9])
        cls_mask = sb("cls_mask", [128, 4, 128])
        mg = probs[:, 1, 1536:2048].rearrange("p (t s) -> p t s", t=TILES)
        mask3 = kv_all[:, 8:11, :].rearrange("p a b -> p (a b)").bitcast(BF16).rearrange("p (t c k) -> p t c k", t=TILES, c=3)
        outside = sb("outside", [128, 128])
        own = sb("own", [128, PER_TILE])
        freq = sb("freq", [128, 4])
        pos_f = sb("pos_f", [128, 4])
        w_qkv = sb("w_qkv", [128, 384])
        w_o1 = sb("w_o1", [128, 128])
        w1_l1 = sb("w1_l1", [128, 512])
        w2_l1 = sb("w2_l1", [128, 4, 128])
        tap_w = sb("tap_w", [128, 3, 512])
        w2_q = sb("w2_q", [128, 4, 128], BF16)
        inv_w = sb("inv_w", [128, 4])
        xqT = sb("xqT", [128, 2, 130])
        q2 = q_pad[:, :, 0:512]
        q2T = k_pad[:, :, 0:512].rearrange("p k (c t) -> p k c t", c=4)
        w_src = sb("w_src", [128, 2, 256])
        w_tgt = sb("w_tgt", [128, 256])
        w_out2 = sb("w_out2", [128, 128])
        mask_f = sb("mask_f", [128, B])
        mask_q = sb("mask_q", [128, B])
        causal = sb("causal", [128, 128], BF16)
        rope = sb("rope", [128, 4, 128])
        w_h1 = sb("w_h1", [128, 320])
        w_h2 = sb("w_h2", [64, 384])
        w_o3 = sb("w_o3", [128, 128])
        gate_w = sb("gate_w", [128, N_EXP3])
        gate_b = sb("gate_b", [128, N_EXP3])
        first_row = sb("first_row", [128, N_EXP3])
        b1_col = sb("b1_col", [128, 16])
        b2_col = sb("b2_col", [128, N_EXP3])

        rowT2 = sb("rowT2", [128, 128])
        scale2 = sb("scale2", [128, RING])
        w_part = q_pad[:].rearrange("p k r -> p (k r)")[:, 0:1152]

        z_all = ctx_all[:, 16:32, :].rearrange("p a b -> p (a b)").rearrange("p (b d) -> p b d", b=B)
        inv_ln = ctx_inv

        phase_no = {}

        def phase_end(engine):
            n = phase_no.get(engine, 0) + 1
            phase_no[engine] = n
            engine.drain().then_inc(sem("phase_done"), 1)
            engine.wait_ge(sem("phase_done"), 5 * n)

        def turn_rows(pe):
            def stage(b, k):
                pe.wait_ge(*after("normed", b + 1))
                wait_reuse(pe, after("rowT"), b, 2)
                hold(pe)
                nc.tensor.transpose(ps[:, k % 2, 0:128], row32[:, k % 2, :], ident[:]).then_inc(sem("turned"), 1)
            return stage

        def take_rows(act, scale=1.0, dst=None):
            def stage(b, k):
                act.wait_ge(*after("turned", b + 1))
                wait_reuse(act, after("used"), b, 2)
                to = rowT[:, k % 2, :] if dst is None else dst(k)
                nc.scalar.activation(to, ps[:, k % 2, 0:128], ACT.Copy, scale=scale).then_inc(sem("rowT"), 1)
            return stage

        def ffn0_prep_tensor(pe):
            pe.wait_ge(sem("l0_weights"), 32)
            for c in range(32):
                last = nc.tensor.matmul(ps[:, 7, 256:384], kv_all[:, c, 0:128], kv_all[:, c, 128:256],
                                        start=c == 0, stop=c == 31)
            last.then_inc(sem("wc_ready"), 1)

        def ffn0_prep_vector(dve):
            dve.wait_ge(sem("wc_ready"), 1)
            nc.vector.tensor_copy(wc[:], ps[:, 7, 256:384]).then_inc(sem("wc_taken"), 1)
            dve.wait_ge(sem("wc_taken"), 1)

        def ffn0_vector(dve):
            def norm_b(b, k):
                wait_reuse(dve, after("turned"), b, 2)
                norm(row32[:, k % 2, :], b).then_inc(sem("normed"), 1)

            def add(b, k):
                dve.wait_ge(*after("used", b + 1))
                nc.vector.tensor_tensor(x_all[:, b, :], x_all[:, b, :], ps[:, 2 + k % 2, 0:128],
                                        ALU.add).then_inc(sem("added"), 1)
                measure(dve, after("added"), b)
            steps(dve, B, [(0, norm_b), (3, add)])

        def ffn0_scalar(act):
            steps(act, B, [(1, take_rows(act))])

        def ffn0_tensor(pe):
            def multiply(b, k):
                pe.wait_ge(*after("rowT", b + 1))
                wait_reuse(pe, after("added"), b, 2)
                nc.tensor.matmul(ps[:, 2 + k % 2, 0:128], rowT[:, k % 2, :], wc[:], start=True,
                                 stop=True).then_inc(sem("used"), 1)
            steps(pe, B, [(1, turn_rows(pe)), (2, multiply)])

        def depool_vector(dve):
            def norm_b(b, k):
                wait_reuse(dve, after("turned"), b, 2)
                norm(row32[:, k % 2, :], b).then_inc(sem("normed"), 1)
                wait_reuse(dve, after("used"), b, 2)
                nc.vector.scalar_tensor_tensor(patch[:, k % 2, :], ctx_all[:, b, 0:D], ctx_inv[:, bass.ts(b, 1)],
                                               g_init[:], ALU.mult, ALU.mult).then_inc(sem("dp_patch"), 1)

            def find(b, k):
                dve.wait_ge(sem("dp_ends"), b + 1)
                link = Link(dve, after("link2"), b, 2)
                nc.vector.tensor_scalar(junk[:, 0:128], ps[:, 4, 0:128], iota_p[:, 1:2], 0.0, ALU.is_equal, ALU.max,
                                        accum_out=bound[:, k % 2, 0:1]).then_inc(sem("dp_bound_a"), 1)
                yield link.count(nc.vector.tensor_scalar(junk[:, 128:256], ps[:, 4, 0:128], iota_p[:, 2:3], 0.0, ALU.is_equal,
                                             ALU.max, accum_out=bound[:, k % 2, 1:2]))
                dve.wait_ge(sem("dp_bound_a"), b + 1)
                yield link.count(nc.vector.tensor_tensor(bound[:, k % 2, 0:1], bound[:, k % 2, 0:1], bound[:, k % 2, 1:2], ALU.max))
                wait_reuse(dve, after("dp_counts"), b, 2)
                nc.vector.tensor_scalar(bound_rep[:, k % 2, :], ones[:], bound[:, k % 2, 0:1], None,
                                        ALU.mult).then_inc(sem("dp_bound"), 1)
                link.end()

            def choose(b, k):
                dve.wait_ge(sem("dp_counts"), b + 1)
                wait_reuse(dve, after("dp_matrix"), b, 2)
                link = Link(dve, after("link3"), b, 1)
                yield link.count(nc.vector.tensor_scalar(hot[:, k % 2, :], ps[:, 5, 0:128], 1.0, 0.0, ALU.subtract, ALU.max))
                nc.vector.tensor_scalar(hot[:, k % 2, :], hot[:, k % 2, :], float(S - 1), iota_p[:, 0:1],
                                        ALU.min, ALU.is_equal).then_inc(sem("dp_hot"), 1)
                link.end()

            def add(b, k):
                dve.wait_ge(*after("used", b + 1))
                nc.vector.tensor_tensor(x_all[:, b, :], x_all[:, b, :], ps[:, 2 + k % 2, 0:128],
                                        ALU.add).then_inc(sem("added"), 1)
                measure(dve, after("added"), b)

            def step(items):
                in_turns(*([find(*items[1])] if 1 in items else []), *([choose(*items[3])] if 3 in items else []))
                if 3 in items:
                    norm_b(*items[3])
                if 6 in items:
                    add(*items[6])
            whole_steps(dve, B, 6, step)

        def depool_scalar(act):
            def spread_lens(b, k):
                wait_reuse(act, after("dp_ends"), b, 2)
                nc.scalar.activation(lens_rep[:, k % 2, :], ones[:], ACT.Copy,
                                     scale=lens_f[:, bass.ts(b, 1)]).then_inc(sem("dp_lens"), 1)

            def take_matrix(b, k):
                act.wait_ge(sem("dp_matrix"), b + 1)
                wait_reuse(act, after("used"), b, 2)
                nc.scalar.activation(spread[:, k % 2, :], ps[:, 6, 0:128], ACT.Copy).then_inc(sem("dp_spread"), 1)

            steps(act, B, [(0, spread_lens), (4, take_matrix), (4, take_rows(act))])

        def depool_tensor(pe):
            def ends(b, k):
                pe.wait_ge(sem("dp_lens"), b + 1)
                wait_reuse(pe, after("dp_bound"), b, 1)
                nc.tensor.matmul(ps[:, 4, 0:128], lens_rep[:, k % 2, :], upper[:], start=True,
                                 stop=True).then_inc(sem("dp_ends"), 1)

            def counts(b, k):
                pe.wait_ge(sem("dp_bound"), b + 1)
                wait_reuse(pe, after("dp_hot"), b, 1)
                nc.tensor.matmul(ps[:, 5, 0:128], bound_rep[:, k % 2, :], upperb[:], start=True,
                                 stop=True).then_inc(sem("dp_counts"), 1)

            def matrix(b, k):
                pe.wait_ge(sem("dp_hot"), b + 1)
                wait_reuse(pe, after("dp_spread"), b, 1)
                nc.tensor.matmul(ps[:, 6, 0:128], toep[:], hot[:, k % 2, :], start=True,
                                 stop=True).then_inc(sem("dp_matrix"), 1)

            def total(b, k):
                pe.wait_ge(*after("rowT", b + 1))
                pe.wait_ge(sem("dp_spread"), b + 1)
                pe.wait_ge(sem("dp_patch"), b + 1)
                wait_reuse(pe, after("added"), b, 2)
                dst = ps[:, 2 + k % 2, 0:128]
                nc.tensor.matmul(dst, rowT[:, k % 2, :], wg[:], start=True, stop=False)
                nc.tensor.matmul(dst, onesb[0:3, :], bias_rows[:, 0:128], start=False, stop=False)
                nc.tensor.matmul(dst, spread[:, k % 2, :], patch[:, k % 2, :], start=False,
                                 stop=True).then_inc(sem("used"), 1)

            steps(pe, B, [(4, matrix), (4, turn_rows(pe)), (5, total), (2, counts), (0, ends)])

        xd_all = q_all

        def route_vector(dve):
            def norm_b(b, k):
                wait_reuse(dve, after("turned"), b, 2)
                norm(row32[:, k % 2, :], b).then_inc(sem("normed"), 1)
                norm(xd_all[:, b, :], b).then_inc(sem("rt_kept"), 1)

            def rank_tokens(b, k):
                dve.wait_ge(sem("rt_wb"), b + 1)
                w, tmp = wb[:, k % 2, :], route_tmp[:, k % 2, :]
                own_w = wcol[:, bass.ts(b, 1)]
                V = nc.vector
                V.scalar_tensor_tensor(tmp[:, 0:128], w, 1.0, ident[:], ALU.mult, ALU.mult,
                                       accum_out=own_w).then_inc(sem("rt_wcol"), 1)
                yield
                dve.wait_ge(sem("rt_wcol"), b + 1)
                V.scalar_tensor_tensor(tmp[:, 128:256], w, own_w, below[:], ALU.is_ge, ALU.mult,
                                       accum_out=ranks[:, 0, bass.ts(b, 1)]).then_inc(sem("rt_ranked"), 1)
                V.scalar_tensor_tensor(tmp[:, 256:384], w, own_w, above[:], ALU.is_gt, ALU.mult,
                                       accum_out=ranks[:, 1, bass.ts(b, 1)]).then_inc(sem("rt_ranked"), 1)
                V.tensor_scalar(tmp[:, 384:512], w, own_w, 0.0, ALU.is_ge, ALU.add,
                                accum_out=ranks[:, 2, bass.ts(b, 1)]).then_inc(sem("rt_done"), 1)

            def step(items):
                rank_it = rank_tokens(*items[3]) if 3 in items else iter(())
                next(rank_it, None)
                if 0 in items:
                    norm_b(*items[0])
                next(rank_it, None)
            whole_steps(dve, B, 3, step)
            dve.wait_ge(sem("rt_done"), B)
            dve.wait_ge(sem("rt_ranked"), 2 * B)
            q = Seq(dve, sem("rt_seq"), moments_taken)
            q(nc.vector.tensor_tensor(picked[:], ranks[:, 0, :], ranks[:, 1, :], ALU.add))
            q(nc.vector.tensor_scalar(picked[:], picked[:], KEPT - 0.5, None, ALU.is_lt))
            q(nc.vector.tensor_scalar(keep[:], ranks[:, 2, :], KEPT + 0.5, None, ALU.is_gt))

        def route_scalar(act):
            def take_w(b, k):
                act.wait_ge(*after("used", b + 1))
                wait_reuse(act, after("rt_done"), b, 2)
                nc.scalar.activation(wb[:, k % 2, :], ps[:, 2 + k % 2, 0:128], ACT.Identity,
                                     bias=col("router_b")).then_inc(sem("rt_wb"), 1)
            steps(act, B, [(1, take_rows(act)), (2, take_w)])

        def route_tensor(pe):
            def weigh(b, k):
                pe.wait_ge(*after("rowT", b + 1))
                wait_reuse(pe, after("rt_wb"), b, 2)
                nc.tensor.matmul(ps[:, 2 + k % 2, 0:128], rw_rep[:], rowT[:, k % 2, :], start=True,
                                 stop=True).then_inc(sem("used"), 1)
            steps(pe, B, [(1, turn_rows(pe)), (2, weigh)])

        qD, kvD = q_all, kv_all

        def gather_tensor(pe):
            pe.wait_ge(sem("ga_picked"), 1)
            nc.tensor.matmul(ps[:, 7, 0:B], above[:], picked[:], start=True, stop=True).then_inc(sem("ga_place"), 1)
            pe.wait_ge(sem("ga_pick"), 1)
            for T in range(TILES):
                for j in range(PER_TILE):
                    b = T * PER_TILE + j
                    spot = slice(128 * T + SLOTS * j, 128 * T + SLOTS * (j + 1))
                    nc.tensor.matmul(ps[:, 0, spot], xd_all[:, b, :], pick[:, b, :], start=True, stop=True)
                    nc.tensor.matmul(ps[0:9, 1, spot], aux[:, b, :], pick[:, b, :], start=True, stop=True)
                    if b < 3:
                        nc.tensor.matmul(ps[:, 2, spot], cls_mask[:, b, :], pick[:, b, :], start=True, stop=True)
                lo = max(T * PER_TILE, 3)
                last = nc.tensor.matmul(ps[:, 2, SLOTS * lo:128 * T + 128], cls_mask[:, 3, :],
                                        pick[:, lo:(T + 1) * PER_TILE, :], start=True, stop=True)
            last.then_inc(sem("ga_gathered"), 1)
            pe.wait_ge(sem("ga_taken"), 3)
            for T in range(TILES):
                nc.tensor.matmul(ps[:, 3, 128 * T:128 * T + 128], mg[:, T, :],
                                 pick[:, T * PER_TILE:(T + 1) * PER_TILE, :], start=True, stop=True)
                nc.tensor.transpose(ps[:, 4, 128 * T:128 * T + 128], x1_T[:, T, :], ident[:])
                last = nc.tensor.transpose(ps[:, 5, 16 * T:16 * T + 9], auxT[:, T, :], ident[0:9, 0:9])
            last.then_inc(sem("ga_rows"), 1)
            for T in range(TILES):
                pe.wait_ge(sem("ga_normed"), T + 1)
                nc.tensor.transpose(ps[:, 6, 0:128], row32[:, T % 2, :], ident[:]).then_inc(sem("ga_turned"), 1)
                pe.wait_ge(sem("ga_rowT"), T + 1)
                if T:
                    pe.wait_ge(sem("ga_roped"), T)
                nc.tensor.matmul(ps[:, 7, 0:384], rowT[:, T % 2, :], w_qkv[:], start=True,
                                 stop=True).then_inc(sem("ga_projected"), 1)

        def gather_gpsimd(pool):
            passed = kv_all[:, 16:32, :].rearrange("p a b -> p (a b)").rearrange("p (b d) -> p b d", b=B)
            nc.gpsimd.tensor_tensor(passed, xd_all[:], keep[:].unsqueeze(2).broadcast_to([128, B, D]),
                                    ALU.mult).then_inc(sem("ga_passed"), 1)
            pool.wait_ge(sem("ga_passed"), 1)
            nc.gpsimd.tensor_tensor(x_all[:], x_all[:], passed, ALU.add).then_inc(sem("ga_passed"), 1)
            pool.wait_ge(sem("ga_passed"), 2)

        def gather_scalar(act):
            moments_scalar(act, TILES)
            for T in range(TILES):
                act.wait_ge(sem("ga_turned"), T + 1)
                nc.scalar.activation(rowT[:, T % 2, :], ps[:, 6, 0:128], ACT.Copy,
                                     scale=col("ln1")).then_inc(sem("ga_rowT"), 1)

        def gather_vector(dve):
            q = Seq(dve, sem("ga_seq"), moments_taken)
            dve.sem_inc(sem("ga_picked"), 1)
            dve.wait_ge(sem("ga_place"), 1)
            q(nc.vector.tensor_copy(place[:], ps[:, 7, 0:B]))
            full = [128, B, SLOTS]
            q(nc.vector.tensor_tensor(pick[:], iota_row[:].unsqueeze(1).broadcast_to(full),
                                      place[:].unsqueeze(2).broadcast_to(full), ALU.is_equal))
            q(nc.vector.tensor_tensor(pick[:], pick[:], picked[:].unsqueeze(2).broadcast_to(full), ALU.mult))
            ang = small[:, 0:32].rearrange("p (s c f) -> p s c f", s=2, c=4)
            turns = small[:, 32:64].rearrange("p (s c f) -> p s c f", s=2, c=4)
            for c in range(4):
                q(nc.vector.tensor_scalar(ang[:, 0, c, :], freq[:], pos_f[:, c:c + 1], None, ALU.mult))
            q(nc.vector.tensor_scalar(turns[:, 0], ang[:, 0], 1.0 / TWO_PI, MAGIC, ALU.mult, ALU.add))
            q(nc.vector.tensor_scalar(turns[:, 0], turns[:, 0], MAGIC, None, ALU.subtract))
            q(nc.vector.tensor_scalar(turns[:, 1], ang[:, 0], 1.0 / TWO_PI, 0.25, ALU.mult, ALU.add))
            q(nc.vector.tensor_scalar(turns[:, 1], turns[:, 1], MAGIC, MAGIC, ALU.add, ALU.subtract))
            q(nc.vector.tensor_copy(ang[:, 1], ang[:, 0]))
            fa = small[:, 0:32]
            ft = small[:, 32:64]
            for part in PI_PARTS:
                q(nc.vector.scalar_tensor_tensor(fa, ft, -part, fa, ALU.mult, ALU.add))
            q(nc.vector.tensor_scalar(ang[:, 1], ang[:, 1], TWO_PI / 4, None, ALU.add))
            q(nc.vector.tensor_scalar(fa, fa, SIN_LIMIT, -SIN_LIMIT, ALU.min, ALU.max))
            dve.sem_inc(sem("ga_angles"), 1)
            dve.wait_ge(sem("ga_sines"), 1)
            sin = small[:, 64:96].rearrange("p (s c f) -> p s c f", s=2, c=4)
            for s, at in ((1, 0), (0, 4)):
                q(nc.vector.tensor_copy(aux[:, 0:3, at:at + 4], sin[:, s, 0:3, :]))
                q(nc.vector.tensor_copy(aux[:, 3:B, at:at + 4],
                                        sin[:, s, 3:4, :].broadcast_to([128, B - 3, 4])))
            q(nc.vector.tensor_copy(aux[:, :, 8], wcol[:]))
            dve.sem_inc(sem("ga_pick"), 1)
            dve.wait_ge(sem("ga_gathered"), 1)
            flat = "p t s -> p (t s)"
            nc.vector.tensor_copy(probs[:, 1, 1024:1536], ps[:, 0, :]).then_inc(sem("ga_taken"), 1)
            nc.vector.tensor_copy(q_room[0:9, 0:512], ps[0:9, 1, :]).then_inc(sem("ga_taken"), 1)
            nc.vector.tensor_copy(probs[:, 1, 1536:2048], ps[:, 2, :]).then_inc(sem("ga_taken"), 1)
            dve.wait_ge(sem("ga_rows"), 1)
            q(nc.vector.tensor_copy(x1_tiles[:].rearrange(flat), ps[:, 4, :]))
            q(nc.vector.tensor_copy(aux_t[:], ps[:, 5, 0:64].rearrange("p (t s) -> p t s", t=TILES)[:, :, 0:9]))
            m = probs[:, 0, 0:512].rearrange("p (t s) -> p t s", t=TILES)
            q(nc.vector.tensor_tensor(m, ps[:, 3, :].rearrange("p (t s) -> p t s", t=TILES),
                                      outside[:].unsqueeze(1).broadcast_to([128, TILES, 128]), ALU.add))
            q(nc.vector.tensor_copy(mask3[:, :, 0, :], m))
            q(nc.vector.tensor_tensor(m, m, mask3[:, :, 0, :], ALU.subtract))
            q(nc.vector.tensor_copy(mask3[:, :, 1, :], m))
            q(nc.vector.tensor_tensor(mask3[:, :, 2, :], m, mask3[:, :, 1, :], ALU.subtract))
            for T in range(TILES):
                q(nc.vector.bn_stats(stat[:, T, :], x1_tiles[:, T, :]))
            moments_vector(dve, "rms", stat[:], TILES)
            for T in range(TILES):
                if T >= 2:
                    dve.wait_ge(sem("ga_turned"), T - 1)
                nc.vector.tensor_scalar(row32[:, T % 2, :], x1_tiles[:, T, :], inv_all[:, T:T + 1], None,
                                        ALU.mult).then_inc(sem("ga_normed"), 1)
                dve.wait_ge(sem("ga_projected"), T + 1)
                t = ps[:, 7, 0:256].rearrange("p (h s f) -> p h s f", s=2, f=4)
                shape = [128, 32, 4]
                cs = aux_t[:, T, 0:4].unsqueeze(1).broadcast_to(shape)
                sn = aux_t[:, T, 4:8].unsqueeze(1).broadcast_to(shape)
                a, c_, d, e = (probs[:, 1, 128 * i:128 * i + 128].rearrange("p (h f) -> p h f", f=4) for i in range(4))
                q(nc.vector.tensor_tensor(a, t[:, :, 0, :], cs, ALU.mult))
                q(nc.vector.tensor_tensor(c_, t[:, :, 1, :], sn, ALU.mult))
                q(nc.vector.tensor_tensor(d, t[:, :, 1, :], cs, ALU.mult))
                q(nc.vector.tensor_tensor(e, t[:, :, 0, :], sn, ALU.mult))
                qk = probs[:, 1, 512:768].rearrange("p (h s f) -> p h s f", s=2, f=4)
                q(nc.vector.tensor_tensor(qk[:, :, 0, :], a, c_, ALU.subtract))
                q(nc.vector.tensor_tensor(qk[:, :, 1, :], d, e, ALU.add))
                q(nc.vector.tensor_copy(kvD[:, T, 128:256], ps[:, 7, 256:384]))
                dve.wait_ge(sem("ga_passed"), 1)
                q(nc.vector.tensor_copy(qD[:, T, :], probs[:, 1, 512:640]))
                q(nc.vector.tensor_scalar(kvD[:, T, 0:128], probs[:, 1, 640:768], 8 ** -0.5, None, ALU.mult))
                dve.sem_inc(sem("ga_roped"), 1)

        def gather_scalar_sines(act):
            act.wait_ge(sem("ga_angles"), 1)
            nc.scalar.activation(small[:, 64:96], small[:, 0:32], ACT.Sin).then_inc(sem("ga_sines"), 1)

        def expand_tensor(pe):
            for T in range(TILES):
                pe.wait_ge(sem("ex_normed"), T + 1)
                nc.tensor.transpose(ps[:, 0, 0:128], row32[:, T % 2, :], ident[:]).then_inc(sem("ex_turned"), 1)
                pe.wait_ge(sem("ex_rowT"), T + 1)
                if T:
                    pe.wait_ge(sem("ex_gelu"), T)
                for c in range(4):
                    last = nc.tensor.matmul(ps[:, 1, 128 * c:128 * c + 128], w1_l1[:, 128 * c:128 * c + 128],
                                            rowT[:, T % 2, :], start=True, stop=True)
                last.then_inc(sem("ex_hidden"), 1)
                pe.wait_ge(sem("ex_gelu"), T + 1)
                if T:
                    pe.wait_ge(sem("ex_spread"), T)
                for c in range(4):
                    last = nc.tensor.matmul(ps[:, 2, 0:128], probs[:, 0, 128 * c:128 * c + 128], w2_l1[:, c, :],
                                            start=c == 0, stop=c == 3)
                last.then_inc(sem("ex_out"), 1)
                nc.tensor.transpose(ps[:, 3, 0:128], pick[:, T * PER_TILE:(T + 1) * PER_TILE, :]
                                    .rearrange("p b s -> p (b s)"), ident[:]).then_inc(sem("ex_pickT"), 1)
                pe.wait_ge(sem("ex_spread"), T + 1)
                if T:
                    pe.wait_ge(sem("ex_added"), T)
                for half in range(2):
                    last = nc.tensor.matmul(ps[:, 4 + half, :], rowT2[:], probs[:, 1, 512 * half:512 * half + 512],
                                            start=True, stop=True)
                last.then_inc(sem("ex_scattered"), 1)

        def expand_scalar(act):
            moments_scalar(act, TILES)
            for T in range(TILES):
                act.wait_ge(sem("ex_turned"), T + 1)
                nc.scalar.activation(rowT[:, T % 2, :], ps[:, 0, 0:128], ACT.Copy,
                                     scale=col("ln2")).then_inc(sem("ex_rowT"), 1)
                act.wait_ge(sem("ex_hidden"), T + 1)
                if T:
                    act.wait_ge(sem("ex_out"), T)
                nc.scalar.activation(probs[:, 0, 0:512], ps[:, 1, :], ACT.Gelu_apprx_tanh).then_inc(sem("ex_gelu"), 1)

        def expand_vector(dve):
            q = Seq(dve, sem("ex_seq"), moments_taken)
            moments_vector(dve, "rms", stat[:], TILES)
            for T in range(TILES):
                nc.vector.tensor_scalar(row32[:, T % 2, :], x1_tiles[:, T, :], inv_all[:, T:T + 1], None,
                                        ALU.mult).then_inc(sem("ex_normed"), 1)
                dve.wait_ge(sem("ex_pickT"), T + 1)
                if T:
                    dve.wait_ge(sem("ex_scattered"), T)
                q(nc.vector.tensor_copy(rowT2[:], ps[:, 3, 0:128]))
                dve.wait_ge(sem("ex_out"), T + 1)
                q(nc.vector.tensor_tensor(x1_tiles[:, T, :], x1_tiles[:, T, :], ps[:, 2, 0:128], ALU.add))
                q(nc.vector.tensor_scalar(x1_tiles[:, T, :], x1_tiles[:, T, :], aux_t[:, T, 8:9], None, ALU.mult))
                full = [128, PER_TILE, 128]
                q(nc.vector.tensor_tensor(probs[:, 1, 0:1024].rearrange("p (b d) -> p b d", b=PER_TILE),
                                          x1_tiles[:, T:T + 1, :].broadcast_to(full),
                                          own[:].unsqueeze(2).broadcast_to(full), ALU.mult))
                dve.sem_inc(sem("ex_spread"), 1)
                dve.wait_ge(sem("ex_scattered"), T + 1)
                part = x_all[:, T * PER_TILE:(T + 1) * PER_TILE, :]
                nc.vector.tensor_tensor(part, part, ps[:, 4:6, :].rearrange("p a (b d) -> p (a b) d", b=4),
                                        ALU.add).then_inc(sem("ex_added"), 1)
                dve.wait_ge(sem("ex_added"), T + 1)
                for b in range(T * PER_TILE, (T + 1) * PER_TILE):
                    nc.vector.bn_stats(stats_all[:, b, :], x_all[:, b, :]).then_inc(sem("measured"), 1)

        def bit_vector(dve):
            def norm_b(b, k):
                wait_reuse(dve, after("turned"), b, 2)
                link = Link(dve, after("link"), b, 6)
                m, r = mv[:, k % 2, :], row32[:, k % 2, :]
                yield link.count(norm(r, b))
                yield link.count(nc.vector.tensor_reduce(m[:, 3:4], r, AX.X, ALU.max, apply_absolute_value=True))
                yield link.count(nc.vector.tensor_scalar(m[:, 3:4], m[:, 3:4], 1e-5, 1.0 / 127.0, ALU.max, ALU.mult))
                yield link.count(nc.vector.reciprocal(m[:, 4:5], m[:, 3:4]))
                yield link.count(nc.vector.tensor_scalar(r, r, m[:, 4:5], MAGIC, ALU.mult, ALU.add))
                yield link.count(nc.vector.tensor_scalar(r, r, MAGIC, m[:, 3:4], ALU.subtract, ALU.mult))
                dve.sem_inc(sem("normed"), 1)
                link.end()

            def quantise(b, k):
                dve.wait_ge(sem("bt_silu"), b + 1)
                link = Link(dve, after("link2"), b, 5)
                h, r = probs[:, k % 2, 0:512], rank[:, k % 2, :]
                yield link.count(nc.vector.tensor_reduce(r[:, 0:1], h, AX.X, ALU.max, apply_absolute_value=True))
                yield link.count(nc.vector.tensor_scalar(r[:, 0:1], r[:, 0:1], 1e-5, 1.0 / 127.0, ALU.max, ALU.mult))
                yield link.count(nc.vector.reciprocal(r[:, 1:2], r[:, 0:1]))
                yield link.count(nc.vector.tensor_tensor(scale2[:, k:k + 1], r[:, 0:1], inv_w[:, 3:4], ALU.mult))
                yield link.count(nc.vector.tensor_scalar(h, h, r[:, 1:2], MAGIC, ALU.mult, ALU.add))
                wait_reuse(dve, after("bt_turned2"), b, 2)
                nc.vector.tensor_scalar(q2[:, k % 2, :], h, MAGIC, None, ALU.subtract).then_inc(sem("bt_quantised"), 1)
                link.end()

            def add(b, k):
                dve.wait_ge(sem("bt_out"), b + 1)
                nc.vector.scalar_tensor_tensor(x_all[:, b, :], ps[:, 6 + k % 2, 0:128], scale2[:, k:k + 1],
                                               x_all[:, b, :], ALU.mult, ALU.add).then_inc(sem("added"), 1)
                measure(dve, after("added"), b)

            def take2(b, k):
                dve.wait_ge(sem("bt_turned2"), b + 1)
                wait_reuse(dve, after("bt_out"), b, 2)
                nc.vector.tensor_copy(q2T[:, k % 2, :, :].rearrange("p c t -> p (c t)"),
                                      bank_b[4 + k % 2][:, 0:512]).then_inc(sem("bt_q2T"), 1)
            def step(items):
                in_turns(*([quantise(*items[3])] if 3 in items else []), *([norm_b(*items[0])] if 0 in items else []))
                if 4 in items:
                    take2(*items[4])
                if 5 in items:
                    add(*items[5])
            whole_steps(dve, B, 5, step)

        def bit_scalar(act):
            def silu(b, k):
                act.wait_ge(*after("used", b + 1))
                wait_reuse(act, after("bt_quantised"), b, 2)
                nc.scalar.activation(probs[:, k % 2, 0:512], ps[:, 2 + k % 2, :], ACT.Silu).then_inc(sem("bt_silu"), 1)
            steps(act, B, [(1, take_rows(act, dst=lambda k: xqT[:, k % 2, 1:129])), (2, silu)])

        def bit_tensor(pe):
            def hidden(b, k):
                pe.wait_ge(*after("rowT", b + 1))
                wait_reuse(pe, after("bt_silu"), b, 2)
                dst = ps[:, 2 + k % 2, :]
                nc.tensor.matmul(dst, onesb[0:3, :], bias_rows[:, 640:1152], start=True, stop=False)
                for tap in range(3):
                    last = nc.tensor.matmul(dst, xqT[:, k % 2, tap:tap + 128], tap_w[:, tap, :],
                                            start=False, stop=tap == 2)
                last.then_inc(sem("used"), 1)

            def turn2(b, k):
                pe.wait_ge(sem("bt_quantised"), b + 1)
                wait_reuse(pe, after("bt_q2T"), b, 2)
                for c in range(4):
                    last = nc.tensor.transpose(bank_b[4 + k % 2][:, 128 * c:128 * c + 128],
                                               q2[:, k % 2, 128 * c:128 * c + 128], identb[:])
                last.then_inc(sem("bt_turned2"), 1)

            def output(b, k):
                pe.wait_ge(sem("bt_q2T"), b + 1)
                wait_reuse(pe, after("added"), b, 2)
                for c in range(4):
                    last = nc.tensor.matmul(ps[:, 6 + k % 2, 0:128], q2T[:, k % 2, c, :], w2_q[:, c, :],
                                            start=c == 0, stop=c == 3)
                last.then_inc(sem("bt_out"), 1)
            steps(pe, B, [(4, turn2), (5, output), (1, turn_rows(pe)), (2, hidden)])

        def cross_vector(dve):
            def norm_b(b, k):
                wait_reuse(dve, after("turned"), b, 2)
                norm(row32[:, k % 2, :], b).then_inc(sem("normed"), 1)

            def take_ctx(b, k):
                dve.wait_ge(sem("cr_ctx_turned"), b + 1)
                wait_reuse(dve, after("cr_kv"), b, 2)
                nc.vector.tensor_copy(probs[:, k % 2, 0:256], ps[:, 2 + k % 2, 0:256]).then_inc(sem("cr_ctxT"), 1)

            def add(b, k):
                dve.wait_ge(*after("used", b + 1))
                nc.vector.tensor_tensor(x_all[:, b, :], x_all[:, b, :], ps[:, 4 + k % 2, 128:256],
                                        ALU.add).then_inc(sem("added"), 1)
            steps(dve, B, [(0, norm_b), (1, take_ctx), (3, add)])

        def cross_gpsimd(pool):
            def copy_ctx(b, k):
                wait_reuse(pool, after("cr_ctx_turned"), b, 2)
                hold(pool)
                nc.gpsimd.tensor_copy(probs[:, k % 2, 256:512], ctx_all[:, b, :]).then_inc(sem("cr_ctx"), 1)
            steps(pool, B, [(0, copy_ctx)])

        def cross_scalar(act):
            def take_q(b, k):
                act.wait_ge(*after("added", b + 1))
                nc.scalar.activation(q_all[:, b, :], ps[:, 4 + k % 2, 0:128], ACT.Copy,
                                     scale=mask_q[:, bass.ts(b, 1)]).then_inc(sem("cr_q"), 1)

            def take_kv(b, k):
                act.wait_ge(sem("cr_kv"), b + 1)
                nc.scalar.activation(kv_all[:, b, :], ps[:, 6 + k % 2, 0:256], ACT.Copy,
                                     scale=mask_f[:, bass.ts(b, 1)]).then_inc(sem("cr_kv_taken"), 1)
            steps(act, B, [(1, take_rows(act)), (3, take_kv), (3, take_q)])

        def cross_tensor(pe):
            def turn_ctx(b, k):
                pe.wait_ge(sem("cr_ctx"), b + 1)
                wait_reuse(pe, after("cr_ctxT"), b, 2)
                hold(pe)
                for c in range(2):
                    last = nc.tensor.transpose(ps[:, 2 + k % 2, 128 * c:128 * c + 128],
                                               probs[:, k % 2, 256 + 128 * c:384 + 128 * c], ident[:])
                last.then_inc(sem("cr_ctx_turned"), 1)

            def queries(b, k):
                pe.wait_ge(*after("rowT", b + 1))
                wait_reuse(pe, after("cr_q"), b, 2)
                dst = ps[:, 4 + k % 2, 0:256]
                nc.tensor.matmul(dst, onesb[0:3, :], bias_rows[:, 384:640], start=True, stop=False)
                nc.tensor.matmul(dst, rowT[:, k % 2, :], w_tgt[:], start=False, stop=True).then_inc(sem("used"), 1)

            def keys(b, k):
                pe.wait_ge(sem("cr_ctxT"), b + 1)
                wait_reuse(pe, after("cr_kv_taken"), b, 2)
                dst = ps[:, 6 + k % 2, 0:256]
                nc.tensor.matmul(dst, onesb[0:3, :], bias_rows[:, 128:384], start=True, stop=False)
                for c in range(2):
                    last = nc.tensor.matmul(dst, probs[:, k % 2, 128 * c:128 * c + 128], w_src[:, c, :],
                                            start=False, stop=c == 1)
                last.then_inc(sem("cr_kv"), 1)
            steps(pe, B, [(1, turn_rows(pe)), (1, turn_ctx), (2, queries), (2, keys)])

        def latent_vector(dve):
            def norm_b(b, k):
                wait_reuse(dve, after("turned"), b, 2)
                norm(row32[:, k % 2, :], b).then_inc(sem("normed"), 1)
                nc.vector.tensor_scalar(z_all[:, b, :], x_all[:, b, :], mean_all[:, bass.ts(b, 1)],
                                        inv_ln[:, bass.ts(b, 1)], ALU.subtract, ALU.mult).then_inc(sem("z_set"), 1)

            def rotate(link, src, at, dst, tmp, signal):
                yield link.count(nc.vector.tensor_tensor(tmp[:, 0:128], src[:, 0:128], rope[:, at, :], ALU.mult))
                yield link.count(nc.vector.tensor_tensor(tmp[:, 128:256], src[:, 128:256], rope[:, at + 1, :], ALU.mult))
                nc.vector.tensor_tensor(dst, tmp[:, 0:128], tmp[:, 128:256], ALU.add).then_inc(signal, 1)

            def query(b, k):
                dve.wait_ge(*after("used", b + 1))
                link = Link(dve, after("link2"), b, 7)
                src = ps[:, 2 + k % 2, :]
                m, st = small[:, 8 * (k % 2):8 * (k % 2) + 8], small[:, 32 + 8 * (k % 2):38 + 8 * (k % 2)]
                yield link.count(nc.vector.bn_stats(st, src[:, 256:320]))
                hold(dve)
                yield link.count(nc.vector.bn_aggr(m[:, 0:2], st))
                yield link.count(nc.vector.tensor_scalar(m[:, 2:3], m[:, 1:2], 1e-5, None, ALU.add))
                dve.sem_inc(sem("la_variance"), 1)
                yield
                yield
                dve.wait_ge(sem("la_root"), b + 1)
                yield link.count(nc.vector.reciprocal(m[:, 4:5], m[:, 3:4]))
                yield link.count(nc.vector.tensor_scalar(m[:, 5:6], m[:, 4:5], m[:, 4:5], m[:, 2:3], ALU.mult, ALU.mult))
                yield link.count(nc.vector.tensor_scalar(m[:, 5:6], m[:, 5:6], -0.5, 1.5, ALU.mult, ALU.add))
                yield link.count(nc.vector.tensor_tensor(m[:, 4:5], m[:, 4:5], m[:, 5:6], ALU.mult))
                wait_reuse(dve, after("la_latent_turned"), b, 2)
                nc.vector.tensor_scalar(o_sb[:, k % 2, 0:LATENT], src[:, 256:320], m[:, 0:1], m[:, 4:5],
                                        ALU.subtract, ALU.mult).then_inc(sem("la_latent"), 1)
                link.end()

            def query_turned(b, k):
                dve.wait_ge(*after("used", b + 1))
                link = Link(dve, after("la_link4"), b, 2)
                yield from rotate(link, ps[:, 2 + k % 2, :], 0, q_all[:, b, :], junk, sem("la_q"))
                link.end()

            def latent(b, k):
                dve.wait_ge(sem("la_latent_turned"), b + 1)
                wait_reuse(dve, after("la_kv"), b, 2)
                nc.vector.tensor_scalar(oT[0:LATENT, k % 2, :], ps[0:LATENT, 4 + k % 2, 0:128], col("ln_g", LATENT),
                                        col("ln_b", LATENT), ALU.mult, ALU.add).then_inc(sem("la_latentT"), 1)

            def key(b, k):
                dve.wait_ge(sem("la_kv"), b + 1)
                link = Link(dve, after("link3"), b, 2)
                yield from rotate(link, ps[:, 6 + k % 2, :], 2, kv_all[:, b, 0:128], probs[:, k % 2, 0:256], sem("la_k"))
                link.end()
            def step(items):
                if 0 in items:
                    norm_b(*items[0])
                in_turns(*([query(*items[3]), query_turned(*items[3])] if 3 in items else []),
                         *([key(*items[6])] if 6 in items else []))
                if 4 in items:
                    latent(*items[4])
            whole_steps(dve, B, 6, step)

        def latent_scalar(act):
            def root(b, k):
                act.wait_ge(sem("la_variance"), b + 1)
                m = small[:, 8 * (k % 2):8 * (k % 2) + 8]
                nc.scalar.activation(m[:, 3:4], m[:, 2:3], ACT.Sqrt).then_inc(sem("la_root"), 1)

            def take_v(b, k):
                act.wait_ge(sem("la_k"), b + 1)
                nc.scalar.activation(kv_all[:, b, 128:256], ps[:, 6 + k % 2, 256:384],
                                     ACT.Copy).then_inc(sem("la_v"), 1)
            steps(act, B, [(1, take_rows(act, col("norm1"))), (3, root), (6, take_v)])

        def latent_tensor(pe):
            def queries(b, k):
                pe.wait_ge(*after("rowT", b + 1))
                wait_reuse(pe, after("la_latent"), b, 2)
                wait_reuse(pe, after("la_q"), b, 2)
                nc.tensor.matmul(ps[:, 2 + k % 2, 0:320], rowT[:, k % 2, :], w_h1[:], start=True,
                                 stop=True).then_inc(sem("used"), 1)

            def turn_latent(b, k):
                pe.wait_ge(sem("la_latent"), b + 1)
                wait_reuse(pe, after("la_latentT"), b, 2)
                hold(pe)
                nc.tensor.transpose(ps[0:LATENT, 4 + k % 2, 0:128], o_sb[:, k % 2, 0:LATENT],
                                    ident[:]).then_inc(sem("la_latent_turned"), 1)

            def keys(b, k):
                pe.wait_ge(sem("la_latentT"), b + 1)
                wait_reuse(pe, after("la_v"), b, 2)
                nc.tensor.matmul(ps[:, 6 + k % 2, 0:384], oT[0:LATENT, k % 2, :], w_h2[:], start=True,
                                 stop=True).then_inc(sem("la_kv"), 1)
            steps(pe, B, [(4, turn_latent), (5, keys), (1, turn_rows(pe)), (2, queries)])

        GROUPS = B // 4
        CHUNKS = N_EXP3 * HID // 128
        w_up = ctx_all[:, 0:8, :].rearrange("p a b -> p (a b)").rearrange("p (c h) -> p c h", c=16)
        w_down = ctx_all[:, 8:16, :].rearrange("p a b -> p (a b)").rearrange("p (c h) -> p c h", c=16)
        work_m = kv_all[:].rearrange("p a b -> p (a b)")
        xm_rows = work_m[:, 0:512]
        total = work_m[:, 512:1024]
        term = work_m[:, 1024:1536]
        hid = work_m[:, 1536:3584].rearrange("p (s t) -> p s t", s=4)
        chosen = work_m[:, 4096:8192].rearrange("p (k e t) -> p k e t", k=2, e=4)
        xm_T = q_all[:, 0:8, :].rearrange("p a b -> p (a b)").rearrange("p (k t) -> p k t", k=2)

        def loop_groups(engine, body):
            body(0, 0)
            with engine.Fori(0, GROUPS // 2 - 1) as pair:
                for u in range(2):
                    body(pair * 2 + (u + 1), (u + 1) % 2)
            body(GROUPS - 1, 1)

        def is_last(i):
            return isinstance(i, int) and i == GROUPS - 1

        def is_first(i):
            return isinstance(i, int) and i == 0

        def expert_vector(dve):
            def prepare(i, k):
                for j in range(4):
                    nc.vector.tensor_scalar(xm_rows[:, 128 * j:128 * j + 128], z_all[:, i * 4 + j, :],
                                            inv_all[:, bass.ts(i * 4 + j, 1)], None,
                                            ALU.mult).then_inc(sem("mo_normed"), 1)
                yield
                dve.wait_ge(sem("mo_turned"), i + 1)
                nc.vector.tensor_scalar(xm_T[:, k, :], ps[:, 2, :], col("norm2"), None,
                                        ALU.mult).then_inc(sem("mo_rowT"), 1)
                yield
                dve.wait_ge(sem("mo_logits"), i + 1)
                lg = small[:, 64:80].rearrange("p (j e) -> p j e", j=4)
                eq = small[:, 80:96].rearrange("p (j e) -> p j e", j=4)
                top = small[:, 96:100]
                full = [128, 4, 4]
                link = Link(dve, (sem("mo_link_choice"), 0), i, 5)
                link(nc.vector.tensor_tensor(lg, ps[:, 3, 0:16].rearrange("p (j e) -> p j e", j=4),
                                             gate_b[:].unsqueeze(1).broadcast_to(full), ALU.add))
                link(nc.vector.tensor_reduce(top, lg, AX.X, ALU.max))
                link(nc.vector.tensor_tensor(eq, lg, top.unsqueeze(2).broadcast_to(full), ALU.is_equal))
                link(nc.vector.tensor_tensor(eq, eq, first_row[:].unsqueeze(1).broadcast_to(full), ALU.mult))
                link(nc.vector.tensor_reduce(top, eq, AX.X, ALU.max))
                link.end()
                nc.vector.tensor_tensor(nm3[:, 0, 0:48].rearrange("p (e j c) -> p j e c", e=4, c=3)[:, :, :, 0], eq,
                                        top.unsqueeze(2).broadcast_to(full), ALU.is_equal).then_inc(sem("mo_choice"), 1)
                yield
                dve.wait_ge(sem("mo_choice_turned"), i + 1)
                nc.vector.tensor_copy(nmT[:, 0, :], bank_b[3][:, 128:256]).then_inc(sem("mo_choiceT"), 1)
                for e in range(N_EXP3):
                    yield
                    dve.wait_ge(sem("mo_along"), i * 4 + (e + 1))
                    nc.vector.tensor_copy(chosen[:, k, e, :], ps[:, 6, :]).then_inc(sem("mo_chosen"), 1)

            def combine(i, k, link, e):
                dve.wait_ge(sem("mo_down"), i * CHUNKS + 4 * (e + 1))
                if e == 0:
                    dve.wait_ge(sem("mo_chosen"), i * 4 + 4)
                dst = total if e == 0 else term
                link(nc.vector.scalar_tensor_tensor(dst, ps[:, 4 + e % 2, :], b2_col[:, e:e + 1], chosen[:, k, e, :],
                                                    ALU.add, ALU.mult))
                dve.sem_inc(sem("mo_combined"), 1)
                if e:
                    link(nc.vector.tensor_tensor(total, total, term, ALU.add))

            def finish(i):
                rows = x_all[:, bass.ts(i, 4), :]
                dve.wait_ge(sem("mo_joined"), i + 1)
                dve.wait_ge(sem("mo_back"), i + 1)
                nc.vector.tensor_tensor(rows, rows, ps[:, 7, :].rearrange("p (j d) -> p j d", j=4),
                                        ALU.add).then_inc(sem("mo_done"), 1)

            def group(i, k):
                if is_first(i):
                    for _ in prepare(0, 0):
                        pass
                coming = iter(()) if is_last(i) else prepare(i + 1, 1 - k)
                link = Link(dve, (sem("mo_link"), 0), i, 7)
                next(coming, None)
                for c in range(1, CHUNKS, 2):
                    dve.wait_ge(sem("mo_hidden"), i * CHUNKS + (c + 1))
                    if c >= 4 or not is_first(i):
                        dve.wait_ge(sem("mo_down"), i * CHUNKS + (c - 3))
                    nc.vector.tensor_scalar(hid[:, c % 4, :], ps[:, c % 2, :], b1_col[:, c:c + 1], 0.0,
                                            ALU.add, ALU.max).then_inc(sem("mo_relu_odd"), 1)
                    if c == 1 and not is_first(i):
                        finish(i - 1)
                    if c % 4 == 3 and c > 4:
                        combine(i, k, link, c // 4 - 1)
                    if c >= 3 and c != 7:
                        next(coming, None)
                combine(i, k, link, 3)
                link.end()
                dve.sem_inc(sem("mo_total"), 1)
                next(coming, None)
                assert next(coming, "through") == "through"
                if is_last(i):
                    finish(i)

            loop_groups(dve, group)

        def expert_scalar(act):
            def group(i, k):
                for c in range(0, CHUNKS, 2):
                    act.wait_ge(sem("mo_hidden"), i * CHUNKS + (c + 1))
                    if c >= 4 or not is_first(i):
                        act.wait_ge(sem("mo_down"), i * CHUNKS + (c - 3))
                    nc.scalar.activation(hid[:, c % 4, :], ps[:, c % 2, :], ACT.Relu,
                                         bias=b1_col[:, c:c + 1]).then_inc(sem("mo_relu_even"), 1)
            loop_groups(act, group)

        def expert_gpsimd(pool):
            with pool.Fori(0, GROUPS) as i:
                rows = x_all[:, bass.ts(i, 4), :]
                nc.gpsimd.tensor_tensor(rows, rows, z_all[:, bass.ts(i, 4), :], ALU.add).then_inc(sem("mo_joined"), 1)

        def expert_tensor(pe):
            def prepare(i, k):
                pe.wait_ge(sem("mo_normed"), i * 4 + 4)
                hold(pe)
                for j in range(4):
                    last = nc.tensor.transpose(ps[:, 2, 128 * j:128 * j + 128], xm_rows[:, 128 * j:128 * j + 128],
                                               ident[:])
                last.then_inc(sem("mo_turned"), 1)
                yield
                pe.wait_ge(sem("mo_rowT"), i + 1)
                for j in range(4):
                    last = nc.tensor.matmul(ps[:, 3, 4 * j:4 * j + 4], xm_T[:, k, 128 * j:128 * j + 128], gate_w[:],
                                            start=True, stop=True)
                last.then_inc(sem("mo_logits"), 1)
                yield
                pe.wait_ge(sem("mo_choice"), i + 1)
                hold(pe)
                nc.tensor.transpose(bank_b[3][:, 128:256], nm3[:, 0, :], identb[:]).then_inc(sem("mo_choice_turned"), 1)
                yield
                pe.wait_ge(sem("mo_choiceT"), i + 1)
                for e in range(N_EXP3):
                    if e or not is_first(i):
                        pe.wait_ge(sem("mo_chosen"), i * 4 + e)
                    for j in range(4):
                        last = nc.tensor.matmul(ps[:, 6, 128 * j:128 * j + 128], sel[:, 4 * e + j, :], nmT[:, 0, :],
                                                start=True, stop=True)
                    last.then_inc(sem("mo_along"), 1)
                    yield

            def up(i, k, c):
                if c >= 2 or not is_first(i):
                    pe.wait_ge(sem("mo_relu_odd" if c % 2 else "mo_relu_even"), i * (CHUNKS // 2) + c // 2)
                nc.tensor.matmul(ps[:, c % 2, :], w_up[:, c, :], xm_T[:, k, :], start=True,
                                 stop=True).then_inc(sem("mo_hidden"), 1)

            def turn_back(i):
                pe.wait_ge(sem("mo_total"), i + 1)
                hold(pe)
                for j in range(4):
                    last = nc.tensor.transpose(ps[:, 7, 128 * j:128 * j + 128], total[:, 128 * j:128 * j + 128],
                                               ident[:])
                last.then_inc(sem("mo_back"), 1)

            def group(i, k):
                if is_first(i):
                    for _ in prepare(0, 0):
                        pass
                    up(i, k, 0)
                    up(i, k, 1)
                coming = iter(()) if is_last(i) else prepare(i + 1, 1 - k)
                for c in range(CHUNKS):
                    e = c // 4
                    pe.wait_ge(sem("mo_relu_odd" if c % 2 else "mo_relu_even"), i * (CHUNKS // 2) + (c // 2 + 1))
                    if c % 4 == 0 and (e >= 2 or not is_first(i)):
                        pe.wait_ge(sem("mo_combined"), i * 4 + (e - 1))
                    nc.tensor.matmul(ps[:, 4 + e % 2, :], w_down[:, c, :], hid[:, c % 4, :], start=c % 4 == 0,
                                     stop=c % 4 == 3).then_inc(sem("mo_down"), 1)
                    if c + 2 < CHUNKS:
                        up(i, k, c + 2)
                    elif not is_last(i):
                        up(i + 1, 1 - k, c + 2 - CHUNKS)
                    if c == 0 and not is_first(i):
                        turn_back(i - 1)
                    if c % 2 == 1 and c != 5:
                        next(coming, None)
                assert next(coming, "through") == "through"
                if is_last(i):
                    turn_back(i)
            loop_groups(pe, group)

        lens_i = probs[:, 1, 1664:1792].bitcast(I32).rearrange("p (n b) -> p n b", n=4)
        bias_rows_f = probs[0:3, 1, 512:1664]
        w2_nat = probs[:, 1, 0:512]
        w1_nat = probs[:, 0, 0:512]
        conv_f = probs[:, 0, 512:2048].rearrange("p (t c) -> p t c", t=3)

        loads = [
            (ident[:], t_in["c_ident"]), (upper[:], t_in["c_upper"]), (below[:], t_in["c_below"]),
            (above[:], t_in["c_above"]), (toep[:], t_in["c_toep"]), (iota_p[:], t_in["c_iota_p"]),
            (iota_row[:], t_in["c_iota_row"]), (sel_col[:], t_in["c_sel"]),
            (rope[:], t_in["c_rope"]), (outside[:], t_in["c_outside"]), (own[:], t_in["c_own"]),
            (freq[:], t_in["c_freq"]), (first_row[:], t_in["c_first"]),
            (lens_i[:, 0, :], t_in["itok"].rearrange("b one -> (one b)").partition_broadcast(128)),
            (lens_i[:, 1, :], t_in["ik0T"]), (lens_i[:, 2, :], t_in["if0T"]),
            (lens_i[:, 3, 0:4], t_in["posT"][0:S, :]),
            (mask_f[:], t_in["fk1T"]),
            (g_init[:], t_in["g_init"][0:D].partition_broadcast(128)),
            (wg[:], t_in["w_inT"]), (w_qkv[:, 0:128], t_in["wq"]), (w_qkv[:, 128:256], t_in["wk"]),
            (w_qkv[:, 256:384], t_in["wv"]), (w_o1[:], t_in["wo"]), (w1_l1[:], t_in["w1"]),
            (w2_l1[:], t_in["w2"].rearrange("(c n) d -> n c d", n=128)),
            (cls_mask[:], t_in["amask"][:, 0, 0:S, 0:S].rearrange("c t u -> t c u")),
            (w1_nat, t_in["b_w1T"]), (w2_nat.rearrange("p (c d) -> p c d", c=4),
                                      t_in["b_w2T"].rearrange("(c n) d -> n c d", n=128)),
            (conv_f, t_in["conv_wT"].partition_broadcast(128)),
            (w_src[:], t_in["W_srcT"].rearrange("(c f) o -> f c o", f=128)),
            (w_tgt[:, 0:128], t_in["W_tgtT"]), (w_tgt[:, 128:256], t_in["W_outT"][0:128, :]),
            (w_out2[:], t_in["W_outT"][128:256, :]),
            (w_h1[:, 0:128], t_in["WqT"]), (w_h1[:, 128:256], t_in["WqT_turned"]), (w_h1[:, 256:320], t_in["WdkvT"]),
            (w_h2[:, 0:128], t_in["WukT"]), (w_h2[:, 128:256], t_in["WukT_turned"]), (w_h2[:, 256:384], t_in["WuvT"]),
            (w_o3[:], t_in["WoT"]), (gate_w[:], t_in["gateT"]), (gate_b[:], t_in["gate_b"].partition_broadcast(128)),
            (b1_col[:], t_in["b1T"]), (b2_col[:], t_in["b2T"]),
            (bias_rows_f[:, 0:128], t_in["b_in"].partition_broadcast(3)),
            (bias_rows_f[:, 128:384], t_in["b_src"].partition_broadcast(3)),
            (bias_rows_f[:, 384:512], t_in["b_tgt"].partition_broadcast(3)),
            (bias_rows_f[:, 512:640], t_in["b_out"].partition_broadcast(3)),
            (bias_rows_f[:, 640:1152], t_in["conv_b"].partition_broadcast(3)),
            (col("L0_b"), t_in["L0_b"].rearrange("(s one) -> s one", one=1)),
            (col("L2_b"), t_in["L2_b"].partition_broadcast(128)),
            (col("router_b"), t_in["router_b"].partition_broadcast(128)),
            (col("router_w"), t_in["router_w"]),
        ] + [(col(n, t_in[n].shape[0]), t_in[n].rearrange("(s one) -> s one", one=1))
             for n in ("g_res", "ln1", "ln2", "norm1", "norm2", "ln_g", "ln_b")]

        def prep_sync(sp):
            sp.dma_start(x_all[:], t_in["x"].rearrange("b s d -> s b d")).then_inc(sem("x_loaded"), 16)
            sp.dma_start(ctx_all[:], t_in["ctx"].rearrange("b s d -> s b d")).then_inc(sem("ctx_loaded"), 16)
            sp.dma_start(kv_all[:, :, 0:128], t_in["f0_w1T"].rearrange("e (c n) h -> n (e c) h", n=128)
                         ).then_inc(sem("l0_weights"), 16)
            sp.dma_start(kv_all[:, :, 128:256], t_in["f0_w2"].rearrange("e (c n) h -> n (e c) h", n=128)
                         ).then_inc(sem("l0_weights"), 16)
            sp.wait_ge(sem("x_loaded"), 16)
            sp.wait_ge(sem("ctx_loaded"), 16)

        def prep_scalar(act):
            for dst, src in loads:
                act.dma_start(dst, src, allow_slow_non_contiguous=True).then_inc(sem("small_loaded"), 16)
            first_stats_scalar(act)

        def prep_tensor(pe):
            ffn0_prep_tensor(pe)
            pe.wait_ge(sem("valid_ready"), 1)
            nc.tensor.matmul(ps[:, 0, 0:B], ones[:], lens_f[:], start=True, stop=True).then_inc(sem("valid_counted"), 1)
            pe.wait_ge(sem("abs_ready"), 1)
            nc.tensor.matmul(ps[:, 1, 0:2], ones[:], inv_w[:, 0:2], start=True, stop=True).then_inc(sem("abs_summed"), 1)

        def prep_gpsimd(pool):
            nc.gpsimd.memset(ones[:], 1.0).then_inc(sem("ones_set"), 1)

        def prep_vector(dve):
            q = Seq(dve, sem("prep_seq"), moments_taken)
            dve.wait_ge(sem("x_loaded"), 16)
            for b in range(B):
                nc.vector.bn_stats(stats_all[:, b, :], x_all[:, b, :]).then_inc(sem("measured"), 1)
            dve.wait_ge(sem("small_loaded"), 16 * len(loads))
            dve.wait_ge(sem("ones_set"), 1)
            V = nc.vector
            q(V.tensor_copy(identb[:], ident[:]))
            q(V.tensor_copy(upperb[:], upper[:]))
            q(V.tensor_copy(onesb[:], ones[:]))
            q(V.memset(xqT[:], 0.0))
            q(V.tensor_copy(sel[:], sel_col[:].unsqueeze(2).broadcast_to([128, 16, 128])))
            q(V.tensor_scalar(causal[:], above[:], BIG, None, ALU.mult))
            bias = small[:, 0:B]
            valid = small[:, B:2 * B]
            q(V.tensor_copy(lens_f[:], lens_i[:, 1, :]))
            dve.sem_inc(sem("valid_ready"), 1)
            dve.wait_ge(sem("valid_counted"), 1)
            q(V.tensor_scalar(k_scale[:, 1, :], ps[:, 0, 0:B], 0.5, 16 ** -0.5, ALU.is_gt, ALU.mult))

            def to_bias(which, penalty, add, any_valid):
                q(V.tensor_scalar(bias, valid, 1.0, penalty, ALU.subtract, ALU.mult))
                if add is not None:
                    q(V.tensor_scalar(bias, bias, add, None, ALU.add))
                if any_valid is not None:
                    q(V.tensor_tensor(bias, bias, any_valid, ALU.mult))
                for part in range(3):
                    q(V.tensor_copy(bias3[:, which, :, part], bias))
                    q(V.tensor_tensor(bias, bias, bias3[:, which, :, part], ALU.subtract))

            q(V.tensor_scalar(valid, ps[:, 0, 0:B], 0.5, None, ALU.is_gt))
            q(V.tensor_copy(small[:, 96:128], valid))
            q(V.tensor_copy(valid, lens_f[:]))
            to_bias(1, 1e30, col("L2_b"), small[:, 96:128])
            q(V.tensor_copy(lens_f[:], lens_i[:, 0, :]))
            q(V.tensor_scalar(valid, lens_f[:], iota_p[:, 0:1], None, ALU.is_gt))
            q(V.tensor_scalar(k_scale[:, 0, :], lens_f[:], 0.0, 8 ** -0.5, ALU.is_gt, ALU.mult))
            q(V.tensor_scalar(small[:, 96:128], lens_f[:], 0.0, None, ALU.is_gt))
            to_bias(0, 1e12, col("L0_b"), small[:, 96:128])
            q(V.tensor_scalar(valid, mask_f[:], 0.0, None, ALU.not_equal))
            to_bias(2, 1e30, None, None)
            q(V.tensor_scalar(mask_q[:], mask_f[:], 0.25, None, ALU.mult))
            q(V.tensor_copy(lens_f[:], lens_i[:, 2, :]))
            q(V.tensor_copy(pos_f[:], lens_i[:, 3, 0:4]))
            q(V.tensor_scalar(wg[:], wg[:], col("g_res"), None, ALU.mult))
            q(V.tensor_scalar(rw_rep[:], ones[:], col("router_w"), None, ALU.mult))
            q(V.tensor_scalar(g_init[:], g_init[:], PATCH_GAIN, None, ALU.mult))
            part = w_part[0:3, :]
            for p in range(3):
                q(V.tensor_copy(part, bias_rows_f))
                q(V.tensor_tensor(bias_rows_f, bias_rows_f, part, ALU.subtract))
                if p == 0:
                    q(V.tensor_scalar(bias_rows[:], part, ident[0:3, 0:1], None, ALU.mult))
                else:
                    q(V.scalar_tensor_tensor(bias_rows[:], part, ident[0:3, p:p + 1], bias_rows[:], ALU.mult, ALU.add))
            q(V.tensor_reduce(inv_w[:, 0:1], w1_nat, AX.X, ALU.add, apply_absolute_value=True))
            q(V.tensor_reduce(inv_w[:, 1:2], w2_nat, AX.X, ALU.add, apply_absolute_value=True))
            dve.sem_inc(sem("abs_ready"), 1)
            dve.wait_ge(sem("abs_summed"), 1)
            q(V.tensor_scalar(inv_w[:, 2:4], ps[:, 1, 0:2], 1.0 / (D * HID), 1e-5, ALU.mult, ALU.max))
            q(V.reciprocal(inv_w[:, 0:2], inv_w[:, 2:4]))
            for w, i in ((w1_nat, 0), (w2_nat, 1)):
                q(V.tensor_scalar(w, w, inv_w[:, i:i + 1], MAGIC, ALU.mult, ALU.add))
                q(V.tensor_scalar(w, w, MAGIC, -1.0, ALU.subtract, ALU.max))
            q(V.tensor_scalar(w1_nat, w1_nat, 1.0, inv_w[:, 2:3], ALU.min, ALU.mult))
            q(V.tensor_scalar(w2_q[:].rearrange("p c d -> p (c d)"), w2_nat, 1.0, None, ALU.min))
            for tap in range(3):
                q(V.tensor_tensor(tap_w[:, tap, :], w1_nat, conv_f[:, tap, :], ALU.mult))
            ffn0_prep_vector(dve)
            dve.wait_ge(sem("squares_ready"), 1)
            moments_vector(dve, "direct")
            nc.vector.tensor_copy(ctx_inv[:], inv_all[:]).then_inc(sem("ctx_measured"), 1)
            dve.wait_ge(sem("measured"), B)
            dve.wait_ge(sem("ctx_measured"), 1)

        setups = {}

        def pads_vector(dve, heads):
            n = setups["v"] = setups.get("v", 0) + 1
            dh, R, NU = rows_of(heads)
            nc.vector.memset(q_pad[:], 0.0).then_inc(sem("q_cleared"), 1)
            nc.vector.memset(nm3[:], 0.0).then_inc(sem("q_cleared"), 1)
            dve.wait_ge(sem("q_cleared"), 2 * n)
            for i in range(2):
                nc.vector.memset(q_pad[:, i, :].rearrange("p (h r) -> p h r", h=heads)[:, :, 6 * dh:6 * dh + 3],
                                 1.0).then_inc(sem("q_ones"), 1)
            dve.wait_ge(sem("q_ones"), 2 * n)

        def pads_gpsimd(pool, heads):
            n = setups["g"] = setups.get("g", 0) + 1
            dh, R, NU = rows_of(heads)
            G, each = heads // 2, dh + 1
            nc.gpsimd.memset(k_pad[:], 0.0).then_inc(sem("k_cleared"), 1)
            nc.gpsimd.memset(v_wide[:], 0.0).then_inc(sem("k_cleared"), 1)
            pool.wait_ge(sem("k_cleared"), 4 * n - 2)
            for i in range(2):
                nc.gpsimd.memset(v_wide[:, i, :, 0:G * (G + 1) * each].rearrange(
                    "p g (h n) -> p g h n", h=G)[:, :, :, dh:each], 1.0).then_inc(sem("k_cleared"), 1)
            pool.wait_ge(sem("k_cleared"), 4 * n)

        def latent_moments_vector(dve):
            moments_vector(dve, "ln")
            nc.vector.tensor_copy(inv_ln[:], inv_all[:]).then_inc(sem("inv_ln_kept"), 1)
            dve.wait_ge(sem("inv_ln_kept"), 1)
            moments_vector(dve, "ln_rms6")

        def expert_loads(sp):
            sp.dma_start(w_up.rearrange("p (e c) h -> p e (c h)", e=N_EXP3), t_in["W1T"].rearrange("e d n -> d e n")).then_inc(sem("experts_loaded"), 16)
            sp.dma_start(w_down, t_in["W2T"].rearrange("e (c h) d -> h (e c) d", h=128)).then_inc(sem("experts_loaded"), 16)
            sp.wait_ge(sem("experts_loaded"), 32)

        def store(sp):
            sp.dma_start(out.rearrange("b s d -> s b d"), x_all[:]).then_inc(sem("stored"), 16)
            sp.wait_ge(sem("stored"), 16)

        def tile_mask(u, k, part):
            return mask3[:, k, part, :]

        def causal_mask(u, k, part):
            return causal[:]

        def clear_choice(dve):
            nc.vector.memset(nm3[:], 0.0).then_inc(sem("choice_cleared"), 1)
            dve.wait_ge(sem("choice_cleared"), 1)

        def gather_act(act):
            gather_scalar_sines(act)
            gather_scalar(act)

        def first_stats_scalar(act):
            act.wait_ge(sem("ctx_loaded"), 16)
            for b in range(B):
                if b >= 2:
                    act.wait_ge(sem("squares"), b - 1)
                nc.scalar.activation(q_all[:, 2 * (b % 2):2 * (b % 2) + 2, :].rearrange("p a d -> p (a d)"), ctx_all[:, b, :], ACT.Square,
                                     accum_out=moment[:, 1, b:b + 1]).then_inc(sem("squares"), 1)
            act.wait_ge(sem("squares"), B)
            act.sem_inc(sem("squares_ready"), 1)
            moments_scalar(act)

        def row_counts(**more):
            return {n: B * each for n, each in dict(normed=1, turned=1, rowT=1, used=1, **more).items()}

        phases = [
            dict(sync=prep_sync, scalar=prep_scalar, tensor=prep_tensor, gpsimd=prep_gpsimd, vector=prep_vector),
            dict(vector=lambda e: (pads_vector(e, 16), attention_vector(e, "L0", B, 16, True, False)),
                 counts=attention_counts(B, 16, True, False),
                 gpsimd=lambda e: (pads_gpsimd(e, 16), attention_gpsimd(e, "L0", B, 16, True)),
                 scalar=lambda e: attention_scalar(e, "L0", B, 16, True, False),
                 tensor=lambda e: attention_tensor(e, "L0", B, 16, 0, None, None)),
            dict(vector=ffn0_vector, scalar=ffn0_scalar, tensor=ffn0_tensor, counts=row_counts(added=1)),
            dict(vector=depool_vector, scalar=depool_scalar, tensor=depool_tensor,
                 counts=row_counts(added=1, link2=2, link3=1)),
            dict(vector=route_vector, scalar=route_scalar, tensor=route_tensor, counts=row_counts()),
            dict(vector=gather_vector, scalar=gather_act, tensor=gather_tensor, gpsimd=gather_gpsimd),
            dict(vector=lambda e: (pads_vector(e, 16), attention_vector(e, "L1", TILES, 16, False, True)),
                 counts=attention_counts(TILES, 16, False, True),
                 gpsimd=lambda e: (pads_gpsimd(e, 16), attention_gpsimd(e, "L1", TILES, 16, False)),
                 scalar=lambda e: attention_scalar(e, "L1", TILES, 16, False, True),
                 tensor=lambda e: attention_tensor(e, "L1", TILES, 16, 3, tile_mask, w_o1[:])),
            dict(vector=expand_vector, scalar=expand_scalar, tensor=expand_tensor),
            dict(vector=lambda e: (pads_vector(e, 8), attention_vector(e, "L2", B, 8, True, False)),
                 counts=attention_counts(B, 8, True, False),
                 gpsimd=lambda e: (pads_gpsimd(e, 8), attention_gpsimd(e, "L2", B, 8, True)),
                 scalar=lambda e: attention_scalar(e, "L2", B, 8, True, False),
                 tensor=lambda e: attention_tensor(e, "L2", B, 8, 0, None, None)),
            dict(vector=bit_vector, scalar=bit_scalar, tensor=bit_tensor,
                 counts=row_counts(added=1, link=6, link2=5)),
            dict(vector=cross_vector, scalar=cross_scalar, tensor=cross_tensor, gpsimd=cross_gpsimd,
                 counts=row_counts(added=1)),
            dict(vector=lambda e: (pads_vector(e, 8), attention_vector(e, "L3", B, 8, False, True)),
                 counts=attention_counts(B, 8, False, True),
                 gpsimd=lambda e: (pads_gpsimd(e, 8), attention_gpsimd(e, "L3", B, 8, False)),
                 scalar=lambda e: attention_scalar(e, "L3", B, 8, False, True),
                 tensor=lambda e: attention_tensor(e, "L3", B, 8, 0, None, w_out2[:])),
            dict(vector=lambda e: (latent_moments_vector(e), latent_vector(e)), tensor=latent_tensor,
                 scalar=lambda e: (moments_scalar(e), moments_scalar(e), latent_scalar(e)),
                 counts=row_counts(link2=7, link3=2)),
            dict(vector=lambda e: (pads_vector(e, 16), attention_vector(e, "L4", B, 16, False, True)),
                 counts=attention_counts(B, 16, False, True),
                 gpsimd=lambda e: (pads_gpsimd(e, 16), attention_gpsimd(e, "L4", B, 16, False)),
                 scalar=lambda e: attention_scalar(e, "L4", B, 16, False, True),
                 tensor=lambda e: attention_tensor(e, "L4", B, 16, 1, causal_mask, w_o3[:]),
                 sync=expert_loads),
            dict(vector=lambda e: (clear_choice(e), expert_vector(e)), scalar=expert_scalar, tensor=expert_tensor, gpsimd=expert_gpsimd),
        ]

        def with_moments(kind, phase):
            v, a = phase["vector"], phase["scalar"]
            return dict(phase, vector=lambda e: (moments_vector(e, kind), v(e)),
                        scalar=lambda e: (moments_scalar(e), a(e)))

        for at, kind in ((1, "ln"), (2, "ln"), (3, "ln_rms"), (4, "ln"), (8, "ln"), (9, "ln"), (10, "ln"),
                         (14, "rms")):
            phases[at] = with_moments(kind, phases[at])

        def run(engine, name):
            engine_name[engine] = name
            begun.clear()
            for phase in phases:
                if name in phase:
                    phase[name](engine)
                phase_end(engine)
                for n, count in phase.get("counts", {}).items():
                    begun[n] = begun.get(n, 0) + count

        block = ctx_.enter_context(nc.Block())

        @block.sync
        def _(sp):
            run(sp, "sync")
            store(sp)

        @block.scalar
        def _(act):
            run(act, "scalar")

        @block.gpsimd
        def _(pool):
            run(pool, "gpsimd")

        @block.vector
        def _(dve):
            run(dve, "vector")

        @block.tensor
        def _(pe):
            run(pe, "tensor")


def constants():
    t = np.arange(128)
    a = np.exp(np.float64(np.log(-np.expm1(-0.001))))
    power = t[:, None] - t[None, :]
    f32 = np.float32
    inv = 1.0 / 10000.0 ** (np.arange(4) / 4)
    ang = np.arange(S)[:, None].astype(f32) * inv.astype(f32)[None, :]
    cos, sin = np.cos(ang.astype(np.float64)), np.sin(ang.astype(np.float64))
    cos_q = np.tile(np.concatenate([cos, cos], 1), (1, 16))
    sin_q = np.tile(np.concatenate([-sin, sin], 1), (1, 16))
    s = 8 ** -0.5
    slot = np.arange(128) % SLOTS
    batch = np.arange(128) // SLOTS
    sel = np.zeros((128, 16))
    for i in range(16):
        sel[3 * i:3 * i + 3, i] = sel[64 + 3 * i:64 + 3 * i + 3, i] = 1
    return {
        "c_ident": np.eye(128, dtype=f32),
        "c_upper": (t[:, None] <= t[None, :]).astype(f32),
        "c_below": (t[None, :] < t[:, None]).astype(f32),
        "c_above": (t[None, :] > t[:, None]).astype(f32),
        "c_toep": np.where(power >= 0, a ** np.maximum(power, 0), 0).astype(f32),
        "c_iota_p": np.stack([t, t + 1, t - 127], 1).astype(f32),
        "c_iota_row": np.tile(np.arange(SLOTS), (128, 1)).astype(f32),
        "c_sel": sel.astype(f32),
        "c_rope": np.stack([cos_q, sin_q, cos_q * s, sin_q * s], 1).astype(f32),
        "c_outside": np.where((batch[:, None] == batch[None, :]) & (slot[None, :] < KEPT), 0, BIG).astype(f32),
        "c_own": (batch[:, None] == np.arange(PER_TILE)[None, :]).astype(f32),
        "c_freq": np.tile(inv.astype(f32), (128, 1)),
        "c_first": np.tile(np.arange(N_EXP3, 0, -1), (128, 1)).astype(f32),
    }


def kernel(**inputs):
    import concourse.bacc as bacc
    from concourse.bass_utils import run_bass_kernel_spmd
    get = {k: np.asarray(v) for k, v in inputs.items()}
    T = lambda a, *p: np.ascontiguousarray(np.transpose(a, p or None))
    turned = np.arange(128).reshape(16, 2, 4)[:, ::-1, :].reshape(-1)
    wqT, wukT = T(get["L3_ffn_Wq"]), T(get["L3_ffn_Wuk"])
    arrays = {
        "x": get["x"], "ctx": get["ctx_2048"], "itok": get["itok_Bx1_68_817"],
        "if0T": T(get["mask_BxS2_if0"]), "ik0T": T(get["mask_BxS2_ik0"]), "fk1T": T(get["mask_BxS2_fk1"]),
        "L0_b": get["L0_xattn_b"], "f0_w1T": T(get["L0_ffn_w1"], 0, 2, 1), "f0_w2": get["L0_ffn_w2"],
        "w_inT": T(get["L1_xattn_W_in"]), "b_in": get["L1_xattn_b_in"], "g_res": get["L1_xattn_g_res"],
        "g_init": get["L1_xattn_g_init"], "amask": get["L1_ffn_attention_mask"],
        "posT": T(get["L1_ffn_position_ids"]), "router_w": get["L1_ffn_router_w"],
        "router_b": get["L1_ffn_router_b"], "wq": get["L1_ffn_wq"], "wk": get["L1_ffn_wk"],
        "wv": get["L1_ffn_wv"], "wo": get["L1_ffn_wo"], "w1": get["L1_ffn_w1"], "w2": get["L1_ffn_w2"],
        "ln1": get["L1_ffn_ln1"], "ln2": get["L1_ffn_ln2"], "L2_b": get["L2_xattn_b"],
        "b_w1T": T(get["L2_ffn_w1"]), "conv_wT": T(get["L2_ffn_conv_w"][:, 0, :]), "conv_b": get["L2_ffn_conv_b"],
        "b_w2T": T(get["L2_ffn_w2"]), "W_srcT": T(get["L3_xattn_W_src"]), "b_src": get["L3_xattn_b_src"],
        "W_tgtT": T(get["L3_xattn_W_tgt"]), "b_tgt": get["L3_xattn_b_tgt"], "W_outT": T(get["L3_xattn_W_out"]),
        "b_out": get["L3_xattn_b_out"], "norm1": get["L3_ffn_norm1_w"], "norm2": get["L3_ffn_norm2_w"],
        "WqT": wqT, "WqT_turned": np.ascontiguousarray(wqT[:, turned]), "WdkvT": T(get["L3_ffn_Wdkv"]),
        "WukT": wukT, "WukT_turned": np.ascontiguousarray(wukT[:, turned]), "WuvT": T(get["L3_ffn_Wuv"]),
        "WoT": T(get["L3_ffn_Wo"]), "ln_g": get["L3_ffn_ln_g"], "ln_b": get["L3_ffn_ln_b"],
        "gateT": T(get["L3_ffn_gate_w"]), "gate_b": get["L3_ffn_gate_b"],
        "W1T": T(get["L3_ffn_W1"], 0, 2, 1), "W2T": T(get["L3_ffn_W2"], 0, 2, 1),
        "b1T": T(get["L3_ffn_b1"].reshape(16, 128)), "b2T": T(get["L3_ffn_b2"]),
    }
    arrays.update(constants())
    nc = bacc.Bacc("TRN2", target_bir_lowering=False, num_devices=1)
    t_in = {n: nc.dram_tensor("in_" + n, a.shape, mybir.dt.from_np(a.dtype), kind="ExternalInput").ap()
            for n, a in arrays.items()}
    out = nc.dram_tensor("out_0", (B, S, D), F32, kind="ExternalOutput").ap()
    build(nc, t_in, out)
    got = run_bass_kernel_spmd(nc, [{"in_" + n: a for n, a in arrays.items()}], core_ids=[0])
    return got.results[0]["out_0"]
```
